# Optimizing a Trainium2 kernel written in Bass

```python
import numpy as np
import jax
import jax.numpy as jnp

def _softmax(x, axis=-1):
    return jax.nn.softmax(x, axis=axis)
def _gelu(x):
    return jax.nn.gelu(x, approximate=True)
def _silu(x):
    return jax.nn.silu(x)
def _sigmoid(x):
    return jax.nn.sigmoid(x)
def _layernorm(x, axis=-1, eps=1e-5):
    m = jnp.mean(x, axis=axis, keepdims=True)
    v = jnp.var(x, axis=axis, keepdims=True)
    return (x - m) / jnp.sqrt(v + eps)
def _scatter_add(tgt, idx, src, axis=0):
    return tgt.at[idx].add(src)
def _segment_sum(src, seg, n):
    return jax.ops.segment_sum(src, seg, n)

kernel_name = 'mk_conv_preact_d4_conv_nchw192_ecabab'

def setup_inputs(seed: int = 0):
    np.random.seed(seed)
    _w = jnp.asarray
    def _rec_inputs():
        import jax
        import jax.numpy as jnp
        _gk = jax.random.key(seed)
        x = -4.65e-05 + 0.9999 * jax.random.normal(jax.random.fold_in(_gk, 1), (32, 192, 64, 64), jnp.float32)
        return x
    x = _rec_inputs()
    def _L0_conv_setup():
        import jax, jax.numpy as jnp
        import numpy as np
        from jax import lax
        N, C_IN, C_OUT, H, W = (64, 192, 192, 64, 64)
        K, STRIDE, DILATION = (3, 1, 2)
        PAD = (K - 1) * DILATION // 2
        BN_EPS = 1e-05
        key = jax.random.key(seed)
        k1, k2, k3 = jax.random.split(key, 3)
        x = jax.random.normal(k1, (N, C_IN, H, W), dtype=jnp.float32)
        dw_w = jax.random.normal(k2, (C_IN, 1, K, K), dtype=jnp.float32) * 0.1
        pw_w = jax.random.normal(k3, (C_OUT, C_IN), dtype=jnp.float32) * 0.05
        gamma = jnp.ones((C_OUT,), dtype=jnp.float32)
        beta = jnp.zeros((C_OUT,), dtype=jnp.float32)
        return {'x': x, 'dw_w': dw_w, 'pw_w': pw_w, 'gamma': gamma, 'beta': beta}
    _L0_conv_all = _L0_conv_setup()
    _L0_conv_in = {k: v for k, v in _L0_conv_all.items() if k in ('dw_w', 'pw_w', 'gamma', 'beta', )}
    del _L0_conv_all

    def _L1_conv_setup():
        import jax, jax.numpy as jnp
        import numpy as np
        import math
        C64 = jnp.complex64

        def _fftconv_full(a, kern):
            L = a.shape[-1] + kern.shape[0] - 1
            A = jnp.fft.fft(a, n=L, axis=-1)
            K = jnp.fft.fft(kern.astype(a.dtype), n=L)
            return jnp.fft.ifft(A * K, axis=-1)

        def _centered_ifft(f):
            N = f.shape[-1]
            shft = (np.arange(N) + int(np.fix(N / 2))) % N
            inv = np.argsort(shft)
            g = jnp.fft.ifft(f[..., shft], axis=-1) * math.sqrt(N)
            return g[..., inv].astype(f.dtype)

        def _sincinterp(f):
            N = f.shape[-1]
            y = jnp.zeros(f.shape[:-1] + (2 * N - 1,), f.dtype).at[..., ::2].set(f)
            kern = jnp.asarray(np.sinc(np.arange(-(2 * N - 3), 2 * N - 2) / 2.0).astype(np.complex64))
            return _fftconv_full(y, kern)[..., 2 * N - 3:4 * N - 4]

        def _frft_chirp(f, a):
            N = f.shape[-1]
            alpha = a * math.pi / 2
            tana2, sina = (math.tan(alpha / 2), math.sin(alpha))
            fi = _sincinterp(f)
            pad = jnp.zeros(f.shape[:-1] + (N - 1,), f.dtype)
            fp = jnp.concatenate([pad, fi, pad], axis=-1)
            n = np.arange(-2 * N + 2, 2 * N - 1).astype(np.float64)
            chrp = jnp.asarray(np.exp(-1j * math.pi / N * tana2 / 4 * n ** 2).astype(np.complex64))
            fp = chrp * fp
            c = math.pi / N / sina / 4
            m = np.arange(-(4 * N - 4), 4 * N - 3).astype(np.float64)
            kern = jnp.asarray(np.exp(1j * c * m ** 2).astype(np.complex64))
            ret = _fftconv_full(fp, kern)[..., 4 * N - 4:8 * N - 7] * math.sqrt(c / math.pi)
            ret = chrp * ret
            phase = np.complex64(np.exp(-1j * (1 - a) * math.pi / 4))
            return phase * ret[..., N - 1:3 * N - 2:2]

        def _frft_last(f, a):
            if a < 0.5:
                f = _centered_ifft(f)
                a = a + 1.0
            return _frft_chirp(f, a)

        def _frft2d(x, a):
            t = _frft_last(x, a)
            return jnp.swapaxes(_frft_last(jnp.swapaxes(t, -1, -2), a), -1, -2)

        def _c1x1(x, w, b=None):
            y = jnp.einsum('nchw,oc->nohw', x, w)
            return y if b is None else y + b[None, :, None, None]

        def _c3x3(x, w, b):
            y = jax.lax.conv_general_dilated(x, w, (1, 1), 'SAME', dimension_numbers=('NCHW', 'OIHW', 'NCHW'))
            return y + b[None, :, None, None]

        def _forward(x, conv1_w, mag_s_w, mag_s_b, mag_f_w, mag_f_b, mag_w, mag_b, pha_w, pha_b, conv_0_w, conv_0_b, conv_1_w, conv_1_b, conv2_w):
            angle = 0.5
            alpha = math.cos(angle * math.pi / 2)
            N, C, H, W = x.shape
            H1, W1 = (int(H * alpha), int(W * alpha))
            x1 = _c1x1(x, conv1_w)
            C1, C0 = (C // 4, C // 4 // 3)
            x_0, x_05, x_1 = (x1[:, :C0], x1[:, C0:C1 - C0], x1[:, C1 - C0:C1])
            h0, w0 = ((H - H1) // 2, (W - W1) // 2)
            mask1 = jnp.zeros((H, W), jnp.float32).at[h0:h0 + H1, w0:w0 + W1].set(1.0)
            mask2 = 1.0 - mask1
            Fre = _frft2d(x_05.astype(C64), angle)
            mag, pha = (jnp.abs(Fre), jnp.angle(Fre))
            mag_out = _c1x1(_c3x3(mag * mask1, mag_s_w, mag_s_b) * mask1 + _c1x1(mag * mask2, mag_f_w, mag_f_b) * mask2, mag_w, mag_b)
            pha_out = _c1x1(pha, pha_w, pha_b)
            Fre_out = jax.lax.complex(mag_out * jnp.cos(pha_out), mag_out * jnp.sin(pha_out))
            ifrft = jnp.abs(_frft2d(Fre_out, -angle))
            fre = jnp.fft.rfft2(x_1)
            fm, fp = (jnp.abs(fre), jnp.angle(fre))
            mo = _c1x1(fm, conv_1_w, conv_1_b)
            po = _c1x1(fp, conv_1_w, conv_1_b)
            x_1o = jnp.fft.irfft2(jax.lax.complex(mo * jnp.cos(po), mo * jnp.sin(po)), s=(H, W))
            x_0o = _c1x1(x_0, conv_0_w, conv_0_b)
            return _c1x1(jnp.concatenate([x_0o, ifrft, x_1o], axis=1), conv2_w)
        key = jax.random.key(seed)
        ks = jax.random.split(key, 16)
        N, C, H, W, Co = (4, 192, 128, 128, 192)
        C1, C0 = (C // 4, C // 4 // 3)
        Cm = C1 - 2 * C0
        s = 0.05
        r = lambda k, sh: jax.random.normal(k, sh, jnp.float32)
        return {'x': r(ks[0], (N, C, H, W)), 'conv1_w': r(ks[1], (C1, C)) * s, 'mag_s_w': r(ks[2], (Cm, Cm, 3, 3)) * s, 'mag_s_b': r(ks[3], (Cm,)) * s, 'mag_f_w': r(ks[4], (Cm, Cm)) * s, 'mag_f_b': r(ks[5], (Cm,)) * s, 'mag_w': r(ks[6], (Cm, Cm)) * s, 'mag_b': r(ks[7], (Cm,)) * s, 'pha_w': r(ks[8], (Cm, Cm)) * s, 'pha_b': r(ks[9], (Cm,)) * s, 'conv_0_w': r(ks[10], (C0, C0)) * s, 'conv_0_b': r(ks[11], (C0,)) * s, 'conv_1_w': r(ks[12], (C0, C0)) * s, 'conv_1_b': r(ks[13], (C0,)) * s, 'conv2_w': r(ks[14], (Co, C1)) * s}
    _L1_conv_all = _L1_conv_setup()
    _L1_conv_in = {k: v for k, v in _L1_conv_all.items() if k in ('conv1_w', 'mag_s_w', 'mag_s_b', 'mag_f_w', 'mag_f_b', 'mag_w', 'mag_b', 'pha_w', 'pha_b', 'conv_0_w', 'conv_0_b', 'conv_1_w', 'conv_1_b', 'conv2_w', )}
    del _L1_conv_all

    def _L2_conv_setup():
        import jax, jax.numpy as jnp
        import numpy as np
        LN_EPS = 1e-05
        NEG_INF = -1e+38

        def wkv_scan(w, u, k, v):
            Bdim, T, C = k.shape

            def step(carry, kv_t):
                p, q, o = carry
                kt, vt = kv_t
                no = jnp.maximum(o, u + kt)
                A = jnp.exp(o - no)
                Bw = jnp.exp(u + kt - no)
                y = (A * p + Bw * vt) / (A * q + Bw)
                no2 = jnp.maximum(w + o, kt)
                A2 = jnp.exp(w + o - no2)
                B2 = jnp.exp(kt - no2)
                return ((A2 * p + B2 * vt, A2 * q + B2, no2), y)
            init = (jnp.zeros((Bdim, C), k.dtype), jnp.zeros((Bdim, C), k.dtype), jnp.full((Bdim, C), NEG_INF, k.dtype))
            kT = jnp.moveaxis(k, 1, 0)
            vT = jnp.moveaxis(v, 1, 0)
            _, ys = jax.lax.scan(step, init, (kT, vT))
            return jnp.moveaxis(ys, 0, 1)
        key = jax.random.key(seed)
        ks = jax.random.split(key, 8)
        B, C, H, W = (16, 192, 56, 56)
        s = 0.02
        x = jax.random.normal(ks[0], (B, C, H, W), jnp.float32)
        Wk = jax.random.normal(ks[1], (C, C), jnp.float32) * s
        Wv = jax.random.normal(ks[2], (C, C), jnp.float32) * s
        Wr = jax.random.normal(ks[3], (C, C), jnp.float32) * s
        Wo = jax.random.normal(ks[4], (C, C), jnp.float32) * s
        ln_g = jnp.ones((C,), jnp.float32)
        ln_b = jnp.zeros((C,), jnp.float32)
        w_decay = -6.0 + 0.1 * jax.random.normal(ks[5], (C,), jnp.float32)
        u = 0.1 * jax.random.normal(ks[6], (C,), jnp.float32)
        return {'x': x, 'Wk': Wk, 'Wv': Wv, 'Wr': Wr, 'Wo': Wo, 'ln_g': ln_g, 'ln_b': ln_b, 'w_decay': w_decay, 'u': u}
    _L2_conv_all = _L2_conv_setup()
    _L2_conv_in = {k: v for k, v in _L2_conv_all.items() if k in ('Wk', 'Wv', 'Wr', 'Wo', 'ln_g', 'ln_b', 'w_decay', 'u', )}
    del _L2_conv_all

    def _L3_conv_setup():
        import jax, jax.numpy as jnp
        import numpy as np
        import math
        C64 = jnp.complex64

        def _fftconv_full(a, kern):
            L = a.shape[-1] + kern.shape[0] - 1
            A = jnp.fft.fft(a, n=L, axis=-1)
            K = jnp.fft.fft(kern.astype(a.dtype), n=L)
            return jnp.fft.ifft(A * K, axis=-1)

        def _centered_ifft(f):
            N = f.shape[-1]
            shft = (np.arange(N) + int(np.fix(N / 2))) % N
            inv = np.argsort(shft)
            g = jnp.fft.ifft(f[..., shft], axis=-1) * math.sqrt(N)
            return g[..., inv].astype(f.dtype)

        def _sincinterp(f):
            N = f.shape[-1]
            y = jnp.zeros(f.shape[:-1] + (2 * N - 1,), f.dtype).at[..., ::2].set(f)
            kern = jnp.asarray(np.sinc(np.arange(-(2 * N - 3), 2 * N - 2) / 2.0).astype(np.complex64))
            return _fftconv_full(y, kern)[..., 2 * N - 3:4 * N - 4]

        def _frft_chirp(f, a):
            N = f.shape[-1]
            alpha = a * math.pi / 2
            tana2, sina = (math.tan(alpha / 2), math.sin(alpha))
            fi = _sincinterp(f)
            pad = jnp.zeros(f.shape[:-1] + (N - 1,), f.dtype)
            fp = jnp.concatenate([pad, fi, pad], axis=-1)
            n = np.arange(-2 * N + 2, 2 * N - 1).astype(np.float64)
            chrp = jnp.asarray(np.exp(-1j * math.pi / N * tana2 / 4 * n ** 2).astype(np.complex64))
            fp = chrp * fp
            c = math.pi / N / sina / 4
            m = np.arange(-(4 * N - 4), 4 * N - 3).astype(np.float64)
            kern = jnp.asarray(np.exp(1j * c * m ** 2).astype(np.complex64))
            ret = _fftconv_full(fp, kern)[..., 4 * N - 4:8 * N - 7] * math.sqrt(c / math.pi)
            ret = chrp * ret
            phase = np.complex64(np.exp(-1j * (1 - a) * math.pi / 4))
            return phase * ret[..., N - 1:3 * N - 2:2]

        def _frft_last(f, a):
            if a < 0.5:
                f = _centered_ifft(f)
                a = a + 1.0
            return _frft_chirp(f, a)

        def _frft2d(x, a):
            t = _frft_last(x, a)
            return jnp.swapaxes(_frft_last(jnp.swapaxes(t, -1, -2), a), -1, -2)

        def _c1x1(x, w, b=None):
            y = jnp.einsum('nchw,oc->nohw', x, w)
            return y if b is None else y + b[None, :, None, None]

        def _c3x3(x, w, b):
            y = jax.lax.conv_general_dilated(x, w, (1, 1), 'SAME', dimension_numbers=('NCHW', 'OIHW', 'NCHW'))
            return y + b[None, :, None, None]

        def _forward(x, conv1_w, mag_s_w, mag_s_b, mag_f_w, mag_f_b, mag_w, mag_b, pha_w, pha_b, conv_0_w, conv_0_b, conv_1_w, conv_1_b, conv2_w):
            angle = 0.5
            alpha = math.cos(angle * math.pi / 2)
            N, C, H, W = x.shape
            H1, W1 = (int(H * alpha), int(W * alpha))
            x1 = _c1x1(x, conv1_w)
            C1, C0 = (C // 4, C // 4 // 3)
            x_0, x_05, x_1 = (x1[:, :C0], x1[:, C0:C1 - C0], x1[:, C1 - C0:C1])
            h0, w0 = ((H - H1) // 2, (W - W1) // 2)
            mask1 = jnp.zeros((H, W), jnp.float32).at[h0:h0 + H1, w0:w0 + W1].set(1.0)
            mask2 = 1.0 - mask1
            Fre = _frft2d(x_05.astype(C64), angle)
            mag, pha = (jnp.abs(Fre), jnp.angle(Fre))
            mag_out = _c1x1(_c3x3(mag * mask1, mag_s_w, mag_s_b) * mask1 + _c1x1(mag * mask2, mag_f_w, mag_f_b) * mask2, mag_w, mag_b)
            pha_out = _c1x1(pha, pha_w, pha_b)
            Fre_out = jax.lax.complex(mag_out * jnp.cos(pha_out), mag_out * jnp.sin(pha_out))
            ifrft = jnp.abs(_frft2d(Fre_out, -angle))
            fre = jnp.fft.rfft2(x_1)
            fm, fp = (jnp.abs(fre), jnp.angle(fre))
            mo = _c1x1(fm, conv_1_w, conv_1_b)
            po = _c1x1(fp, conv_1_w, conv_1_b)
            x_1o = jnp.fft.irfft2(jax.lax.complex(mo * jnp.cos(po), mo * jnp.sin(po)), s=(H, W))
            x_0o = _c1x1(x_0, conv_0_w, conv_0_b)
            return _c1x1(jnp.concatenate([x_0o, ifrft, x_1o], axis=1), conv2_w)
        key = jax.random.key(seed)
        ks = jax.random.split(key, 16)
        N, C, H, W, Co = (4, 192, 128, 128, 192)
        C1, C0 = (C // 4, C // 4 // 3)
        Cm = C1 - 2 * C0
        s = 0.05
        r = lambda k, sh: jax.random.normal(k, sh, jnp.float32)
        return {'x': r(ks[0], (N, C, H, W)), 'conv1_w': r(ks[1], (C1, C)) * s, 'mag_s_w': r(ks[2], (Cm, Cm, 3, 3)) * s, 'mag_s_b': r(ks[3], (Cm,)) * s, 'mag_f_w': r(ks[4], (Cm, Cm)) * s, 'mag_f_b': r(ks[5], (Cm,)) * s, 'mag_w': r(ks[6], (Cm, Cm)) * s, 'mag_b': r(ks[7], (Cm,)) * s, 'pha_w': r(ks[8], (Cm, Cm)) * s, 'pha_b': r(ks[9], (Cm,)) * s, 'conv_0_w': r(ks[10], (C0, C0)) * s, 'conv_0_b': r(ks[11], (C0,)) * s, 'conv_1_w': r(ks[12], (C0, C0)) * s, 'conv_1_b': r(ks[13], (C0,)) * s, 'conv2_w': r(ks[14], (Co, C1)) * s}
    _L3_conv_all = _L3_conv_setup()
    _L3_conv_in = {k: v for k, v in _L3_conv_all.items() if k in ('conv1_w', 'mag_s_w', 'mag_s_b', 'mag_f_w', 'mag_f_b', 'mag_w', 'mag_b', 'pha_w', 'pha_b', 'conv_0_w', 'conv_0_b', 'conv_1_w', 'conv_1_b', 'conv2_w', )}
    del _L3_conv_all

    return {
        "x": x,
        "L0_conv_dw_w": _L0_conv_in["dw_w"],
        "L0_conv_pw_w": _L0_conv_in["pw_w"],
        "L0_conv_gamma": _L0_conv_in["gamma"],
        "L0_conv_beta": _L0_conv_in["beta"],
        "L1_conv_conv1_w": _L1_conv_in["conv1_w"],
        "L1_conv_mag_s_w": _L1_conv_in["mag_s_w"],
        "L1_conv_mag_s_b": _L1_conv_in["mag_s_b"],
        "L1_conv_mag_f_w": _L1_conv_in["mag_f_w"],
        "L1_conv_mag_f_b": _L1_conv_in["mag_f_b"],
        "L1_conv_mag_w": _L1_conv_in["mag_w"],
        "L1_conv_mag_b": _L1_conv_in["mag_b"],
        "L1_conv_pha_w": _L1_conv_in["pha_w"],
        "L1_conv_pha_b": _L1_conv_in["pha_b"],
        "L1_conv_conv_0_w": _L1_conv_in["conv_0_w"],
        "L1_conv_conv_0_b": _L1_conv_in["conv_0_b"],
        "L1_conv_conv_1_w": _L1_conv_in["conv_1_w"],
        "L1_conv_conv_1_b": _L1_conv_in["conv_1_b"],
        "L1_conv_conv2_w": _L1_conv_in["conv2_w"],
        "L2_conv_Wk": _L2_conv_in["Wk"],
        "L2_conv_Wv": _L2_conv_in["Wv"],
        "L2_conv_Wr": _L2_conv_in["Wr"],
        "L2_conv_Wo": _L2_conv_in["Wo"],
        "L2_conv_ln_g": _L2_conv_in["ln_g"],
        "L2_conv_ln_b": _L2_conv_in["ln_b"],
        "L2_conv_w_decay": _L2_conv_in["w_decay"],
        "L2_conv_u": _L2_conv_in["u"],
        "L3_conv_conv1_w": _L3_conv_in["conv1_w"],
        "L3_conv_mag_s_w": _L3_conv_in["mag_s_w"],
        "L3_conv_mag_s_b": _L3_conv_in["mag_s_b"],
        "L3_conv_mag_f_w": _L3_conv_in["mag_f_w"],
        "L3_conv_mag_f_b": _L3_conv_in["mag_f_b"],
        "L3_conv_mag_w": _L3_conv_in["mag_w"],
        "L3_conv_mag_b": _L3_conv_in["mag_b"],
        "L3_conv_pha_w": _L3_conv_in["pha_w"],
        "L3_conv_pha_b": _L3_conv_in["pha_b"],
        "L3_conv_conv_0_w": _L3_conv_in["conv_0_w"],
        "L3_conv_conv_0_b": _L3_conv_in["conv_0_b"],
        "L3_conv_conv_1_w": _L3_conv_in["conv_1_w"],
        "L3_conv_conv_1_b": _L3_conv_in["conv_1_b"],
        "L3_conv_conv2_w": _L3_conv_in["conv2_w"],
    }

def reference(x, L0_conv_dw_w, L0_conv_pw_w, L0_conv_gamma, L0_conv_beta, L1_conv_conv1_w, L1_conv_mag_s_w, L1_conv_mag_s_b, L1_conv_mag_f_w, L1_conv_mag_f_b, L1_conv_mag_w, L1_conv_mag_b, L1_conv_pha_w, L1_conv_pha_b, L1_conv_conv_0_w, L1_conv_conv_0_b, L1_conv_conv_1_w, L1_conv_conv_1_b, L1_conv_conv2_w, L2_conv_Wk, L2_conv_Wv, L2_conv_Wr, L2_conv_Wo, L2_conv_ln_g, L2_conv_ln_b, L2_conv_w_decay, L2_conv_u, L3_conv_conv1_w, L3_conv_mag_s_w, L3_conv_mag_s_b, L3_conv_mag_f_w, L3_conv_mag_f_b, L3_conv_mag_w, L3_conv_mag_b, L3_conv_pha_w, L3_conv_pha_b, L3_conv_conv_0_w, L3_conv_conv_0_b, L3_conv_conv_1_w, L3_conv_conv_1_b, L3_conv_conv2_w):
    import jax
    import jax.numpy as jnp
    def _L0_conv_ref(x, dw_w, pw_w, gamma, beta):
        import jax, jax.numpy as jnp
        import numpy as np
        from jax import lax
        N, C_IN, C_OUT, H, W = (64, 192, 192, 64, 64)
        K, STRIDE, DILATION = (3, 1, 2)
        PAD = (K - 1) * DILATION // 2
        BN_EPS = 1e-05
        h = jax.nn.relu(x)
        y = lax.conv_general_dilated(h, dw_w, window_strides=(STRIDE, STRIDE), padding=((PAD, PAD), (PAD, PAD)), rhs_dilation=(DILATION, DILATION), dimension_numbers=('NCHW', 'OIHW', 'NCHW'), feature_group_count=C_IN)
        z = jnp.einsum('nchw,oc->nohw', y, pw_w)
        mean = jnp.mean(z, axis=(0, 2, 3), keepdims=True)
        var = jnp.var(z, axis=(0, 2, 3), keepdims=True)
        zhat = (z - mean) * lax.rsqrt(var + BN_EPS)
        return zhat * gamma[None, :, None, None] + beta[None, :, None, None]

    def _L1_conv_ref(x, conv1_w, mag_s_w, mag_s_b, mag_f_w, mag_f_b, mag_w, mag_b, pha_w, pha_b, conv_0_w, conv_0_b, conv_1_w, conv_1_b, conv2_w):
        import jax, jax.numpy as jnp
        import numpy as np
        import math
        C64 = jnp.complex64

        def _fftconv_full(a, kern):
            L = a.shape[-1] + kern.shape[0] - 1
            A = jnp.fft.fft(a, n=L, axis=-1)
            K = jnp.fft.fft(kern.astype(a.dtype), n=L)
            return jnp.fft.ifft(A * K, axis=-1)

        def _centered_ifft(f):
            N = f.shape[-1]
            shft = (np.arange(N) + int(np.fix(N / 2))) % N
            inv = np.argsort(shft)
            g = jnp.fft.ifft(f[..., shft], axis=-1) * math.sqrt(N)
            return g[..., inv].astype(f.dtype)

        def _sincinterp(f):
            N = f.shape[-1]
            y = jnp.zeros(f.shape[:-1] + (2 * N - 1,), f.dtype).at[..., ::2].set(f)
            kern = jnp.asarray(np.sinc(np.arange(-(2 * N - 3), 2 * N - 2) / 2.0).astype(np.complex64))
            return _fftconv_full(y, kern)[..., 2 * N - 3:4 * N - 4]

        def _frft_chirp(f, a):
            N = f.shape[-1]
            alpha = a * math.pi / 2
            tana2, sina = (math.tan(alpha / 2), math.sin(alpha))
            fi = _sincinterp(f)
            pad = jnp.zeros(f.shape[:-1] + (N - 1,), f.dtype)
            fp = jnp.concatenate([pad, fi, pad], axis=-1)
            n = np.arange(-2 * N + 2, 2 * N - 1).astype(np.float64)
            chrp = jnp.asarray(np.exp(-1j * math.pi / N * tana2 / 4 * n ** 2).astype(np.complex64))
            fp = chrp * fp
            c = math.pi / N / sina / 4
            m = np.arange(-(4 * N - 4), 4 * N - 3).astype(np.float64)
            kern = jnp.asarray(np.exp(1j * c * m ** 2).astype(np.complex64))
            ret = _fftconv_full(fp, kern)[..., 4 * N - 4:8 * N - 7] * math.sqrt(c / math.pi)
            ret = chrp * ret
            phase = np.complex64(np.exp(-1j * (1 - a) * math.pi / 4))
            return phase * ret[..., N - 1:3 * N - 2:2]

        def _frft_last(f, a):
            if a < 0.5:
                f = _centered_ifft(f)
                a = a + 1.0
            return _frft_chirp(f, a)

        def _frft2d(x, a):
            t = _frft_last(x, a)
            return jnp.swapaxes(_frft_last(jnp.swapaxes(t, -1, -2), a), -1, -2)

        def _c1x1(x, w, b=None):
            y = jnp.einsum('nchw,oc->nohw', x, w)
            return y if b is None else y + b[None, :, None, None]

        def _c3x3(x, w, b):
            y = jax.lax.conv_general_dilated(x, w, (1, 1), 'SAME', dimension_numbers=('NCHW', 'OIHW', 'NCHW'))
            return y + b[None, :, None, None]

        def _forward(x, conv1_w, mag_s_w, mag_s_b, mag_f_w, mag_f_b, mag_w, mag_b, pha_w, pha_b, conv_0_w, conv_0_b, conv_1_w, conv_1_b, conv2_w):
            angle = 0.5
            alpha = math.cos(angle * math.pi / 2)
            N, C, H, W = x.shape
            H1, W1 = (int(H * alpha), int(W * alpha))
            x1 = _c1x1(x, conv1_w)
            C1, C0 = (C // 4, C // 4 // 3)
            x_0, x_05, x_1 = (x1[:, :C0], x1[:, C0:C1 - C0], x1[:, C1 - C0:C1])
            h0, w0 = ((H - H1) // 2, (W - W1) // 2)
            mask1 = jnp.zeros((H, W), jnp.float32).at[h0:h0 + H1, w0:w0 + W1].set(1.0)
            mask2 = 1.0 - mask1
            Fre = _frft2d(x_05.astype(C64), angle)
            mag, pha = (jnp.abs(Fre), jnp.angle(Fre))
            mag_out = _c1x1(_c3x3(mag * mask1, mag_s_w, mag_s_b) * mask1 + _c1x1(mag * mask2, mag_f_w, mag_f_b) * mask2, mag_w, mag_b)
            pha_out = _c1x1(pha, pha_w, pha_b)
            Fre_out = jax.lax.complex(mag_out * jnp.cos(pha_out), mag_out * jnp.sin(pha_out))
            ifrft = jnp.abs(_frft2d(Fre_out, -angle))
            fre = jnp.fft.rfft2(x_1)
            fm, fp = (jnp.abs(fre), jnp.angle(fre))
            mo = _c1x1(fm, conv_1_w, conv_1_b)
            po = _c1x1(fp, conv_1_w, conv_1_b)
            x_1o = jnp.fft.irfft2(jax.lax.complex(mo * jnp.cos(po), mo * jnp.sin(po)), s=(H, W))
            x_0o = _c1x1(x_0, conv_0_w, conv_0_b)
            return _c1x1(jnp.concatenate([x_0o, ifrft, x_1o], axis=1), conv2_w)
        return _forward(x, conv1_w, mag_s_w, mag_s_b, mag_f_w, mag_f_b, mag_w, mag_b, pha_w, pha_b, conv_0_w, conv_0_b, conv_1_w, conv_1_b, conv2_w)

    def _L2_conv_ref(x, Wk, Wv, Wr, Wo, ln_g, ln_b, w_decay, u):
        import jax, jax.numpy as jnp
        import numpy as np
        LN_EPS = 1e-05
        NEG_INF = -1e+38

        def wkv_scan(w, u, k, v):
            Bdim, T, C = k.shape

            def step(carry, kv_t):
                p, q, o = carry
                kt, vt = kv_t
                no = jnp.maximum(o, u + kt)
                A = jnp.exp(o - no)
                Bw = jnp.exp(u + kt - no)
                y = (A * p + Bw * vt) / (A * q + Bw)
                no2 = jnp.maximum(w + o, kt)
                A2 = jnp.exp(w + o - no2)
                B2 = jnp.exp(kt - no2)
                return ((A2 * p + B2 * vt, A2 * q + B2, no2), y)
            init = (jnp.zeros((Bdim, C), k.dtype), jnp.zeros((Bdim, C), k.dtype), jnp.full((Bdim, C), NEG_INF, k.dtype))
            kT = jnp.moveaxis(k, 1, 0)
            vT = jnp.moveaxis(v, 1, 0)
            _, ys = jax.lax.scan(step, init, (kT, vT))
            return jnp.moveaxis(ys, 0, 1)
        B, C, H, W = x.shape
        xs = jnp.transpose(x.reshape(B, C, H * W), (0, 2, 1))
        k = jnp.einsum('btc,dc->btd', xs, Wk)
        v = jnp.einsum('btc,dc->btd', xs, Wv)
        r = jnp.einsum('btc,dc->btd', xs, Wr)
        real_w = -jnp.exp(w_decay)
        x_fwd = wkv_scan(real_w, u, k, v)
        x_bwd = jnp.flip(wkv_scan(real_w, u, jnp.flip(k, 1), jnp.flip(v, 1)), 1)
        x_bi = 0.5 * (x_fwd + x_bwd)
        h = jax.nn.sigmoid(r) * x_bi
        mu = jnp.mean(h, axis=-1, keepdims=True)
        var = jnp.var(h, axis=-1, keepdims=True)
        h = (h - mu) * jax.lax.rsqrt(var + LN_EPS) * ln_g + ln_b
        out = jnp.einsum('btc,dc->btd', h, Wo)
        return jnp.transpose(out, (0, 2, 1)).reshape(B, C, H, W)

    def _L3_conv_ref(x, conv1_w, mag_s_w, mag_s_b, mag_f_w, mag_f_b, mag_w, mag_b, pha_w, pha_b, conv_0_w, conv_0_b, conv_1_w, conv_1_b, conv2_w):
        import jax, jax.numpy as jnp
        import numpy as np
        import math
        C64 = jnp.complex64

        def _fftconv_full(a, kern):
            L = a.shape[-1] + kern.shape[0] - 1
            A = jnp.fft.fft(a, n=L, axis=-1)
            K = jnp.fft.fft(kern.astype(a.dtype), n=L)
            return jnp.fft.ifft(A * K, axis=-1)

        def _centered_ifft(f):
            N = f.shape[-1]
            shft = (np.arange(N) + int(np.fix(N / 2))) % N
            inv = np.argsort(shft)
            g = jnp.fft.ifft(f[..., shft], axis=-1) * math.sqrt(N)
            return g[..., inv].astype(f.dtype)

        def _sincinterp(f):
            N = f.shape[-1]
            y = jnp.zeros(f.shape[:-1] + (2 * N - 1,), f.dtype).at[..., ::2].set(f)
            kern = jnp.asarray(np.sinc(np.arange(-(2 * N - 3), 2 * N - 2) / 2.0).astype(np.complex64))
            return _fftconv_full(y, kern)[..., 2 * N - 3:4 * N - 4]

        def _frft_chirp(f, a):
            N = f.shape[-1]
            alpha = a * math.pi / 2
            tana2, sina = (math.tan(alpha / 2), math.sin(alpha))
            fi = _sincinterp(f)
            pad = jnp.zeros(f.shape[:-1] + (N - 1,), f.dtype)
            fp = jnp.concatenate([pad, fi, pad], axis=-1)
            n = np.arange(-2 * N + 2, 2 * N - 1).astype(np.float64)
            chrp = jnp.asarray(np.exp(-1j * math.pi / N * tana2 / 4 * n ** 2).astype(np.complex64))
            fp = chrp * fp
            c = math.pi / N / sina / 4
            m = np.arange(-(4 * N - 4), 4 * N - 3).astype(np.float64)
            kern = jnp.asarray(np.exp(1j * c * m ** 2).astype(np.complex64))
            ret = _fftconv_full(fp, kern)[..., 4 * N - 4:8 * N - 7] * math.sqrt(c / math.pi)
            ret = chrp * ret
            phase = np.complex64(np.exp(-1j * (1 - a) * math.pi / 4))
            return phase * ret[..., N - 1:3 * N - 2:2]

        def _frft_last(f, a):
            if a < 0.5:
                f = _centered_ifft(f)
                a = a + 1.0
            return _frft_chirp(f, a)

        def _frft2d(x, a):
            t = _frft_last(x, a)
            return jnp.swapaxes(_frft_last(jnp.swapaxes(t, -1, -2), a), -1, -2)

        def _c1x1(x, w, b=None):
            y = jnp.einsum('nchw,oc->nohw', x, w)
            return y if b is None else y + b[None, :, None, None]

        def _c3x3(x, w, b):
            y = jax.lax.conv_general_dilated(x, w, (1, 1), 'SAME', dimension_numbers=('NCHW', 'OIHW', 'NCHW'))
            return y + b[None, :, None, None]

        def _forward(x, conv1_w, mag_s_w, mag_s_b, mag_f_w, mag_f_b, mag_w, mag_b, pha_w, pha_b, conv_0_w, conv_0_b, conv_1_w, conv_1_b, conv2_w):
            angle = 0.5
            alpha = math.cos(angle * math.pi / 2)
            N, C, H, W = x.shape
            H1, W1 = (int(H * alpha), int(W * alpha))
            x1 = _c1x1(x, conv1_w)
            C1, C0 = (C // 4, C // 4 // 3)
            x_0, x_05, x_1 = (x1[:, :C0], x1[:, C0:C1 - C0], x1[:, C1 - C0:C1])
            h0, w0 = ((H - H1) // 2, (W - W1) // 2)
            mask1 = jnp.zeros((H, W), jnp.float32).at[h0:h0 + H1, w0:w0 + W1].set(1.0)
            mask2 = 1.0 - mask1
            Fre = _frft2d(x_05.astype(C64), angle)
            mag, pha = (jnp.abs(Fre), jnp.angle(Fre))
            mag_out = _c1x1(_c3x3(mag * mask1, mag_s_w, mag_s_b) * mask1 + _c1x1(mag * mask2, mag_f_w, mag_f_b) * mask2, mag_w, mag_b)
            pha_out = _c1x1(pha, pha_w, pha_b)
            Fre_out = jax.lax.complex(mag_out * jnp.cos(pha_out), mag_out * jnp.sin(pha_out))
            ifrft = jnp.abs(_frft2d(Fre_out, -angle))
            fre = jnp.fft.rfft2(x_1)
            fm, fp = (jnp.abs(fre), jnp.angle(fre))
            mo = _c1x1(fm, conv_1_w, conv_1_b)
            po = _c1x1(fp, conv_1_w, conv_1_b)
            x_1o = jnp.fft.irfft2(jax.lax.complex(mo * jnp.cos(po), mo * jnp.sin(po)), s=(H, W))
            x_0o = _c1x1(x_0, conv_0_w, conv_0_b)
            return _c1x1(jnp.concatenate([x_0o, ifrft, x_1o], axis=1), conv2_w)
        return _forward(x, conv1_w, mag_s_w, mag_s_b, mag_f_w, mag_f_b, mag_w, mag_b, pha_w, pha_b, conv_0_w, conv_0_b, conv_1_w, conv_1_b, conv2_w)

    def _gn(v, G=32, eps=1e-5):
        B_, C_, H_, W_ = v.shape
        g = v.reshape(B_, G, C_ // G, H_, W_)
        m = jnp.mean(g, axis=(2, 3, 4), keepdims=True)
        s = jnp.var(g, axis=(2, 3, 4), keepdims=True)
        return ((g - m) / jnp.sqrt(s + eps)).reshape(v.shape)

    def _ln_c(v, eps=1e-6):
        m = jnp.mean(v, axis=1, keepdims=True)
        s = jnp.var(v, axis=1, keepdims=True)
        return (v - m) / jnp.sqrt(s + eps)

    def _ln_t(v, eps=1e-5):
        m = jnp.mean(v, axis=-1, keepdims=True)
        s = jnp.var(v, axis=-1, keepdims=True)
        return (v - m) / jnp.sqrt(s + eps)

    def _to_tokens(v):
        B_, C_, H_, W_ = v.shape
        return v.reshape(B_, C_, H_ * W_).transpose(0, 2, 1)
    def _from_tokens(t, like):
        B_, C_, H_, W_ = like.shape
        return t.transpose(0, 2, 1).reshape(B_, C_, H_, W_)

    x = x + _L0_conv_ref(_gn(x), L0_conv_dw_w, L0_conv_pw_w, L0_conv_gamma, L0_conv_beta)
    x = x + _L1_conv_ref(_gn(x), L1_conv_conv1_w, L1_conv_mag_s_w, L1_conv_mag_s_b, L1_conv_mag_f_w, L1_conv_mag_f_b, L1_conv_mag_w, L1_conv_mag_b, L1_conv_pha_w, L1_conv_pha_b, L1_conv_conv_0_w, L1_conv_conv_0_b, L1_conv_conv_1_w, L1_conv_conv_1_b, L1_conv_conv2_w)
    x = x + _L2_conv_ref(_gn(x), L2_conv_Wk, L2_conv_Wv, L2_conv_Wr, L2_conv_Wo, L2_conv_ln_g, L2_conv_ln_b, L2_conv_w_decay, L2_conv_u)
    x = x + _L3_conv_ref(_gn(x), L3_conv_conv1_w, L3_conv_mag_s_w, L3_conv_mag_s_b, L3_conv_mag_f_w, L3_conv_mag_f_b, L3_conv_mag_w, L3_conv_mag_b, L3_conv_pha_w, L3_conv_pha_b, L3_conv_conv_0_w, L3_conv_conv_0_b, L3_conv_conv_1_w, L3_conv_conv_1_b, L3_conv_conv2_w)
    return x


_drawn_inputs = setup_inputs


def setup_inputs(seed=0):
    import zlib

    import numpy as np

    out = dict(_drawn_inputs(seed))
    spreads = {'L0_conv_gamma': (1.0, 0.2),
     'L0_conv_beta': (0.0, 0.1),
     'L2_conv_ln_g': (1.0, 0.2),
     'L2_conv_ln_b': (0.0, 0.403)}
    factors = {'L1_conv_mag_s_w': 6.576,
     'L1_conv_mag_s_b': 8.0,
     'L1_conv_mag_f_w': 8.0,
     'L1_conv_mag_f_b': 8.0,
     'L1_conv_mag_w': 6.683,
     'L1_conv_mag_b': 6.567,
     'L1_conv_pha_w': 8.0,
     'L1_conv_pha_b': 64.0,
     'L1_conv_conv_0_w': 2.755,
     'L1_conv_conv_0_b': 2.782,
     'L1_conv_conv_1_w': 3.159,
     'L1_conv_conv_1_b': 8.0,
     'L2_conv_w_decay': 8.0,
     'L2_conv_u': 8.0,
     'L3_conv_conv1_w': 2.675,
     'L3_conv_mag_s_w': 8.0,
     'L3_conv_mag_s_b': 8.0,
     'L3_conv_mag_f_w': 8.0,
     'L3_conv_mag_f_b': 26.617,
     'L3_conv_mag_w': 8.0,
     'L3_conv_mag_b': 24.485,
     'L3_conv_pha_w': 8.0,
     'L3_conv_pha_b': 64.0,
     'L3_conv_conv_0_w': 2.797,
     'L3_conv_conv_0_b': 6.802,
     'L3_conv_conv_1_w': 3.289,
     'L3_conv_conv_1_b': 8.0}
    for name, (base, spread) in spreads.items():
        noise = np.random.default_rng([zlib.crc32(name.encode()), seed]).standard_normal(out[name].shape)
        drawn = base * np.exp(spread * noise) if base else spread * noise
        out[name] = jnp.asarray(drawn.astype(out[name].dtype))
    for name, factor in factors.items():
        out[name] = (out[name] * factor).astype(out[name].dtype)
    return out
```

```python
import math
from contextlib import ExitStack

import numpy as np

import concourse.bass as bass
from concourse import mybir

P = 128
BATCH, CH, SIDE = 32, 192, 64
TOKENS = SIDE * SIDE
ROWS = BATCH * CH
TILES = 3
PAIRS = ROWS // (P * TILES)
SOURCES = ((0, 1), (0, 1, 2), (1, 2))
BLOCK = {(s, t): n for n, (s, t) in enumerate((s, t) for t in range(TILES) for s in SOURCES[t])}
GN_EPS, LN_EPS, BN_EPS = 1e-5, 1e-5, 1e-5
NEG_INF = -1e38

F32 = mybir.dt.float32
ALU = mybir.AluOpType
ACT = mybir.ActivationFunctionType


def makers(nc, ctx, prefix):
    return (lambda name, shape: ctx.enter_context(nc.sbuf_tensor(prefix + name, shape, F32)),
            lambda name, shape: ctx.enter_context(nc.psum_tensor(prefix + name, shape, F32)),
            lambda name: ctx.enter_context(nc.semaphore(prefix + name)))


class GroupNorm:

    DVE_STEPS = 10

    def __init__(self, nc, sb, sem, parts):
        self.mix = sb("gn_mix", [P, 7, P])
        self.raw = sb("gn_raw", [P, TILES, 8, 6])
        self.mv = sb("gn_mv", [P, TILES, 2])
        self.group = sb("gn_group", [P, TILES, 2])
        self.sq = sb("gn_sq", [P, TILES])
        self.var = sb("gn_var", [P, TILES])
        self.rstd = sb("gn_rstd", [P, TILES])
        self.shift = sb("gn_shift", [P, TILES])
        self.half = sb("gn_half", [P, TILES])
        self.stat, self.mixed, self.powered = sem("gn_stat"), sem("gn_mixed"), sem("gn_powered")

    def statistics(self, dve, i, x, loaded):
        n = i * self.DVE_STEPS
        for t in range(TILES):
            loaded(t)
            for j in range(8):
                ins = dve.bn_stats(self.raw[:, t, j, :], x[:, t, j * 512:(j + 1) * 512])
        ins.then_inc(self.stat, 1)
        dve.wait_ge(self.stat, n + 1)
        dve.memset(self.sq[:, :], 0.0)
        for t in range(TILES):
            ins = dve.bn_aggr(self.mv[:, t, :], self.raw[:, t, :, :])
        ins.then_inc(self.stat, 1)
        dve.wait_ge(self.stat, n + 2)
        dve.tensor_tensor(self.sq[:, :], self.mv[:, :, 0], self.mv[:, :, 0], ALU.mult).then_inc(self.stat, 1)
        dve.wait_ge(self.stat, n + 3)
        dve.tensor_tensor(self.mv[:, :, 1], self.mv[:, :, 1], self.sq[:, :], ALU.add).then_inc(self.stat, 1)

    def mix_stats(self, pe, i, bank):
        pe.wait_ge(self.stat, i * self.DVE_STEPS + 4)
        for t in range(TILES):
            for n, s in enumerate(SOURCES[t]):
                ins = pe.matmul(bank[:, 2 * t:2 * t + 2], self.mix[:, BLOCK[s, t], :], self.mv[:, s, :],
                                start=(n == 0), stop=(n == len(SOURCES[t]) - 1))
        ins.then_inc(self.mixed, 1)

    def power(self, pool, i):
        pool.wait_ge(self.stat, i * self.DVE_STEPS + 8)
        pool.tensor_tensor(self.rstd[:, :], self.var[:, :], self.half[:, :], ALU.pow).then_inc(self.powered, 1)

    def scales(self, dve, i, bank):
        n = i * self.DVE_STEPS
        dve.wait_ge(self.mixed, i + 1)
        dve.tensor_copy(self.group[:, :, :], bank.rearrange("p (t c) -> p t c", c=2)).then_inc(self.stat, 1)
        dve.wait_ge(self.stat, n + 5)
        dve.tensor_tensor(self.sq[:, :], self.group[:, :, 0], self.group[:, :, 0], ALU.mult).then_inc(self.stat, 1)
        dve.wait_ge(self.stat, n + 6)
        dve.tensor_tensor(self.var[:, :], self.group[:, :, 1], self.sq[:, :], ALU.subtract).then_inc(self.stat, 1)
        dve.wait_ge(self.stat, n + 7)
        dve.tensor_scalar(self.var[:, :], self.var[:, :], 0.0, GN_EPS, ALU.max, ALU.add).then_inc(self.stat, 1)
        dve.wait_ge(self.powered, i + 1)
        dve.tensor_tensor(self.shift[:, :], self.group[:, :, 0], self.rstd[:, :], ALU.mult).then_inc(self.stat, 1)
        dve.wait_ge(self.stat, n + 9)
        dve.tensor_scalar(self.shift[:, :], self.shift[:, :], -1.0, None, ALU.mult).then_inc(self.stat, 1)
        dve.wait_ge(self.stat, n + 10)

    def ready(self, eng, i):
        eng.wait_ge(self.stat, (i + 1) * self.DVE_STEPS)


def convolution_layer(nc, x_in, z_out, bn_out, par, pairs=PAIRS):
    PAD = 2
    SPAN = SIDE + 2 * PAD
    PE_TAPS = 3
    VEC_TAPS = 9 - PE_TAPS
    ROWS_A_JOB = 16
    JOBS = TILES * SIDE // ROWS_A_JOB
    WIDE = ROWS_A_JOB * SIDE
    Z_JOBS = 2 * JOBS
    STATS = 5

    with ExitStack() as ctx:
        sb, ps, sem = makers(nc, ctx, "conv_")
        x = sb("x", [P, TILES, TOKENS])
        padded = sb("padded", [P, TILES, SPAN, SPAN])
        y = sb("y", [P, TILES, TOKENS])
        z = sb("z", [P, 2, TILES, 512])
        gn = GroupNorm(nc, sb, sem, P)
        pointwise = sb("pointwise", [P, 7, P])
        taps = sb("taps", [P, TILES, 9])
        ident = sb("ident", [P, P])
        diagonal = sb("diagonal", [P, TILES, PE_TAPS, P])
        same = sb("same", [P, 9, P])
        affine = sb("affine", [P, 2, TILES])
        raw = sb("raw", [P, TILES, 8, 6])
        mv = sb("mv", [P, TILES, 2])
        total = sb("total", [P, TILES, 2])
        sq = sb("sq", [P, TILES])
        cols = sb("cols", [P, 2, TILES])

        tap_ps = ps("tap_ps", [P, 2, WIDE])
        z_ps = ps("z_ps", [P, 4, 512])

        par_in, prepared, last = sem("par_in"), sem("prepared"), sem("last")
        x_in_s = [sem(f"x_in{t}") for t in range(TILES)]
        relued, taps_made, tapped = sem("relued"), sem("taps_made"), sem("tapped")
        z_made, z_seen, z_copied, z_stat = sem("z_made"), sem("z_seen"), sem("z_copied"), sem("z_stat")
        stored = [sem("stored0"), sem("stored1")]
        bn_stored = sem("bn_stored")

        rows = x_in.rearrange("(q t p) n -> q p t n", p=P, t=TILES)
        z_rows = z_out.rearrange("(q t p) n -> q p t n", p=P, t=TILES)
        loads = [(pointwise, "pointwise", "b p n -> p b n"), (taps, "taps", None), (ident, "ident", None),
                 (same, "same", "b p n -> p b n"), (affine, "affine", None), (gn.mix, "gn_mix", "b p n -> p b n")]
        block = ctx.enter_context(nc.Block())

        def job(j):
            return divmod(j, TILES)

        def shifted(t, first, count, tap):
            dh, dw = divmod(tap, 3)
            return padded[:, t, first + 2 * dh:first + 2 * dh + count, 2 * dw:2 * dw + SIDE]

        @block.sync
        def _(sp):
            for to, name, view in loads:
                sp.dma_start(to.ap(), par[name] if view is None else par[name].rearrange(view)).then_inc(par_in, 16)

            def load_x(i):
                for t in range(TILES):
                    sp.dma_start(x[:, t, :], rows[i, :, t, :]).then_inc(x_in_s[t], 16)

            def store_z(i):
                for n in range(8):
                    sp.wait_ge(z_copied, i * Z_JOBS + 3 * (n + 1))
                    sp.dma_start(z_rows[i, :, :, 512 * n:512 * n + 512], z[:, n % 2, :, :]).then_inc(stored[n % 2], 16)

            load_x(0)
            if pairs > 1:
                with sp.Fori(0, pairs - 1) as i:
                    sp.wait_ge(relued, (i + 1) * TILES)
                    load_x(i + 1)
                    store_z(i)
            store_z(pairs - 1)
            for s in stored:
                sp.wait_ge(s, pairs * 4 * 16)
            sp.wait_ge(last, 8)
            sp.dma_start(bn_out, cols[:, :, :]).then_inc(bn_stored, 16)
            sp.wait_ge(bn_stored, 16)

        @block.gpsimd
        def _(pool):
            with pool.Fori(0, pairs) as i:
                gn.power(pool, i)
            pool.wait_ge(last, 4)
            pool.tensor_tensor(mv[:, :, 1], mv[:, :, 1], gn.half[:, :], ALU.pow).then_inc(last, 1)

        @block.scalar
        def _(act):
            with act.Fori(0, pairs) as i:
                gn.ready(act, i)
                for t in range(TILES):
                    act.wait_ge(tapped, i * JOBS * VEC_TAPS)
                    act.wait_ge(prepared, 1)
                    act.activation(padded[:, t, PAD:PAD + SIDE, PAD:PAD + SIDE], x[:, t, :].rearrange("p (h w) -> p h w", w=SIDE),
                                   ACT.Relu, bias=gn.shift[:, t:t + 1], scale=gn.rstd[:, t:t + 1]).then_inc(relued, 1)
                for m in range(Z_JOBS):
                    n, t = divmod(m, TILES)
                    act.wait_ge(z_made, i * Z_JOBS + m + 1)
                    act.wait_ge(z_seen, i * Z_JOBS + max(m - 5, 0))
                    if t == 0:
                        act.wait_ge(stored[n % 2], i * 4 * 16 + 16 * (n // 2))
                    act.activation(z[:, n % 2, t, :], z_ps[:, m % 4, :], ACT.Copy).then_inc(z_copied, 1)

        @block.tensor
        def _(pe):
            pe.wait_ge(par_in, 16 * len(loads))
            pe.wait_ge(prepared, 2)
            with pe.Fori(0, pairs) as i:
                def tap_job(j):
                    b, t = job(j)
                    if b == 0:
                        pe.wait_ge(relued, i * TILES + t + 1)
                    pe.wait_ge(tapped, i * JOBS * VEC_TAPS + max(j - 1, 0) * VEC_TAPS)
                    for half in range(2):
                        for tap in range(PE_TAPS):
                            ins = pe.matmul(tap_ps[:, j % 2, 512 * half:512 * half + 512], diagonal[:, t, tap, :],
                                            shifted(t, ROWS_A_JOB * b + 8 * half, 8, tap), start=(tap == 0), stop=(tap == PE_TAPS - 1))
                    ins.then_inc(taps_made, 1)

                def z_job(m):
                    n, t = divmod(m, TILES)
                    pe.wait_ge(tapped, i * JOBS * VEC_TAPS + (n // 2 + 1) * TILES * VEC_TAPS)
                    pe.wait_ge(z_copied, i * Z_JOBS + max(m - 3, 0))
                    for q, s in enumerate(SOURCES[t]):
                        ins = pe.matmul(z_ps[:, m % 4, :], pointwise[:, BLOCK[s, t], :], y[:, s, 512 * n:512 * n + 512],
                                        start=(q == 0), stop=(q == len(SOURCES[t]) - 1))
                    ins.then_inc(z_made, 1)

                pe.wait_ge(z_copied, i * Z_JOBS)
                gn.mix_stats(pe, i, z_ps[:, 0, 0:2 * TILES])
                gn.ready(pe, i)
                tap_job(0)
                for j in range(JOBS + TILES):
                    if j + 1 < JOBS:
                        tap_job(j + 1)
                    if j >= TILES:
                        z_job(2 * (j - TILES))
                        z_job(2 * (j - TILES) + 1)
            pe.wait_ge(last, 1)
            for t in range(TILES):
                for s in range(TILES):
                    ins = pe.matmul(z_ps[:, 0, 2 * t:2 * t + 2], same[:, 3 * s + t, :], total[:, s, :],
                                    start=(s == 0), stop=(s == TILES - 1))
            ins.then_inc(last, 1)

        @block.vector
        def _(dve):
            dve.memset(gn.half[:, :], -0.5)
            dve.memset(total[:, :, :], 0.0)
            dve.memset(padded[:, :, :, :], 0.0).then_inc(prepared, 1)
            dve.wait_ge(par_in, 16 * len(loads))
            for t in range(TILES):
                for tap in range(PE_TAPS):
                    ins = dve.tensor_scalar(diagonal[:, t, tap, :], ident[:, :], taps[:, t, tap:tap + 1], None, ALU.mult)
            ins.then_inc(prepared, 1)

            with dve.Fori(0, pairs) as i:
                gn.statistics(dve, i, x, lambda t: dve.wait_ge(x_in_s[t], (i + 1) * 16))
                gn.scales(dve, i, z_ps[:, 0, 0:2 * TILES])

                def see(m):
                    n, t = divmod(m, TILES)
                    dve.wait_ge(z_copied, i * Z_JOBS + m + 1)
                    dve.bn_stats(raw[:, t, n, :], z[:, n % 2, t, :]).then_inc(z_seen, 1)

                for j in range(JOBS + TILES):
                    if j < JOBS:
                        b, t = job(j)
                        first = ROWS_A_JOB * b
                        at = y[:, t, first * SIDE:(first + ROWS_A_JOB) * SIDE].rearrange("p (h w) -> p h w", w=SIDE)
                        dve.wait_ge(taps_made, i * JOBS + j + 1)
                        dve.wait_ge(z_made, i * Z_JOBS)
                        for n, tap in enumerate(range(PE_TAPS, 9)):
                            if n:
                                dve.wait_ge(tapped, (i * JOBS + j) * VEC_TAPS + n)
                            so_far = at if n else tap_ps[:, j % 2, :].rearrange("p (h w) -> p h w", w=SIDE)
                            dve.scalar_tensor_tensor(out=at, in0=shifted(t, first, ROWS_A_JOB, tap), scalar=taps[:, t, tap:tap + 1],
                                                     in1=so_far, op0=ALU.mult, op1=ALU.add).then_inc(tapped, 1)
                    if j >= TILES:
                        see(2 * (j - TILES))
                        see(2 * (j - TILES) + 1)
                dve.wait_ge(z_seen, (i + 1) * Z_JOBS)
                dve.memset(sq[:, :], 0.0)
                for t in range(TILES):
                    ins = dve.bn_aggr(mv[:, t, :], raw[:, t, :, :])
                ins.then_inc(z_stat, 1)
                dve.wait_ge(z_stat, i * STATS + 1)
                dve.tensor_tensor(sq[:, :], mv[:, :, 0], mv[:, :, 0], ALU.mult).then_inc(z_stat, 1)
                dve.wait_ge(z_stat, i * STATS + 2)
                dve.tensor_tensor(mv[:, :, 1], mv[:, :, 1], sq[:, :], ALU.add).then_inc(z_stat, 1)
                dve.wait_ge(z_stat, i * STATS + 3)
                dve.tensor_tensor(total[:, :, :], total[:, :, :], mv[:, :, :], ALU.add).then_inc(z_stat, 1)
                dve.wait_ge(z_stat, i * STATS + 4)
                dve.tensor_copy(sq[:, :], mv[:, :, 0]).then_inc(z_stat, 1)
            dve.wait_ge(z_stat, pairs * STATS)
            dve.tensor_copy(total[:, :, :], total[:, :, :]).then_inc(last, 1)
            dve.wait_ge(last, 2)
            dve.tensor_copy(mv[:, :, :], z_ps[:, 0, 0:2 * TILES].rearrange("p (t c) -> p t c", c=2)).then_inc(z_stat, 1)
            dve.wait_ge(z_stat, pairs * STATS + 1)
            dve.tensor_tensor(sq[:, :], mv[:, :, 0], mv[:, :, 0], ALU.mult).then_inc(last, 1)
            dve.wait_ge(last, 3)
            dve.tensor_tensor(mv[:, :, 1], mv[:, :, 1], sq[:, :], ALU.subtract).then_inc(z_stat, 1)
            dve.wait_ge(z_stat, pairs * STATS + 2)
            dve.tensor_scalar(mv[:, :, 1], mv[:, :, 1], 0.0, BN_EPS, ALU.max, ALU.add).then_inc(last, 1)
            dve.wait_ge(last, 5)
            dve.tensor_tensor(cols[:, 0, :], mv[:, :, 1], affine[:, 0, :], ALU.mult).then_inc(last, 1)
            dve.wait_ge(last, 6)
            dve.tensor_tensor(sq[:, :], mv[:, :, 0], cols[:, 0, :], ALU.mult).then_inc(last, 1)
            dve.wait_ge(last, 7)
            dve.tensor_tensor(cols[:, 1, :], affine[:, 1, :], sq[:, :], ALU.subtract).then_inc(last, 1)


def fourier_layer(nc, x_in, x_out, par, tag, batch_norm=None, pairs=PAIRS):
    G = 16
    C1 = 3 * G
    MIX = 2 * G
    HB = 8
    NB = SIDE // HB
    ROUND = 12582912.0
    TWO_PI = 6.2831850
    ACT_JOBS = dict(conv1=8, forward=8, turned=10, turned_s=2, phase=4, inverse=8, final=8)
    VEC_JOBS = dict(forward=8, spatial=2, fourier=2, magnitude=4, inverse=6, final=24)
    ACT_TOTAL, VEC_TOTAL = sum(ACT_JOBS.values()), sum(VEC_JOBS.values())

    def place(jobs, name):
        return sum(list(jobs.values())[:list(jobs).index(name)])

    LUTS, CALCS = 11, 19

    def blocked(plane):
        return plane.rearrange("p c h -> p (c h)").rearrange("p (b c r) -> p c b r", b=NB, c=G)

    def by_block(plane):
        return plane.rearrange("p c (b r) -> p c b r", b=NB)

    def block_of(plane, b):
        return plane.rearrange("p c h -> p (c h)")[:, b * P:(b + 1) * P]

    with ExitStack() as ctx:
        sb, ps, sem = makers(nc, ctx, tag)
        x = sb("x", [P, TILES, TOKENS])
        xn = sb("xn", [P, TILES, TOKENS])
        flat = xn[:, :, :].rearrange("p t n -> p (t n)")
        field = flat[:, 0:4096].rearrange("p (r c h) -> p r c h", r=2, c=MIX)
        w0, w1 = (flat[:, 4096 + 2048 * j:6144 + 2048 * j].rearrange("p (c h) -> p c h", c=MIX) for j in range(2))
        cat_t = flat[:, 8192:12288]
        mixed_in = cat_t.rearrange("p (z b n) -> p z b n", z=4, b=NB)
        cat = sb("cat", [P, 64, SIDE])
        half_way = sb("half_way", [P, MIX // 2, 256])
        halves = half_way[:, :, :].rearrange("p a n -> p (a n)")
        w2, w3 = (halves[:, 2048 * j:2048 * j + 2048].rearrange("p (c h) -> p c h", c=MIX) for j in range(2))
        spatial_in = sb("spatial_in", [P, NB, P + 2])

        gn = GroupNorm(nc, sb, sem, P)
        trans = sb("trans", [P, 5, 2, 256])
        FRFT, FFT, IFRFT, IFFT_W, IFFT_H = range(5)
        conv1 = sb("conv1", [P, TILES, C1])
        mixers = sb("mixers", [P, 4, P])
        MAG_F, MAG, PHA, CONV_1 = range(4)
        spatial = sb("spatial", [P, 9, P])
        ident = sb("ident", [P, P])
        conv2 = sb("conv2", [P, 2 * CH])
        conv0 = sb("conv0", [2 * G, P])
        conv2_0 = sb("conv2_0", [2 * G, 2 * CH])
        bias0 = sb("bias0", [2 * G, 1])
        rows_in = sb("rows_in", [P, 6, G])
        mask = sb("mask", [P, SIDE])
        bias_map = sb("bias_map", [P, G, SIDE])
        turn_bias = sb("turn_bias", [P, MIX])
        out_bias = sb("out_bias", [P, TILES])
        quarter = sb("quarter", [P, 1])
        bn_cols = sb("bn_cols", [P, 2, TILES])

        act_ps = ps("act_ps", [P, 4, 512])
        vec_ps = ps("vec_ps", [P, 4, 512])

        par_in, prepared, bias_steps = sem("par_in"), sem("prepared"), sem("bias_steps")
        x_in_s = [sem(f"x_in{t}") for t in range(TILES)]
        z_in_s = [sem(f"z_in{t}") for t in range(TILES)]
        shifted, based, normed = sem("shifted"), sem("based"), sem("normed")
        act_made, act_read = sem("act_made"), sem("act_read")
        vec_made, vec_read = sem("vec_made"), sem("vec_read")
        lut, calc = sem("lut"), sem("calc")
        stored = sem("stored")

        src = x_in.rearrange("(q t p) n -> q p t n", p=P, t=TILES)
        dst = x_out.rearrange("(q t p) n -> q p t n", p=P, t=TILES)
        loads = [
            (trans, "trans", "f p r n -> p f r n"), (mixers, "mixers", "b p n -> p b n"),
            (spatial, "spatial", "b p n -> p b n"), (ident, "ident", None), (conv2, "conv2_rest", None),
            (conv1, "conv1", "t p n -> p t n"), (conv0, "conv0", None), (conv2_0, "conv2_0", None),
            (bias0, "bias0", None), (rows_in, "rows", None), (mask, "mask", None), (gn.mix, "gn_mix", "b p n -> p b n")]
        if batch_norm:
            z_rows = batch_norm[0].rearrange("(q t p) n -> q p t n", p=P, t=TILES)
            loads.append((bn_cols, "bn_cols", None))
        N_LOADS = len(loads)
        MAG_S_B, MAG_F_B, MAG_B, CONV_1_B, PHA_B, CONV_1_B2 = range(6)

        block = ctx.enter_context(nc.Block())

        @block.sync
        def _(sp):
            for to, name, view in loads:
                here = par[name] if view is None else par[name].rearrange(view)
                sp.dma_start(to.ap() if hasattr(to, "ap") and callable(to.ap) else to, here).then_inc(par_in, 16)
            with sp.Fori(0, pairs) as i:
                sp.wait_ge(stored, i * 16)
                for t in range(TILES):
                    sp.dma_start(x[:, t, :], src[i, :, t, :]).then_inc(x_in_s[t], 16)
                    if batch_norm:
                        sp.dma_start(xn[:, t, :], z_rows[i, :, t, :]).then_inc(z_in_s[t], 16)
                sp.wait_ge(vec_read, (i + 1) * VEC_TOTAL)
                sp.dma_start(dst[i, :, :, :], x[:, :, :]).then_inc(stored, 16)
            sp.wait_ge(stored, pairs * 16)

        @block.gpsimd
        def _(pool):
            with pool.Fori(0, pairs) as i:
                gn.power(pool, i)

        @block.scalar
        def _(act):
            with act.Fori(0, pairs) as i:
                if batch_norm:
                    for t in range(TILES):
                        act.wait_ge(par_in, 16 * N_LOADS)
                        act.wait_ge(z_in_s[t], (i + 1) * 16)
                        act.activation(xn[:, t, :], xn[:, t, :], ACT.Identity, bias=bn_cols[:, 1, t:t + 1],
                                       scale=bn_cols[:, 0, t:t + 1]).then_inc(shifted, 1)

                def read(name, j, out, **kw):
                    m = place(ACT_JOBS, name) + j
                    act.wait_ge(act_made, i * ACT_TOTAL + m + 1)
                    bank = act_ps[:, m % 4, :]
                    return act.activation(out, kw.pop("view", lambda b: b)(bank), ACT.Copy, **kw).then_inc(act_read, 1)

                def step(n, *args, **kw):
                    act.activation(*args, **kw).then_inc(lut, 1)

                for j in range(8):
                    read("conv1", j, cat[:, 0:C1, 8 * j:8 * j + 8].rearrange("p c h -> p h c"),
                         view=lambda b: b.rearrange("p (h c) -> p h c", c=64)[:, :, 0:C1])
                for j in range(8):
                    read("forward", j, half_way[:, 2 * j:2 * j + 2, :].rearrange("p a n -> p (a n)"))
                act.wait_ge(vec_read, i * VEC_TOTAL + 8)
                step(1, w0, field[:, 0], ACT.Square)
                step(2, w1, field[:, 1], ACT.Square)
                act.wait_ge(calc, i * CALCS + 1)
                step(3, w1, w0, ACT.Sqrt)
                act.wait_ge(calc, i * CALCS + 5)
                step(4, w2, w0, ACT.Arctan)
                act.wait_ge(calc, i * CALCS + 10)
                step(5, blocked(w2[:, 0:G]), by_block(w1[:, G:MIX]), ACT.Copy)
                for plane in range(5):
                    for half in range(2):
                        if plane == 0:
                            read("turned", half, spatial_in[:, 4 * half:4 * half + 4, 1:P + 1],
                                 view=lambda b: b.rearrange("p (b w) -> p b w", b=4))
                        else:
                            read("turned", 2 * plane + half, mixed_in[:, plane - 1, 4 * half:4 * half + 4, :]
                                 .rearrange("p b n -> p (b n)"))
                act.wait_ge(vec_read, i * VEC_TOTAL + place(VEC_JOBS, "magnitude"))
                for half in range(2):
                    read("turned_s", half, mixed_in[:, 0, 4 * half:4 * half + 4, :].rearrange("p b n -> p (b n)"))
                for j in range(4):
                    g, half = divmod(j, 2)
                    read("phase", j, w3[:, G * g:G * g + G, 32 * half:32 * half + 32],
                         view=lambda b: b.rearrange("p (o h) -> p o h", h=32), scale=1.0 / math.pi)
                act.wait_ge(calc, i * CALCS + 16)
                step(6, w0, w3, ACT.Abs)
                step(7, w2, w3, ACT.Sin, scale=TWO_PI)
                act.wait_ge(lut, i * LUTS + 6)
                step(8, w0, w0, ACT.Sin, scale=-TWO_PI, bias=quarter[:, 0:1])
                for j in range(8):
                    read("inverse", j, half_way[:, 2 * j:2 * j + 2, :].rearrange("p a n -> p (a n)"))
                act.wait_ge(vec_read, i * VEC_TOTAL + place(VEC_JOBS, "inverse") + 4)
                step(9, w0[:, 0:G], field[:, 0, 0:G], ACT.Square)
                step(10, w1[:, 0:G], field[:, 1, 0:G], ACT.Square)
                act.wait_ge(calc, i * CALCS + 19)
                step(11, cat[:, G:2 * G, :], w0[:, 0:G], ACT.Sqrt)
                for j in range(8):
                    read("final", j, cat_t[:, 512 * j:512 * j + 512])

        @block.tensor
        def _(pe):
            pe.wait_ge(par_in, 16 * N_LOADS)
            pe.matmul(vec_ps[:, 0, 0:2 * CH], conv0[:, :], conv2_0[:, :], start=True, stop=True)
            for t in range(TILES):
                ins = pe.matmul(vec_ps[:, 1, t:t + 1], conv2_0[:, t * P:t * P + P], bias0[:, :], start=True, stop=True)
            ins.then_inc(prepared, 1)
            pe.wait_ge(prepared, 2)

            with pe.Fori(0, pairs) as i:
                def bank_for_act(name, j):
                    m = place(ACT_JOBS, name) + j
                    pe.wait_ge(act_read, i * ACT_TOTAL + max(m - 3, 0))
                    return act_ps[:, m % 4, :]

                def bank_for_vec(name, j):
                    m = place(VEC_JOBS, name) + j
                    pe.wait_ge(vec_read, i * VEC_TOTAL + max(m - 3, 0))
                    return vec_ps[:, m % 4, :]

                pe.wait_ge(vec_read, i * VEC_TOTAL)
                gn.mix_stats(pe, i, vec_ps[:, 0, 0:2 * TILES])
                pe.wait_ge(normed, (i + 1) * TILES)
                for j in range(8):
                    bank = bank_for_act("conv1", j)
                    for r in range(8):
                        at = slice((8 * j + r) * SIDE, (8 * j + r + 1) * SIDE)
                        out = bank[:, 64 * r:64 * r + C1]
                        pe.matmul(out[0:64], xn[:, 0, at], conv1[:, 0, :], start=True, stop=False)
                        pe.matmul(out[0:64], xn[0:64, 1, at], conv1[0:64, 1, :], start=False, stop=True)
                        pe.matmul(out[64:128], xn[:, 2, at], conv1[:, 2, :], start=True, stop=False)
                        ins = pe.matmul(out[64:128], xn[64:128, 1, at], conv1[64:128, 1, :], start=False, stop=True)
                    ins.then_inc(act_made, 1)
                pe.wait_ge(act_read, i * ACT_TOTAL + 8)
                for j in range(8):
                    bank = bank_for_act("forward", j)
                    for a in range(2):
                        c = G + 4 * j + 2 * a
                        ins = pe.matmul(bank[:, 256 * a:256 * a + 256], cat[:, c:c + 2, :], trans[:, FRFT if j < 4 else FFT, 0, :],
                                        start=True, stop=True)
                    ins.then_inc(act_made, 1)
                for j in range(8):
                    pe.wait_ge(act_read, i * ACT_TOTAL + place(ACT_JOBS, "forward") + j + 1)
                    bank = bank_for_vec("forward", j)
                    for a in range(2):
                        for r in range(2):
                            ins = pe.matmul(bank[:, 256 * a:256 * a + 256], half_way[:, 2 * j + a, P * r:P * r + P],
                                            trans[:, FRFT if j < 4 else FFT, r, :], start=(r == 0), stop=(r == 1))
                    ins.then_inc(vec_made, 1)

                def turn(name, j, plane, half):
                    bank = bank_for_act(name, j)
                    for b in range(4):
                        ins = pe.matmul(bank[:, P * b:P * b + P], block_of(plane, 4 * half + b), ident[:, :], start=True, stop=True)
                    ins.then_inc(act_made, 1)

                pe.wait_ge(calc, i * CALCS + 12)
                pe.wait_ge(lut, i * LUTS + 5)
                for n, plane in enumerate((w0[:, 0:G], w0[:, G:MIX], w3[:, 0:G], w2[:, 0:G], w3[:, G:MIX])):
                    for half in range(2):
                        turn("turned", 2 * n + half, plane, half)

                pe.wait_ge(act_read, i * ACT_TOTAL + place(ACT_JOBS, "turned") + 4)
                for half in range(2):
                    bank = bank_for_vec("spatial", half).rearrange("p (o h) -> p o h", h=32)
                    for b in range(4):
                        q = 4 * half + b
                        terms = [(dw, n, q + n - 1) for dw in range(3) for n in range(3) if 0 <= q + n - 1 < NB]
                        for dw, n, from_q in terms:
                            ins = pe.matmul(bank[:, :, HB * b:HB * b + HB], spatial_in[:, from_q, dw:dw + P],
                                            spatial[:, 3 * dw + n, :], start=((dw, n, from_q) == terms[0]),
                                            stop=((dw, n, from_q) == terms[-1]))
                    ins.then_inc(vec_made, 1)

                def mix(bank, source, w, half, made):
                    bank = bank.rearrange("p (o h) -> p o h", h=32)
                    for b in range(4):
                        ins = pe.matmul(bank[:, :, HB * b:HB * b + HB], mixed_in[:, source, 4 * half + b, :], mixers[:, w, :],
                                        start=True, stop=True)
                    ins.then_inc(made, 1)

                for half in range(2):
                    mix(bank_for_vec("fourier", half), 0, MAG_F, half, vec_made)
                pe.wait_ge(act_read, i * ACT_TOTAL + place(ACT_JOBS, "turned_s"))
                pe.wait_ge(calc, i * CALCS + 13)
                for half in range(2):
                    turn("turned_s", half, w2[:, G:MIX], half)
                for j in range(4):
                    mix(bank_for_act("phase", j), (1, 3)[j // 2], (PHA, CONV_1)[j // 2], j % 2, act_made)
                pe.wait_ge(act_read, i * ACT_TOTAL + place(ACT_JOBS, "phase"))
                for j in range(4):
                    mix(bank_for_vec("magnitude", j), (0, 2)[j // 2], (MAG, CONV_1)[j // 2], j % 2, vec_made)

                pe.wait_ge(calc, i * CALCS + 18)
                for j in range(8):
                    bank = bank_for_act("inverse", j)
                    for a in range(2):
                        c = 4 * j + 2 * a
                        for r in range(2):
                            ins = pe.matmul(bank[:, 256 * a:256 * a + 256], field[:, r, c:c + 2, :],
                                            trans[:, IFRFT if j < 4 else IFFT_W, r, :], start=(r == 0), stop=(r == 1))
                    ins.then_inc(act_made, 1)
                for j in range(6):
                    n = 2 * (j + 1) if j < 4 else 8 + 4 * (j - 3)
                    pe.wait_ge(act_read, i * ACT_TOTAL + place(ACT_JOBS, "inverse") + n // 2)
                    bank = bank_for_vec("inverse", j)
                    per = 2 if j < 4 else 4
                    width = 512 // per
                    for a in range(per):
                        for r in range(2):
                            ins = pe.matmul(bank[:, width * a:width * a + width], half_way[:, n - per + a, P * r:P * r + P],
                                            trans[:, IFRFT if j < 4 else IFFT_H, r, 0:width], start=(r == 0), stop=(r == 1))
                    ins.then_inc(vec_made, 1)

                pe.wait_ge(lut, i * LUTS + 11)
                pe.wait_ge(vec_read, i * VEC_TOTAL + place(VEC_JOBS, "final"))
                for j in range(8):
                    bank = bank_for_act("final", j)
                    for r in range(8):
                        for im in (slice(0, 64), slice(64, 128)):
                            ins = pe.matmul(bank[im, 64 * r:64 * r + 64], cat[:, :, 8 * j + r], ident[:, im],
                                            start=True, stop=True)
                    ins.then_inc(act_made, 1)
                for j in range(8):
                    pe.wait_ge(act_read, i * ACT_TOTAL + place(ACT_JOBS, "final") + j + 1)
                    for t in range(TILES):
                        bank = bank_for_vec("final", 3 * j + t)
                        pe.matmul(bank, conv2[:, t * P:t * P + P], cat_t[:, 512 * j:512 * j + 512],
                                  start=True, stop=True).then_inc(vec_made, 1)

        @block.vector
        def _(dve):
            dve.memset(gn.half[:, :], -0.5)
            dve.memset(quarter[:, :], math.pi / 2)
            dve.memset(spatial_in[:, :, :], 0.0)
            dve.memset(cat[:, :, :], 0.0)
            dve.wait_ge(par_in, 16 * N_LOADS)
            by_channel = lambda r: rows_in[:, r, :].unsqueeze(2).to_broadcast([P, G, SIDE])
            by_row = mask[:, :].unsqueeze(1).to_broadcast([P, G, SIDE])
            dve.tensor_scalar(turn_bias[:, :], rows_in[:, PHA_B:PHA_B + 2, :].rearrange("p a c -> p (a c)"),
                              1.0 / (2 * math.pi), None, ALU.mult)
            dve.tensor_tensor(bias_map[:, :, :], by_channel(MAG_S_B), by_row, ALU.mult).then_inc(bias_steps, 1)
            dve.tensor_tensor(w2[:, 0:G], by_channel(MAG_F_B), by_row, ALU.mult).then_inc(bias_steps, 1)
            dve.wait_ge(bias_steps, 2)
            dve.tensor_tensor(w2[:, 0:G], by_channel(MAG_F_B), w2[:, 0:G], ALU.subtract).then_inc(bias_steps, 1)
            dve.wait_ge(bias_steps, 3)
            dve.tensor_tensor(bias_map[:, :, :], bias_map[:, :, :], w2[:, 0:G], ALU.add).then_inc(bias_steps, 1)
            dve.wait_ge(prepared, 1)
            dve.tensor_copy(out_bias[:, :], vec_ps[:, 1, 0:TILES])
            dve.wait_ge(bias_steps, 4)
            dve.tensor_tensor(conv2[:, :], vec_ps[:, 0, 0:2 * CH], conv2[:, :], ALU.add).then_inc(prepared, 1)
            dve.wait_ge(prepared, 2)

            with dve.Fori(0, pairs) as i:
                def base(t):
                    dve.wait_ge(x_in_s[t], (i + 1) * 16)
                    if batch_norm:
                        dve.wait_ge(shifted, i * TILES + t + 1)
                        dve.tensor_tensor(x[:, t, :], x[:, t, :], xn[:, t, :], ALU.add).then_inc(based, 1)
                        dve.wait_ge(based, i * TILES + t + 1)

                gn.statistics(dve, i, x, base)
                gn.scales(dve, i, vec_ps[:, 0, 0:2 * TILES])
                for t in range(TILES):
                    dve.tensor_scalar(xn[:, t, :], x[:, t, :], gn.rstd[:, t:t + 1], gn.shift[:, t:t + 1],
                                      ALU.mult, ALU.add).then_inc(normed, 1)

                def bank_of(name, j):
                    m = place(VEC_JOBS, name) + j
                    dve.wait_ge(vec_made, i * VEC_TOTAL + m + 1)
                    return vec_ps[:, m % 4, :]

                def after(n):
                    dve.wait_ge(calc, i * CALCS + n)

                re, im = field[:, 0], field[:, 1]
                for j in range(8):
                    dve.tensor_copy(field[:, :, 4 * j:4 * j + 4, :].rearrange("p r (a c) h -> p r a (c h)", a=2),
                                    bank_of("forward", j).rearrange("p (a r n) -> p r a n", a=2, r=2)).then_inc(vec_read, 1)
                dve.wait_ge(lut, i * LUTS + 2)
                dve.tensor_tensor(w0, w0, w1, ALU.add).then_inc(calc, 1)
                dve.wait_ge(lut, i * LUTS + 3)
                dve.scalar_tensor_tensor(out=w0, in0=re, scalar=-1.0, in1=re, op0=ALU.mult, op1=ALU.max).then_inc(calc, 1)
                after(2)
                dve.scalar_tensor_tensor(out=w0, in0=w0, scalar=1e-30, in1=w1, op0=ALU.max, op1=ALU.add).then_inc(calc, 1)
                after(3)
                dve.reciprocal(w0, w0).then_inc(calc, 1)
                after(4)
                dve.tensor_tensor(w0, w0, im, ALU.mult).then_inc(calc, 1)
                dve.wait_ge(lut, i * LUTS + 4)
                dve.tensor_scalar(w0, im, 0.0, math.pi, ALU.is_ge, ALU.mult).then_inc(calc, 1)
                after(6)
                dve.scalar_tensor_tensor(out=w0, in0=w2, scalar=-2.0, in1=w0, op0=ALU.mult, op1=ALU.add).then_inc(calc, 1)
                dve.tensor_scalar(w3, re, 0.0, None, ALU.is_lt).then_inc(calc, 1)
                after(8)
                dve.scalar_tensor_tensor(out=w0, in0=w0, scalar=-math.pi / 2, in1=w3, op0=ALU.add, op1=ALU.mult).then_inc(calc, 1)
                after(9)
                for g in (0, G):
                    ins = dve.tensor_tensor(blocked(w3[:, g:g + G]), by_block(w2[:, g:g + G]), by_block(w0[:, g:g + G]), ALU.add)
                ins.then_inc(calc, 1)
                after(10)
                dve.tensor_tensor(blocked(w0[:, 0:G]), by_block(w1[:, 0:G]), by_block(by_row), ALU.mult).then_inc(calc, 1)
                after(11)
                dve.tensor_tensor(blocked(w0[:, G:MIX]), by_block(w1[:, 0:G]), blocked(w0[:, 0:G]), ALU.subtract).then_inc(calc, 1)

                dve.wait_ge(act_read, i * ACT_TOTAL + place(ACT_JOBS, "turned_s"))
                for half in range(2):
                    rows = slice(32 * half, 32 * half + 32)
                    dve.tensor_tensor(w0[:, 0:G, rows], bank_of("spatial", half).rearrange("p (o h) -> p o h", h=32),
                                      by_row[:, :, rows], ALU.mult).then_inc(vec_read, 1)
                for half in range(2):
                    rows = slice(32 * half, 32 * half + 32)
                    dve.wait_ge(vec_read, i * VEC_TOTAL + place(VEC_JOBS, "spatial") + half + 1)
                    dve.tensor_tensor(w0[:, 0:G, rows], bank_of("fourier", half).rearrange("p (o h) -> p o h", h=32),
                                      w0[:, 0:G, rows], ALU.add).then_inc(vec_read, 1)
                dve.wait_ge(vec_read, i * VEC_TOTAL + place(VEC_JOBS, "magnitude"))
                dve.tensor_tensor(blocked(w2[:, G:MIX]), by_block(w0[:, 0:G]), by_block(bias_map[:, :, :]), ALU.add).then_inc(calc, 1)
                for j in range(4):
                    g, half = divmod(j, 2)
                    bias = rows_in[:, MAG_B + g, :].unsqueeze(2).to_broadcast([P, G, 32])
                    dve.tensor_tensor(w1[:, G * g:G * g + G, 32 * half:32 * half + 32],
                                      bank_of("magnitude", j).rearrange("p (o h) -> p o h", h=32), bias, ALU.add)\
                        .then_inc(vec_read, 1)
                dve.wait_ge(act_read, i * ACT_TOTAL + place(ACT_JOBS, "inverse"))
                dve.tensor_tensor(w3, w3, turn_bias[:, :].unsqueeze(2).to_broadcast([P, MIX, SIDE]), ALU.add).then_inc(calc, 1)
                after(14)
                dve.tensor_scalar(w0, w3, ROUND, -ROUND, ALU.add, ALU.add).then_inc(calc, 1)
                after(15)
                dve.tensor_tensor(w3, w3, w0, ALU.subtract).then_inc(calc, 1)
                dve.wait_ge(lut, i * LUTS + 8)
                dve.wait_ge(vec_read, i * VEC_TOTAL + place(VEC_JOBS, "inverse"))
                dve.tensor_tensor(re, w1, w0, ALU.mult).then_inc(calc, 1)
                dve.tensor_tensor(im, w1, w2, ALU.mult).then_inc(calc, 1)
                for j in range(4):
                    dve.tensor_copy(field[:, :, 4 * j:4 * j + 4, :].rearrange("p r (a c) h -> p r a (c h)", a=2),
                                    bank_of("inverse", j).rearrange("p (a r n) -> p r a n", a=2, r=2)).then_inc(vec_read, 1)
                for j in range(4, 6):
                    c = 2 * G + 8 * (j - 4)
                    dve.tensor_copy(cat[:, c:c + 8, :].rearrange("p c h -> p (c h)"), bank_of("inverse", j)).then_inc(vec_read, 1)
                dve.wait_ge(lut, i * LUTS + 10)
                dve.tensor_tensor(w0[:, 0:G], w0[:, 0:G], w1[:, 0:G], ALU.add).then_inc(calc, 1)
                for j in range(8):
                    for t in range(TILES):
                        at = slice(512 * j, 512 * j + 512)
                        dve.scalar_tensor_tensor(out=x[:, t, at], in0=bank_of("final", 3 * j + t), scalar=out_bias[:, t:t + 1],
                                                 in1=x[:, t, at], op0=ALU.add, op1=ALU.add).then_inc(vec_read, 1)


def wkv_layer(nc, x_in, x_out, par, pairs=PAIRS):
    T = 512
    STEPS = TOKENS // T
    UNITS = TILES * STEPS * 2
    ORDER = [b for s in range(STEPS // 2) for b in (s, STEPS - 1 - s)]
    BLOCKS = TILES * STEPS

    def unit(u):
        t, s, d = u // (2 * STEPS), u // 2 % STEPS, u % 2
        return t, s, d, (s if d == 0 else STEPS - 1 - s), u % 3

    def folds(u):
        t, r = divmod(u, 2 * STEPS)
        return t * 4 * STEPS + min(r, STEPS) + 3 * max(r - STEPS, 0)

    def copies_before(t, b, which):
        return (t * STEPS + ORDER.index(b)) * 2 + which

    def last_visit(t, b):
        s, d = (b, 0) if b >= STEPS // 2 else (STEPS - 1 - b, 1)
        return (t * STEPS + s) * 2 + d

    with ExitStack() as ctx:
        sb, ps, sem = makers(nc, ctx, "wkv_")
        xn = sb("xn", [P, TILES, TOKENS])
        h = sb("h", [P, TILES, TOKENS])
        k = sb("k", [P, TOKENS])
        v = sb("v", [P, TOKENS])
        gate = sb("gate", [P, TOKENS])
        top = sb("top", [P, 3, T + 2])
        rise = sb("rise", [P, 3, T])
        decay = sb("decay", [P, 3, T])
        own = sb("own", [P, 3, T])
        own_v = sb("own_v", [P, 3, T])
        qp = sb("qp", [P, 3, 2, T + 2])
        wk, wv, wr, wo = (sb(n, [P, 7, P]) for n in ("wk", "wv", "wr", "wo"))
        centre = h[:, 0, 0:7 * P].rearrange("p (b n) -> p b n", b=7)
        wo_raw = h[:, 1, 0:7 * P].rearrange("p (b n) -> p b n", b=7)
        col = sb("col", [P, 8, TILES])
        LNG, LNB, WD, U, OB = range(5)
        gn = GroupNorm(nc, sb, sem, P)
        ones = sb("ones", [P, 3, P])
        half_log = sb("half_log", [P, 1])
        squares = gate[:, 0:6 * T].rearrange("p (r t n) -> p r t n", r=2, t=TILES)
        spread = gate[:, 6 * T:8 * T].rearrange("p (r n) -> p r n", r=2)
        x_again = k[:, 0:6 * T].rearrange("p (r t n) -> p r t n", r=2, t=TILES)
        result = v[:, 0:6 * T].rearrange("p (r t n) -> p r t n", r=2, t=TILES)
        mean_sq = k[:, 6 * T:8 * T].rearrange("p (r n) -> p r n", r=2)

        kv_ps = ps("kv_ps", [P, 4, 512])
        gate_ps = ps("gate_ps", [P, 2, 512])
        stat_ps = ps("stat_ps", [P, 2, 512])

        par_in, prepared = sem("par_in"), sem("prepared")
        x_in_s = [sem(f"x_in{t}") for t in range(TILES)]
        normed = sem("normed")
        kv_made, kv_copied = sem("kv_made"), sem("kv_copied")
        gate_made, gate_ready = sem("gate_made"), sem("gate_ready")
        trend, weighted, sums, fraction, inverse, folded = (
            sem(n) for n in ("trend", "weighted", "sums", "fraction", "inverse", "folded"))
        squared, stats_made, var_ready, rs_ready, out_made, scaled, out_ready = (
            sem(n) for n in ("squared", "stats_made", "var_ready", "rs_ready", "out_made", "scaled", "out_ready"))
        again_in = [sem("again_in0"), sem("again_in1")]
        stored = [sem("stored0"), sem("stored1")]

        rows = x_in.rearrange("(q t p) n -> q p t n", p=P, t=TILES)
        out_rows = x_out.rearrange("(q t p) n -> q p t n", p=P, t=TILES)
        block = ctx.enter_context(nc.Block())
        LOADS = 10

        @block.sync
        def _(sp):
            for dst, name in ((wk, "wk"), (wv, "wv"), (wr, "wr")):
                sp.dma_start(dst[:, :, :], par[name].rearrange("b p n -> p b n")).then_inc(par_in, 16)
            sp.dma_start(wo_raw, par["wo"].rearrange("b p n -> p b n")).then_inc(par_in, 16)
            sp.dma_start(centre, par["centre"].rearrange("b p n -> p b n")).then_inc(par_in, 16)
            sp.dma_start(gn.mix[:, :, :], par["gn_mix"].rearrange("b p n -> p b n")).then_inc(par_in, 16)
            sp.dma_start(ones[:, :, :], par["image_mean"].rearrange("t p n -> p t n")).then_inc(par_in, 16)
            for c, name in ((LNG, "ln_g"), (LNB, "ln_b"), (WD, "w_decay")):
                sp.dma_start(col[:, c, :], par[name]).then_inc(par_in, 16)
            sp.dma_start(col[:, U, :], par["u"]).then_inc(par_in, 16)

            def load_x(i):
                for t in range(TILES):
                    sp.dma_start(xn[:, t, :], rows[i, :, t, :]).then_inc(x_in_s[t], 16)

            def final_traffic(i):
                def load(b):
                    if b < 2:
                        sp.wait_ge(folded, (i + 1) * folds(UNITS))
                    else:
                        sp.wait_ge(out_ready, i * BLOCKS + 3 * (b - 1))
                    sp.dma_start(x_again[:, b % 2, :, :], rows[i, :, :, b * T:(b + 1) * T]).then_inc(again_in[b % 2], 16)

                load(0)
                load(1)
                for b in range(STEPS):
                    sp.wait_ge(out_ready, i * BLOCKS + 3 * (b + 1))
                    sp.dma_start(out_rows[i, :, :, b * T:(b + 1) * T], result[:, b % 2, :, :]).then_inc(stored[b % 2], 16)
                    if b + 2 < STEPS:
                        load(b + 2)

            load_x(0)
            if pairs > 1:
                with sp.Fori(0, pairs - 1) as i:
                    sp.wait_ge(gate_made, i * BLOCKS + BLOCKS)
                    load_x(i + 1)
                    final_traffic(i)
            final_traffic(pairs - 1)
            for s in stored:
                sp.wait_ge(s, pairs * 16 * STEPS // 2)

        @block.gpsimd
        def _(pool):
            with pool.Fori(0, pairs) as i:
                gn.power(pool, i)
                for u in range(UNITS):
                    t, s, d, c, z = unit(u)
                    own_pos = slice(0, T) if d == 0 else slice(1, T + 1)
                    n = i * 4 * UNITS + 4 * u
                    pool.wait_ge(sums, n + 4)
                    pool.tensor_tensor(decay[:, z, :], rise[:, z, :], qp[:, z, 1, own_pos], ALU.mult).then_inc(fraction, 1)
                    pool.wait_ge(fraction, n + 1)
                    pool.tensor_tensor(decay[:, z, :], decay[:, z, :], own_v[:, z, :], ALU.add).then_inc(fraction, 1)
                    pool.tensor_tensor(rise[:, z, :], rise[:, z, :], qp[:, z, 0, own_pos], ALU.mult).then_inc(fraction, 1)
                    pool.wait_ge(fraction, n + 3)
                    pool.tensor_tensor(rise[:, z, :], rise[:, z, :], own[:, z, :], ALU.add).then_inc(fraction, 1)

        @block.scalar
        def _(act):
            act.wait_ge(par_in, 16 * (LOADS + 1))
            act.activation(col[:, 5, :], col[:, WD, :], ACT.Exp).then_inc(prepared, 1)

            with act.Fori(0, pairs) as i:
                def copy(t, b, which):
                    m = copies_before(t, b, which)
                    act.wait_ge(kv_made, i * 2 * BLOCKS + m + 1)
                    if t:
                        u = last_visit(t - 1, b)
                        if which == 0:
                            act.wait_ge(trend, i * 4 * UNITS + 4 * u + 4)
                        else:
                            act.wait_ge(sums, i * 4 * UNITS + 4 * u + 2)
                    elif which == 0:
                        act.wait_ge(out_ready, i * BLOCKS)
                    else:
                        for q in stored:
                            act.wait_ge(q, i * 16 * STEPS // 2)
                    act.activation((k, v)[which][:, b * T:(b + 1) * T], kv_ps[:, m % 4, :], ACT.Copy).then_inc(kv_copied, 1)

                def exps(u):
                    t, s, d, c, z = unit(u)
                    act.wait_ge(trend, i * 4 * UNITS + 4 * u + 4)
                    act.activation(decay[:, z, :], rise[:, z, :], ACT.Exp, bias=col[:, 6, t:t + 1]).then_inc(weighted, 1)
                    act.wait_ge(weighted, i * 3 * UNITS + 3 * u + 1)
                    act.activation(rise[:, z, :], rise[:, z, :], ACT.Exp, bias=col[:, 7, t:t + 1]).then_inc(weighted, 1)
                    act.activation(own[:, z, :], own[:, z, :], ACT.Exp).then_inc(weighted, 1)

                def invert(u):
                    z = unit(u)[4]
                    act.wait_ge(fraction, i * 4 * UNITS + 4 * u + 4)
                    act.activation(rise[:, z, :], rise[:, z, :], ACT.Ln).then_inc(inverse, 1)
                    act.wait_ge(inverse, i * 2 * UNITS + 2 * u + 1)
                    act.activation(rise[:, z, :], rise[:, z, :], ACT.Exp, bias=half_log[:, 0:1], scale=-1.0).then_inc(inverse, 1)

                for u in range(-1, UNITS + 1):
                    if u + 1 < UNITS:
                        t, s, d, c, z = unit(u + 1)
                        if s < STEPS // 2:
                            copy(t, c, 0)
                        if u == -1:
                            act.wait_ge(prepared, 5)
                        exps(u + 1)
                    if u >= 1:
                        invert(u - 1)
                    if u + 1 < UNITS:
                        if s < STEPS // 2:
                            copy(t, c, 1)
                        if s == STEPS // 2 - 1 and d == 1:
                            for b in range(STEPS):
                                act.wait_ge(gate_made, i * BLOCKS + t * STEPS + b + 1)
                                if t and b == 0:
                                    act.wait_ge(folded, i * folds(UNITS) + folds(t * 2 * STEPS))
                                elif b == 0:
                                    act.wait_ge(out_ready, i * BLOCKS)
                                act.activation(gate[:, b * T:(b + 1) * T], gate_ps[:, b % 2, :], ACT.Sigmoid)\
                                    .then_inc(gate_ready, 1)
                for b in range(STEPS):
                    if b == 0:
                        act.wait_ge(folded, (i + 1) * folds(UNITS))
                    else:
                        act.wait_ge(stats_made, i * STEPS + max(b - 1, 0))
                    act.activation(squares[:, b % 2, :, :], h[:, :, b * T:(b + 1) * T], ACT.Square).then_inc(squared, 1)
                    act.wait_ge(stats_made, i * STEPS + b + 1)
                    if b >= 1:
                        act.wait_ge(var_ready, i * 2 * STEPS + 2 * b)
                    act.activation(mean_sq[:, b % 2, :], stat_ps[:, 0, :], ACT.Square).then_inc(squared, 1)
                    act.wait_ge(var_ready, i * 2 * STEPS + 2 * b + 2)
                    act.activation(spread[:, b % 2, :], spread[:, b % 2, :], ACT.Ln).then_inc(rs_ready, 1)
                    act.wait_ge(rs_ready, i * 2 * STEPS + 2 * b + 1)
                    act.activation(spread[:, b % 2, :], spread[:, b % 2, :], ACT.Exp, scale=-0.5).then_inc(rs_ready, 1)

        @block.tensor
        def _(pe):
            pe.wait_ge(par_in, 16 * (LOADS + 1))
            pe.wait_ge(prepared, 3)
            for t in range(TILES):
                for j, s in enumerate(SOURCES[t]):
                    both = [q for q in SOURCES[s] if q in SOURCES[t]]
                    for q in both:
                        pe.matmul(kv_ps[:, t, j * P:(j + 1) * P], centre[:, BLOCK[q, s], :], wo[:, BLOCK[q, t], :],
                                  start=(q == both[0]), stop=(q == both[-1]))
            for t in range(TILES):
                for n, s in enumerate(SOURCES[t]):
                    ins = pe.matmul(stat_ps[:, 0, t:t + 1], wo_raw[:, BLOCK[s, t], :], col[:, LNB, s:s + 1],
                                    start=(n == 0), stop=(n == len(SOURCES[t]) - 1))
            ins.then_inc(prepared, 1)
            pe.wait_ge(prepared, 5)

            with pe.Fori(0, pairs) as i:
                pe.wait_ge(var_ready, i * 2 * STEPS)
                gn.mix_stats(pe, i, stat_ps[:, 0, 0:2 * TILES])

                def product(w, out, t, b, sem_):
                    for n, s in enumerate(SOURCES[t]):
                        ins = pe.matmul(out, w[:, BLOCK[s, t], :], xn[:, s, b * T:(b + 1) * T],
                                        start=(n == 0), stop=(n == len(SOURCES[t]) - 1))
                    ins.then_inc(sem_, 1)

                for t in range(TILES):
                    pe.wait_ge(normed, i * TILES + (2, 3, 3)[t])
                    for j, b in enumerate(ORDER):
                        for which in range(2):
                            m = (t * STEPS + j) * 2 + which
                            pe.wait_ge(kv_copied, i * 2 * BLOCKS + max(m - 3, 0))
                            if t == 0 and j == 0:
                                pe.wait_ge(scaled, i * BLOCKS)
                            product((wk, wv)[which], kv_ps[:, m % 4, :], t, b, kv_made)
                    for b in range(STEPS):
                        pe.wait_ge(gate_ready, i * BLOCKS + max(t * STEPS + b - 1, 0))
                        product(wr, gate_ps[:, b % 2, :], t, b, gate_made)
                for b in range(STEPS):
                    chunk = slice(b * T, (b + 1) * T)
                    pe.wait_ge(squared, i * 2 * STEPS + 2 * b + 1)
                    if b:
                        pe.wait_ge(var_ready, i * 2 * STEPS + 2 * b)
                    for which in range(2):
                        for s in range(TILES):
                            ins = pe.matmul(stat_ps[:, which, :], ones[:, s, :],
                                            (h[:, s, chunk], squares[:, b % 2, s, :])[which],
                                            start=(s == 0), stop=(s == TILES - 1))
                    ins.then_inc(stats_made, 1)
                    if b == 0:
                        pe.wait_ge(kv_copied, (i + 1) * 2 * BLOCKS)
                    for t in range(TILES):
                        m = b * TILES + t
                        pe.wait_ge(scaled, i * BLOCKS + max(m - 3, 0))
                        for n, s in enumerate(SOURCES[t]):
                            ins = pe.matmul(kv_ps[:, m % 4, :], wo[:, BLOCK[s, t], :], h[:, s, chunk],
                                            start=(n == 0), stop=(n == len(SOURCES[t]) - 1))
                        ins.then_inc(out_made, 1)

        @block.vector
        def _(dve):
            dve.memset(gn.half[:, :], -0.5)
            dve.memset(half_log[:, :], -math.log(2.0)).then_inc(prepared, 1)
            dve.wait_ge(par_in, 16 * (LOADS + 1))
            for t in range(TILES):
                for s in SOURCES[t]:
                    ins = dve.tensor_scalar(wo[:, BLOCK[s, t], :], wo_raw[:, BLOCK[s, t], :], col[:, LNG, s:s + 1], None, ALU.mult)
            ins.then_inc(prepared, 1)
            dve.wait_ge(prepared, 4)
            for t in range(TILES):
                n = len(SOURCES[t])
                for j, s in enumerate(SOURCES[t]):
                    dve.tensor_copy(wo[:, BLOCK[s, t], :], kv_ps[:, t, j * P:(j + 1) * P])
            dve.tensor_copy(col[:, OB, :], stat_ps[:, 0, 0:TILES])
            dve.tensor_scalar(col[:, 6, :], col[:, 5, :], -1.0, None, ALU.mult)
            dve.tensor_scalar(col[:, 7, :], col[:, U, :], -1.0, None, ALU.mult).then_inc(prepared, 1)

            with dve.Fori(0, pairs) as i:
                gn.statistics(dve, i, xn, lambda t: dve.wait_ge(x_in_s[t], i * 16 + 16))
                gn.scales(dve, i, stat_ps[:, 0, 0:2 * TILES])
                for t in range(TILES):
                    dve.tensor_scalar(xn[:, t, :], xn[:, t, :], gn.rstd[:, t:t + 1], gn.shift[:, t:t + 1],
                                      ALU.mult, ALU.add).then_inc(normed, 1)

                def trends(u):
                    t, s, d, c, z = unit(u)
                    new, old, at = ((slice(1, T + 1), slice(0, T), 0), (slice(0, T), slice(1, T + 1), T))[d]
                    flip = (lambda a: a) if d == 0 else (lambda a: a[:, ::-1])
                    n = i * 4 * UNITS + 4 * u
                    if s == 0:
                        dve.memset(top[:, z, at:at + 1], NEG_INF).then_inc(trend, 1)
                    else:
                        y = unit(u - 2)[4]
                        dve.tensor_copy(top[:, z, at:at + 1], top[:, y, (T, 0)[d]:(T, 0)[d] + 1]).then_inc(trend, 1)
                    dve.wait_ge(trend, n + 1)
                    if s < STEPS // 2:
                        dve.wait_ge(kv_copied, i * 2 * BLOCKS + copies_before(t, c, 0) + 1)
                    chunk = k[:, c * T:(c + 1) * T]
                    dve.tensor_tensor_scan(flip(top[:, z, new]), col[:, 6, t:t + 1].to_broadcast([P, T]), flip(chunk),
                                           top[:, z, at:at + 1], ALU.add, ALU.max).then_inc(trend, 1)
                    dve.wait_ge(trend, n + 2)
                    dve.tensor_tensor(rise[:, z, :], top[:, z, old], top[:, z, new], ALU.subtract).then_inc(trend, 1)
                    dve.tensor_tensor(own[:, z, :], chunk, top[:, z, new], ALU.subtract).then_inc(trend, 1)

                def accumulate(u):
                    t, s, d, c, z = unit(u)
                    new, at = ((slice(1, T + 1), 0), (slice(0, T), T))[d]
                    flip = (lambda a: a) if d == 0 else (lambda a: a[:, ::-1])
                    n = i * 4 * UNITS + 4 * u
                    if s == 0:
                        dve.memset(qp[:, z, :, at:at + 1], 0.0).then_inc(sums, 1)
                    else:
                        y, e = unit(u - 2)[4], (T, 0)[d]
                        dve.tensor_copy(qp[:, z, :, at:at + 1], qp[:, y, :, e:e + 1]).then_inc(sums, 1)
                    dve.wait_ge(weighted, i * 3 * UNITS + 3 * u + 3)
                    if s < STEPS // 2:
                        dve.wait_ge(kv_copied, i * 2 * BLOCKS + copies_before(t, c, 1) + 1)
                    dve.tensor_tensor(own_v[:, z, :], own[:, z, :], v[:, c * T:(c + 1) * T], ALU.mult).then_inc(sums, 1)
                    dve.wait_ge(sums, n + 1)
                    dve.tensor_tensor_scan(flip(qp[:, z, 0, new]), flip(decay[:, z, :]), flip(own[:, z, :]),
                                           qp[:, z, 0, at:at + 1], ALU.mult, ALU.add).then_inc(sums, 1)
                    dve.wait_ge(sums, n + 2)
                    dve.tensor_tensor_scan(flip(qp[:, z, 1, new]), flip(decay[:, z, :]), flip(own_v[:, z, :]),
                                           qp[:, z, 1, at:at + 1], ALU.mult, ALU.add).then_inc(sums, 1)

                def fold(u):
                    t, s, d, c, z = unit(u)
                    chunk = h[:, t, c * T:(c + 1) * T]
                    n = i * folds(UNITS) + folds(u)
                    dve.wait_ge(inverse, i * 2 * UNITS + 2 * u + 2)
                    if s < STEPS // 2:
                        dve.tensor_tensor(chunk, decay[:, z, :], rise[:, z, :], ALU.mult).then_inc(folded, 1)
                        return
                    dve.tensor_tensor(decay[:, z, :], decay[:, z, :], rise[:, z, :], ALU.mult).then_inc(folded, 1)
                    dve.wait_ge(folded, n + 1)
                    dve.tensor_tensor(chunk, chunk, decay[:, z, :], ALU.add).then_inc(folded, 1)
                    dve.wait_ge(folded, n + 2)
                    dve.wait_ge(gate_ready, i * BLOCKS + t * STEPS + STEPS)
                    dve.tensor_tensor(chunk, chunk, gate[:, c * T:(c + 1) * T], ALU.mult).then_inc(folded, 1)

                for u in range(-1, UNITS + 1):
                    if u + 1 < UNITS:
                        trends(u + 1)
                    if 0 <= u < UNITS:
                        accumulate(u)
                    if u >= 1:
                        fold(u - 1)

                for b in range(STEPS):
                    chunk = slice(b * T, (b + 1) * T)
                    dve.wait_ge(squared, i * 2 * STEPS + 2 * b + 2)
                    if b >= 2:
                        dve.wait_ge(scaled, i * BLOCKS + 3 * (b - 1))
                    dve.scalar_tensor_tensor(out=spread[:, b % 2, :], in0=mean_sq[:, b % 2, :], scalar=-1.0,
                                             in1=stat_ps[:, 1, :], op0=ALU.mult, op1=ALU.add).then_inc(var_ready, 1)
                    dve.wait_ge(var_ready, i * 2 * STEPS + 2 * b + 1)
                    dve.tensor_scalar(spread[:, b % 2, :], spread[:, b % 2, :], 0.0, LN_EPS, ALU.max, ALU.add).then_inc(var_ready, 1)
                    dve.wait_ge(rs_ready, i * 2 * STEPS + 2 * b + 2)
                    if b >= 2:
                        dve.wait_ge(stored[b % 2], i * 16 * STEPS // 2 + 16 * (b // 2))
                    dve.wait_ge(again_in[b % 2], i * 16 * STEPS // 2 + 16 * (b // 2 + 1))
                    for t in range(TILES):
                        m = b * TILES + t
                        dve.wait_ge(out_made, i * BLOCKS + m + 1)
                        for half in range(2):
                            image = (0, 0, 1) [t] if half == 0 else (0, 1, 1)[t]
                            mine = slice(64 * half, 64 * half + 64)
                            ins = dve.tensor_tensor(result[mine, b % 2, t, :], kv_ps[mine, m % 4, :],
                                                    spread[64 * image:64 * image + 64, b % 2, :], ALU.mult)
                        ins.then_inc(scaled, 1)
                        dve.wait_ge(scaled, i * BLOCKS + m + 1)
                        dve.scalar_tensor_tensor(out=result[:, b % 2, t, :], in0=result[:, b % 2, t, :], scalar=col[:, OB, t:t + 1],
                                                 in1=x_again[:, b % 2, t, :], op0=ALU.add, op1=ALU.add).then_inc(out_ready, 1)



def _blocks(big):
    return np.stack([big[P * s:P * s + P, P * t:P * t + P] for (s, t) in BLOCK])


def _twice(w):
    big = np.zeros((2 * w.shape[0], 2 * w.shape[1]), np.float32)
    big[:w.shape[0], :w.shape[1]] = w
    big[w.shape[0]:, w.shape[1]:] = w
    return big


def _columns(v):
    return np.ascontiguousarray(np.concatenate([v, v]).reshape(TILES, P).T)


def wkv_params(p, inputs):
    r = np.arange(2 * CH)
    same = (r[:, None] // CH == r[None, :] // CH)
    arrays = {}
    for n, key in (("wk", "Wk"), ("wv", "Wv"), ("wr", "Wr"), ("wo", "Wo")):
        arrays[n] = _blocks(_twice(inputs[p + key].T))
    arrays["centre"] = _blocks((np.eye(2 * CH) - same / CH).astype(np.float32))
    for n, key in (("ln_g", "ln_g"), ("ln_b", "ln_b"), ("w_decay", "w_decay"), ("u", "u")):
        arrays[n] = _columns(inputs[p + key])
    return arrays


def shared_constants():
    r = np.arange(2 * CH)
    group = CH // 32
    mix = (r[:, None] // group == r[None, :] // group) / group
    image = (r.reshape(TILES, P, 1) // CH == np.arange(P)[None, None, :] // 64) / CH
    return {"gn_mix": _blocks(mix.astype(np.float32)), "image_mean": image.astype(np.float32)}


def fractional_matrix(a):
    n = SIDE
    eye = np.eye(n, dtype=np.complex128)
    if a < 0.5:
        shift = (np.arange(n) + n // 2) % n
        eye = np.fft.ifft(eye[:, shift], axis=-1) * math.sqrt(n)
        eye = eye[:, np.argsort(shift)]
        a = a + 1.0

    def full_convolution(f, kern):
        length = f.shape[-1] + kern.shape[0] - 1
        return np.fft.ifft(np.fft.fft(f, n=length, axis=-1) * np.fft.fft(kern, n=length), axis=-1)

    alpha = a * math.pi / 2
    tana2, sina = math.tan(alpha / 2), math.sin(alpha)
    y = np.zeros((n, 2 * n - 1), np.complex128)
    y[:, ::2] = eye
    fi = full_convolution(y, np.sinc(np.arange(-(2 * n - 3), 2 * n - 2) / 2.0))[:, 2 * n - 3:4 * n - 4]
    pad = np.zeros((n, n - 1))
    t = np.arange(-2 * n + 2, 2 * n - 1).astype(np.float64)
    chirp = np.exp(-1j * math.pi / n * tana2 / 4 * t ** 2)
    c = math.pi / n / sina / 4
    m = np.arange(-(4 * n - 4), 4 * n - 3).astype(np.float64)
    ret = full_convolution(chirp * np.concatenate([pad, fi, pad], axis=-1), np.exp(1j * c * m ** 2))
    ret = ret[:, 4 * n - 4:8 * n - 7] * math.sqrt(c / math.pi) * chirp
    return np.exp(-1j * (1 - a) * math.pi / 4) * ret[:, n - 1:3 * n - 2:2]


def fourier_constants():
    n = SIDE
    k = np.arange(n)
    turn = np.outer(k, k) % n
    cos, sin = np.cos(2 * math.pi * turn / n), np.sin(2 * math.pi * turn / n)
    cos[turn % 32 == 16] = 0.0
    sin[turn % 32 == 0] = 0.0
    weight = np.where((k == 0) | (k == n // 2), 1.0, np.where(k < n // 2, 2.0, 0.0)) / (n * n)
    trans = np.zeros((5, P, 2, 256), np.float32)
    for f, m in enumerate((fractional_matrix(0.5), cos - 1j * sin, fractional_matrix(-0.5),
                           (cos + 1j * sin) * weight[:, None], cos + 1j * sin)):
        for r, parts in enumerate(((m.real, m.imag), (-m.imag, m.real))):
            for c, part in enumerate(parts):
                for image in range(2):
                    q = slice(n * image, n * image + n)
                    trans[f, q, r, P * c + n * image:P * c + n * image + n] = part
    inner = int(n * math.cos(0.25 * math.pi))
    first = (n - inner) // 2
    inside = ((k >= first) & (k < first + inner)).astype(np.float32)
    mask = np.outer(np.concatenate([inside, inside]), inside)
    return {"trans": trans, "mask": mask.astype(np.float32), "ident": np.eye(P, dtype=np.float32)}


def fourier_params(p, inputs):
    g, hb = 16, 8

    def by_rows(w):
        m = np.zeros((g, hb, g, hb), np.float32)
        for r in range(hb):
            m[:, r, :, r] = w.T
        return m.reshape(P, P)

    spatial = np.zeros((3, 3, g, hb, g, hb), np.float32)
    w = inputs[p + "mag_s_w"]
    for dw in range(3):
        for dh in range(3):
            for r in range(hb):
                q, s = divmod(r + dh - 1, hb)
                spatial[dw, q + 1, :, s, :, r] = w[:, :, dh, dw].T
    conv2 = inputs[p + "conv2_w"]
    rest = np.zeros((64, CH), np.float32)
    rest[g:3 * g] = conv2[:, g:].T
    first = np.zeros((g, 64), np.float32)
    first[:, :g] = inputs[p + "conv_0_w"]
    row = lambda key: inputs[p + key]
    rows = np.stack([row("mag_s_b"), row("mag_f_b"), row("mag_b"), row("conv_1_b"), row("pha_b"), row("conv_1_b")])
    c1 = inputs[p + "conv1_w"].T
    return {
        "mixers": np.stack([by_rows(row(k)) for k in ("mag_f_w", "mag_w", "pha_w", "conv_1_w")]),
        "spatial": spatial.reshape(9, P, P),
        "conv2_rest": _twice(rest),
        "conv0": _twice(first),
        "conv2_0": _twice(conv2[:, :g].T),
        "bias0": np.concatenate([row("conv_0_b")] * 2).reshape(2 * g, 1),
        "rows": np.ascontiguousarray(np.broadcast_to(rows, (P, 6, g))),
        "conv1": np.concatenate([c1, c1]).reshape(TILES, P, 3 * g),
    }


def conv_params(p, inputs):
    dw = inputs[p + "dw_w"].reshape(CH, 9)
    return {
        "pointwise": _blocks(_twice(inputs[p + "pw_w"].T)),
        "taps": np.ascontiguousarray(np.concatenate([dw, dw]).reshape(TILES, P, 9).transpose(1, 0, 2)),
        "affine": np.stack([_columns(inputs[p + "gamma"]), _columns(inputs[p + "beta"])], axis=1),
    }


def same_channel(pairs=PAIRS):
    r = np.arange(2 * CH)
    big = ((r[:, None] % CH == r[None, :] % CH) / (2.0 * pairs)).astype(np.float32)
    return np.stack([big[P * s:P * s + P, P * t:P * t + P] for s in range(TILES) for t in range(TILES)])


def build(nc, x, out, par):
    def scratch(name, shape):
        return nc.dram_tensor(name, shape, F32, kind="Internal").ap()

    z, bn_cols = scratch("z", [ROWS, TOKENS]), scratch("bn_cols", [P, 2, TILES])
    after_1, after_2 = scratch("after_1", [ROWS, TOKENS]), scratch("after_2", [ROWS, TOKENS])
    convolution_layer(nc, x, z, bn_cols, par["L0"])
    fourier_layer(nc, x, after_1, dict(par["L1"], bn_cols=bn_cols), "f1_", (z,))
    wkv_layer(nc, after_1, after_2, par["L2"])
    fourier_layer(nc, after_2, out, par["L3"], "f3_")


def kernel(**inputs):
    import concourse.bacc as _bacc
    from concourse.bass_utils import run_bass_kernel_spmd as _run

    nc = _bacc.Bacc("TRN2", target_bir_lowering=False, num_devices=1)
    inputs = {k: np.asarray(v) for k, v in inputs.items()}
    shared, waves = shared_constants(), fourier_constants()
    layers = {
        "L0": dict(conv_params("L0_conv_", inputs), same=same_channel(), ident=waves["ident"], gn_mix=shared["gn_mix"]),
        "L1": dict(fourier_params("L1_conv_", inputs), gn_mix=shared["gn_mix"], **waves),
        "L2": dict(wkv_params("L2_conv_", inputs), **shared),
        "L3": dict(fourier_params("L3_conv_", inputs), gn_mix=shared["gn_mix"], **waves),
    }
    arrays, par = {}, {}
    for layer, named in layers.items():
        par[layer] = {}
        for name, a in named.items():
            arrays[f"{layer}_{name}"] = a = np.ascontiguousarray(a)
            par[layer][name] = nc.dram_tensor(f"{layer}_{name}", a.shape, F32, kind="ExternalInput").ap()
    arrays["x"] = np.ascontiguousarray(inputs["x"]).reshape(ROWS, TOKENS)
    x = nc.dram_tensor("x", (ROWS, TOKENS), F32, kind="ExternalInput").ap()
    out = nc.dram_tensor("out", (ROWS, TOKENS), F32, kind="ExternalOutput").ap()
    build(nc, x, out, par)
    r = _run(nc, [arrays], core_ids=[0])
    return r.results[0]["out"].reshape(BATCH, CH, SIDE, SIDE)
```

```python
import math
from contextlib import ExitStack

import numpy as np

import concourse.bass as bass
from concourse import mybir

P = 128
BATCH, CH, SIDE = 32, 192, 64
TOKENS = SIDE * SIDE
ROWS = BATCH * CH
TILES = 3
PAIRS = ROWS // (P * TILES)
SOURCES = ((0, 1), (0, 1, 2), (1, 2))
BLOCK = {(s, t): n for n, (s, t) in enumerate((s, t) for t in range(TILES) for s in SOURCES[t])}
GN_EPS, LN_EPS, BN_EPS = 1e-5, 1e-5, 1e-5
NEG_INF = -1e38

F32 = mybir.dt.float32
ALU = mybir.AluOpType
ACT = mybir.ActivationFunctionType


def makers(nc, ctx, prefix):
    return (lambda name, shape: ctx.enter_context(nc.sbuf_tensor(prefix + name, shape, F32)),
            lambda name, shape: ctx.enter_context(nc.psum_tensor(prefix + name, shape, F32)),
            lambda name: ctx.enter_context(nc.semaphore(prefix + name)))


class GroupNorm:

    DVE_STEPS = 12

    def __init__(self, nc, sb, sem, parts):
        self.mix = sb("gn_mix", [P, 7, P])
        self.raw = sb("gn_raw", [P, TILES, 8, 6])
        self.mv = sb("gn_mv", [P, TILES, 2])
        self.group = sb("gn_group", [P, TILES, 2])
        self.mean = sb("gn_mean", [P, TILES])
        self.sq = sb("gn_sq", [P, TILES])
        self.var = sb("gn_var", [P, TILES])
        self.rstd = sb("gn_rstd", [P, TILES])
        self.shift = sb("gn_shift", [P, TILES])
        self.half = sb("gn_half", [P, TILES])
        self.stat, self.mixed, self.powered = sem("gn_stat"), sem("gn_mixed"), sem("gn_powered")

    def statistics(self, dve, i, x, loaded, offset=None):
        n = i * self.DVE_STEPS
        for t in range(TILES):
            loaded(t)
            for j in range(8):
                ins = dve.bn_stats(self.raw[:, t, j, :], x[:, t, j * 512:(j + 1) * 512])
        ins.then_inc(self.stat, 1)
        dve.wait_ge(self.stat, n + 1)
        dve.memset(self.sq[:, :], 0.0)
        for t in range(TILES):
            ins = dve.bn_aggr(self.mv[:, t, :], self.raw[:, t, :, :])
        ins.then_inc(self.stat, 1)
        dve.wait_ge(self.stat, n + 2)
        if offset is None:
            dve.tensor_copy(self.mean[:, :], self.mv[:, :, 0]).then_inc(self.stat, 1)
        else:
            dve.tensor_tensor(self.mean[:, :], self.mv[:, :, 0], offset, ALU.add).then_inc(self.stat, 1)
        dve.wait_ge(self.stat, n + 3)
        dve.tensor_copy(self.mv[:, :, 0], self.mean[:, :]).then_inc(self.stat, 1)
        dve.tensor_tensor(self.sq[:, :], self.mean[:, :], self.mean[:, :], ALU.mult).then_inc(self.stat, 1)
        dve.wait_ge(self.stat, n + 5)
        dve.tensor_tensor(self.mv[:, :, 1], self.mv[:, :, 1], self.sq[:, :], ALU.add).then_inc(self.stat, 1)

    def mix_stats(self, pe, i, bank):
        pe.wait_ge(self.stat, i * self.DVE_STEPS + 6)
        for t in range(TILES):
            for n, s in enumerate(SOURCES[t]):
                ins = pe.matmul(bank[:, 2 * t:2 * t + 2], self.mix[:, BLOCK[s, t], :], self.mv[:, s, :],
                                start=(n == 0), stop=(n == len(SOURCES[t]) - 1))
        ins.then_inc(self.mixed, 1)

    def power(self, pool, i):
        pool.wait_ge(self.stat, i * self.DVE_STEPS + 10)
        pool.tensor_tensor(self.rstd[:, :], self.var[:, :], self.half[:, :], ALU.pow).then_inc(self.powered, 1)

    def scales(self, dve, i, bank, offset=None):
        n = i * self.DVE_STEPS
        dve.wait_ge(self.mixed, i + 1)
        dve.tensor_copy(self.group[:, :, :], bank.rearrange("p (t c) -> p t c", c=2)).then_inc(self.stat, 1)
        dve.wait_ge(self.stat, n + 7)
        dve.tensor_tensor(self.sq[:, :], self.group[:, :, 0], self.group[:, :, 0], ALU.mult).then_inc(self.stat, 1)
        dve.wait_ge(self.stat, n + 8)
        dve.tensor_tensor(self.var[:, :], self.group[:, :, 1], self.sq[:, :], ALU.subtract).then_inc(self.stat, 1)
        dve.wait_ge(self.stat, n + 9)
        dve.tensor_scalar(self.var[:, :], self.var[:, :], 0.0, GN_EPS, ALU.max, ALU.add).then_inc(self.stat, 1)
        if offset is None:
            dve.tensor_scalar(self.sq[:, :], self.group[:, :, 0], -1.0, None, ALU.mult).then_inc(self.stat, 1)
        else:
            dve.tensor_tensor(self.sq[:, :], offset, self.group[:, :, 0], ALU.subtract).then_inc(self.stat, 1)
        dve.wait_ge(self.stat, n + 11)
        dve.wait_ge(self.powered, i + 1)
        dve.tensor_tensor(self.shift[:, :], self.sq[:, :], self.rstd[:, :], ALU.mult).then_inc(self.stat, 1)
        dve.wait_ge(self.stat, n + 12)

    def ready(self, eng, i):
        eng.wait_ge(self.stat, (i + 1) * self.DVE_STEPS)


def convolution_layer(nc, x_in, z_out, bn_out, par, pairs=PAIRS):
    PAD = 2
    SPAN = SIDE + 2 * PAD
    PE_TAPS = 3
    VEC_TAPS = 9 - PE_TAPS
    ROWS_A_JOB = 16
    JOBS = TILES * SIDE // ROWS_A_JOB
    WIDE = ROWS_A_JOB * SIDE
    Z_JOBS = 2 * JOBS
    STATS = 5

    with ExitStack() as ctx:
        sb, ps, sem = makers(nc, ctx, "conv_")
        x = sb("x", [P, TILES, TOKENS])
        padded = sb("padded", [P, TILES, SPAN, SPAN])
        y = sb("y", [P, TILES, TOKENS])
        z = sb("z", [P, 2, TILES, 512])
        gn = GroupNorm(nc, sb, sem, P)
        pointwise = sb("pointwise", [P, 7, P])
        taps = sb("taps", [P, TILES, 9])
        ident = sb("ident", [P, P])
        diagonal = sb("diagonal", [P, TILES, PE_TAPS, P])
        same = sb("same", [P, 9, P])
        affine = sb("affine", [P, 2, TILES])
        raw = sb("raw", [P, TILES, 8, 6])
        mv = sb("mv", [P, TILES, 2])
        total = sb("total", [P, TILES, 2])
        sq = sb("sq", [P, TILES])
        cols = sb("cols", [P, 2, TILES])

        tap_ps = ps("tap_ps", [P, 2, WIDE])
        z_ps = ps("z_ps", [P, 4, 512])

        par_in, prepared, last = sem("par_in"), sem("prepared"), sem("last")
        x_in_s = [sem(f"x_in{t}") for t in range(TILES)]
        relued, taps_made, tapped = sem("relued"), sem("taps_made"), sem("tapped")
        z_made, z_seen, z_copied, z_stat = sem("z_made"), sem("z_seen"), sem("z_copied"), sem("z_stat")
        stored = [sem("stored0"), sem("stored1")]
        bn_stored = sem("bn_stored")

        rows = x_in.rearrange("(q t p) n -> q p t n", p=P, t=TILES)
        z_rows = z_out.rearrange("(q t p) n -> q p t n", p=P, t=TILES)
        loads = [(pointwise, "pointwise", "b p n -> p b n"), (taps, "taps", None), (ident, "ident", None),
                 (same, "same", "b p n -> p b n"), (affine, "affine", None), (gn.mix, "gn_mix", "b p n -> p b n")]
        block = ctx.enter_context(nc.Block())

        def job(j):
            return divmod(j, TILES)

        def shifted(t, first, count, tap):
            dh, dw = divmod(tap, 3)
            return padded[:, t, first + 2 * dh:first + 2 * dh + count, 2 * dw:2 * dw + SIDE]

        @block.sync
        def _(sp):
            for to, name, view in loads:
                sp.dma_start(to.ap(), par[name] if view is None else par[name].rearrange(view)).then_inc(par_in, 16)

            def load_x(i):
                for t in range(TILES):
                    sp.dma_start(x[:, t, :], rows[i, :, t, :]).then_inc(x_in_s[t], 16)

            def store_z(i):
                for n in range(8):
                    sp.wait_ge(z_copied, i * Z_JOBS + 3 * (n + 1))
                    sp.dma_start(z_rows[i, :, :, 512 * n:512 * n + 512], z[:, n % 2, :, :]).then_inc(stored[n % 2], 16)

            load_x(0)
            if pairs > 1:
                with sp.Fori(0, pairs - 1) as i:
                    sp.wait_ge(relued, (i + 1) * TILES)
                    load_x(i + 1)
                    store_z(i)
            store_z(pairs - 1)
            for s in stored:
                sp.wait_ge(s, pairs * 4 * 16)
            sp.wait_ge(last, 8)
            sp.dma_start(bn_out, cols[:, :, :]).then_inc(bn_stored, 16)
            sp.wait_ge(bn_stored, 16)

        @block.gpsimd
        def _(pool):
            with pool.Fori(0, pairs) as i:
                gn.power(pool, i)
            pool.wait_ge(last, 4)
            pool.tensor_tensor(mv[:, :, 1], mv[:, :, 1], gn.half[:, :], ALU.pow).then_inc(last, 1)

        @block.scalar
        def _(act):
            with act.Fori(0, pairs) as i:
                gn.ready(act, i)
                for t in range(TILES):
                    act.wait_ge(tapped, i * JOBS * VEC_TAPS)
                    act.wait_ge(prepared, 1)
                    act.activation(padded[:, t, PAD:PAD + SIDE, PAD:PAD + SIDE], x[:, t, :].rearrange("p (h w) -> p h w", w=SIDE),
                                   ACT.Relu, bias=gn.shift[:, t:t + 1], scale=gn.rstd[:, t:t + 1]).then_inc(relued, 1)
                for m in range(Z_JOBS):
                    n, t = divmod(m, TILES)
                    act.wait_ge(z_made, i * Z_JOBS + m + 1)
                    act.wait_ge(z_seen, i * Z_JOBS + max(m - 5, 0))
                    if t == 0:
                        act.wait_ge(stored[n % 2], i * 4 * 16 + 16 * (n // 2))
                    act.activation(z[:, n % 2, t, :], z_ps[:, m % 4, :], ACT.Copy).then_inc(z_copied, 1)

        @block.tensor
        def _(pe):
            pe.wait_ge(par_in, 16 * len(loads))
            pe.wait_ge(prepared, 2)
            with pe.Fori(0, pairs) as i:
                def tap_job(j):
                    b, t = job(j)
                    if b == 0:
                        pe.wait_ge(relued, i * TILES + t + 1)
                    pe.wait_ge(tapped, i * JOBS * VEC_TAPS + max(j - 1, 0) * VEC_TAPS)
                    for half in range(2):
                        for tap in range(PE_TAPS):
                            ins = pe.matmul(tap_ps[:, j % 2, 512 * half:512 * half + 512], diagonal[:, t, tap, :],
                                            shifted(t, ROWS_A_JOB * b + 8 * half, 8, tap), start=(tap == 0), stop=(tap == PE_TAPS - 1))
                    ins.then_inc(taps_made, 1)

                def z_job(m):
                    n, t = divmod(m, TILES)
                    pe.wait_ge(tapped, i * JOBS * VEC_TAPS + (n // 2 + 1) * TILES * VEC_TAPS)
                    pe.wait_ge(z_copied, i * Z_JOBS + max(m - 3, 0))
                    for q, s in enumerate(SOURCES[t]):
                        ins = pe.matmul(z_ps[:, m % 4, :], pointwise[:, BLOCK[s, t], :], y[:, s, 512 * n:512 * n + 512],
                                        start=(q == 0), stop=(q == len(SOURCES[t]) - 1))
                    ins.then_inc(z_made, 1)

                pe.wait_ge(z_copied, i * Z_JOBS)
                gn.mix_stats(pe, i, z_ps[:, 0, 0:2 * TILES])
                gn.ready(pe, i)
                tap_job(0)
                for j in range(JOBS + TILES):
                    if j + 1 < JOBS:
                        tap_job(j + 1)
                    if j >= TILES:
                        z_job(2 * (j - TILES))
                        z_job(2 * (j - TILES) + 1)
            pe.wait_ge(last, 1)
            for t in range(TILES):
                for s in range(TILES):
                    ins = pe.matmul(z_ps[:, 0, 2 * t:2 * t + 2], same[:, 3 * s + t, :], total[:, s, :],
                                    start=(s == 0), stop=(s == TILES - 1))
            ins.then_inc(last, 1)

        @block.vector
        def _(dve):
            dve.memset(gn.half[:, :], -0.5)
            dve.memset(total[:, :, :], 0.0)
            dve.memset(padded[:, :, :, :], 0.0).then_inc(prepared, 1)
            dve.wait_ge(par_in, 16 * len(loads))
            for t in range(TILES):
                for tap in range(PE_TAPS):
                    ins = dve.tensor_scalar(diagonal[:, t, tap, :], ident[:, :], taps[:, t, tap:tap + 1], None, ALU.mult)
            ins.then_inc(prepared, 1)

            with dve.Fori(0, pairs) as i:
                gn.statistics(dve, i, x, lambda t: dve.wait_ge(x_in_s[t], (i + 1) * 16))
                gn.scales(dve, i, z_ps[:, 0, 0:2 * TILES])

                def see(m):
                    n, t = divmod(m, TILES)
                    dve.wait_ge(z_copied, i * Z_JOBS + m + 1)
                    dve.bn_stats(raw[:, t, n, :], z[:, n % 2, t, :]).then_inc(z_seen, 1)

                for j in range(JOBS + TILES):
                    if j < JOBS:
                        b, t = job(j)
                        first = ROWS_A_JOB * b
                        at = y[:, t, first * SIDE:(first + ROWS_A_JOB) * SIDE].rearrange("p (h w) -> p h w", w=SIDE)
                        dve.wait_ge(taps_made, i * JOBS + j + 1)
                        dve.wait_ge(z_made, i * Z_JOBS)
                        for n, tap in enumerate(range(PE_TAPS, 9)):
                            if n:
                                dve.wait_ge(tapped, (i * JOBS + j) * VEC_TAPS + n)
                            so_far = at if n else tap_ps[:, j % 2, :].rearrange("p (h w) -> p h w", w=SIDE)
                            dve.scalar_tensor_tensor(out=at, in0=shifted(t, first, ROWS_A_JOB, tap), scalar=taps[:, t, tap:tap + 1],
                                                     in1=so_far, op0=ALU.mult, op1=ALU.add).then_inc(tapped, 1)
                    if j >= TILES:
                        see(2 * (j - TILES))
                        see(2 * (j - TILES) + 1)
                dve.wait_ge(z_seen, (i + 1) * Z_JOBS)
                dve.memset(sq[:, :], 0.0)
                for t in range(TILES):
                    ins = dve.bn_aggr(mv[:, t, :], raw[:, t, :, :])
                ins.then_inc(z_stat, 1)
                dve.wait_ge(z_stat, i * STATS + 1)
                dve.tensor_tensor(sq[:, :], mv[:, :, 0], mv[:, :, 0], ALU.mult).then_inc(z_stat, 1)
                dve.wait_ge(z_stat, i * STATS + 2)
                dve.tensor_tensor(mv[:, :, 1], mv[:, :, 1], sq[:, :], ALU.add).then_inc(z_stat, 1)
                dve.wait_ge(z_stat, i * STATS + 3)
                dve.tensor_tensor(total[:, :, :], total[:, :, :], mv[:, :, :], ALU.add).then_inc(z_stat, 1)
                dve.wait_ge(z_stat, i * STATS + 4)
                dve.tensor_copy(sq[:, :], mv[:, :, 0]).then_inc(z_stat, 1)
            dve.wait_ge(z_stat, pairs * STATS)
            dve.tensor_copy(total[:, :, :], total[:, :, :]).then_inc(last, 1)
            dve.wait_ge(last, 2)
            dve.tensor_copy(mv[:, :, :], z_ps[:, 0, 0:2 * TILES].rearrange("p (t c) -> p t c", c=2)).then_inc(z_stat, 1)
            dve.wait_ge(z_stat, pairs * STATS + 1)
            dve.tensor_tensor(sq[:, :], mv[:, :, 0], mv[:, :, 0], ALU.mult).then_inc(last, 1)
            dve.wait_ge(last, 3)
            dve.tensor_tensor(mv[:, :, 1], mv[:, :, 1], sq[:, :], ALU.subtract).then_inc(z_stat, 1)
            dve.wait_ge(z_stat, pairs * STATS + 2)
            dve.tensor_scalar(mv[:, :, 1], mv[:, :, 1], 0.0, BN_EPS, ALU.max, ALU.add).then_inc(last, 1)
            dve.wait_ge(last, 5)
            dve.tensor_tensor(cols[:, 0, :], mv[:, :, 1], affine[:, 0, :], ALU.mult).then_inc(last, 1)
            dve.wait_ge(last, 6)
            dve.tensor_tensor(sq[:, :], mv[:, :, 0], cols[:, 0, :], ALU.mult).then_inc(last, 1)
            dve.wait_ge(last, 7)
            dve.tensor_tensor(cols[:, 1, :], affine[:, 1, :], sq[:, :], ALU.subtract).then_inc(last, 1)


def fourier_layer(nc, x_in, x_out, par, tag, batch_norm=None, pairs=PAIRS):
    G = 16
    C1 = 3 * G
    MIX = 2 * G
    HB = 8
    NB = SIDE // HB
    ROUND = 12582912.0
    TWO_PI = 6.2831850
    FRONT_ACT = dict(conv1=8, forward=8)
    FRONT_VEC = dict(forward=8)
    BACK_ACT = dict(turned=10, turned_s=2, phase=4, inverse=8, final=8)
    BACK_VEC = dict(spatial=2, fourier=2, magnitude=4, inverse=6, final=24)

    def place(jobs, name):
        return sum(list(jobs.values())[:list(jobs).index(name)])

    LUTS, CALCS = 11, 19

    def blocked(plane):
        return plane.rearrange("p c h -> p (c h)").rearrange("p (b c r) -> p c b r", b=NB, c=G)

    def by_block(plane):
        return plane.rearrange("p c (b r) -> p c b r", b=NB)

    def block_of(plane, b):
        return plane.rearrange("p c h -> p (c h)")[:, b * P:(b + 1) * P]

    with ExitStack() as ctx:
        sb, ps, sem = makers(nc, ctx, tag)
        x = sb("x", [P, TILES, TOKENS])
        z = sb("z", [P, TOKENS]) if batch_norm else None
        planes = sb("planes", [P, 3 * 4096])
        flat = planes[:, :]
        field = flat[:, 0:4096].rearrange("p (r c h) -> p r c h", r=2, c=MIX)
        w0, w1 = (flat[:, 4096 + 2048 * j:6144 + 2048 * j].rearrange("p (c h) -> p c h", c=MIX) for j in range(2))
        cat_t = flat[:, 8192:12288]
        mixed_in = cat_t.rearrange("p (z b n) -> p z b n", z=4, b=NB)
        first = sb("first", [P, C1, SIDE])
        cat = sb("cat", [P, 64, SIDE])
        again = sb("again", [P, 2, TILES, 512])
        half_way = sb("half_way", [P, MIX // 2, 256])
        halves = half_way[:, :, :].rearrange("p a n -> p (a n)")
        w2, w3 = (halves[:, 2048 * j:2048 * j + 2048].rearrange("p (c h) -> p c h", c=MIX) for j in range(2))
        spatial_in = sb("spatial_in", [P, NB, P + 2])

        gn = GroupNorm(nc, sb, sem, P)
        trans = sb("trans", [P, 5, 2, 256])
        FRFT, FFT, IFRFT, IFFT_W, IFFT_H = range(5)
        conv1 = sb("conv1", [P, TILES, C1])
        mixers = sb("mixers", [P, 4, P])
        MAG_F, MAG, PHA, CONV_1 = range(4)
        spatial = sb("spatial", [P, 9, P])
        ident = sb("ident", [P, P])
        conv2 = sb("conv2", [P, 2 * CH])
        conv0 = sb("conv0", [2 * G, P])
        conv2_0 = sb("conv2_0", [2 * G, 2 * CH])
        bias0 = sb("bias0", [2 * G, 1])
        rows_in = sb("rows_in", [P, 6, G])
        mask = sb("mask", [P, SIDE])
        bias_map = sb("bias_map", [P, G, SIDE])
        turn_bias = sb("turn_bias", [P, MIX])
        out_bias = sb("out_bias", [P, TILES])
        quarter = sb("quarter", [P, 1])
        zero = sb("zero", [P, 1])
        bn_cols = sb("bn_cols", [P, 2, TILES])

        front_act_ps = ps("front_act_ps", [P, 2, 512])
        front_vec_ps = ps("front_vec_ps", [P, 2, 512])
        back_act_ps = ps("back_act_ps", [P, 2, 512])
        back_vec_ps = ps("back_vec_ps", [P, 2, 512])

        par_in, prepared, bias_steps = sem("par_in"), sem("prepared"), sem("bias_steps")
        x_in_s = [sem(f"x_in{t}") for t in range(TILES)]
        z_in, based, normed, first_kept = sem("z_in"), sem("based"), sem("normed"), sem("first_kept")
        base_stored = [sem(f"base_stored{t}") for t in range(TILES)]
        front_act_made, front_act_read = sem("front_act_made"), sem("front_act_read")
        front_vec_made, front_vec_read = sem("front_vec_made"), sem("front_vec_read")
        back_act_made, back_act_read = sem("back_act_made"), sem("back_act_read")
        back_vec_made, back_vec_read = sem("back_vec_made"), sem("back_vec_read")
        lut, calc = sem("lut"), sem("calc")
        again_in = [sem("again_in0"), sem("again_in1")]
        stored = [sem("stored0"), sem("stored1")]

        src = x_in.rearrange("(q t p) n -> q p t n", p=P, t=TILES)
        dst = x_out.rearrange("(q t p) n -> q p t n", p=P, t=TILES)
        loads = [
            (trans, "trans", "f p r n -> p f r n"), (mixers, "mixers", "b p n -> p b n"),
            (spatial, "spatial", "b p n -> p b n"), (ident, "ident", None), (conv2, "conv2_rest", None),
            (conv1, "conv1", "t p n -> p t n"), (conv0, "conv0", None), (conv2_0, "conv2_0", None),
            (bias0, "bias0", None), (rows_in, "rows", None), (mask, "mask", None), (gn.mix, "gn_mix", "b p n -> p b n")]
        if batch_norm:
            z_rows = batch_norm[0].rearrange("(q t p) n -> q p t n", p=P, t=TILES)
            loads.append((bn_cols, "bn_cols", None))
        N_LOADS = len(loads)
        residual = dst if batch_norm else src
        MAG_S_B, MAG_F_B, MAG_B, CONV_1_B, PHA_B, CONV_1_B2 = range(6)

        block = ctx.enter_context(nc.Block())

        class Ring:

            def __init__(self, banks, jobs, made, read):
                self.banks, self.jobs, self.made, self.read = banks, jobs, made, read
                self.total = sum(jobs.values())

            def after(self, i, name, j=0):
                return i * self.total + place(self.jobs, name) + j

            def end(self, i, name):
                return self.after(i, name, self.jobs[name])

            def to_write(self, i, name, j):
                m = place(self.jobs, name) + j
                nc.tensor.wait_ge(self.read, i * self.total + max(m - 1, 0))
                return self.banks[:, m % 2, :]

            def to_read(self, eng, i, name, j):
                m = place(self.jobs, name) + j
                eng.wait_ge(self.made, i * self.total + m + 1)
                return self.banks[:, m % 2, :]

        front_act = Ring(front_act_ps, FRONT_ACT, front_act_made, front_act_read)
        front_vec = Ring(front_vec_ps, FRONT_VEC, front_vec_made, front_vec_read)
        back_act = Ring(back_act_ps, BACK_ACT, back_act_made, back_act_read)
        back_vec = Ring(back_vec_ps, BACK_VEC, back_vec_made, back_vec_read)

        @block.sync
        def _(sp):
            for to, name, view in loads:
                here = par[name] if view is None else par[name].rearrange(view)
                sp.dma_start(to.ap(), here).then_inc(par_in, 16)

            def load_x(i):
                for t in range(TILES):
                    sp.dma_start(x[:, t, :], src[i, :, t, :]).then_inc(x_in_s[t], 16)

            def bases(i):
                for t in range(TILES):
                    sp.wait_ge(based, i * TILES + t)
                    sp.dma_start(z[:, :], z_rows[i, :, t, :]).then_inc(z_in, 16)
                    if t:
                        sp.dma_start(dst[i, :, t - 1, :], x[:, t - 1, :]).then_inc(base_stored[t - 1], 16)
                sp.wait_ge(based, i * TILES + TILES)
                sp.dma_start(dst[i, :, TILES - 1, :], x[:, TILES - 1, :]).then_inc(base_stored[TILES - 1], 16)
                for s in base_stored:
                    sp.wait_ge(s, (i + 1) * 16)

            def load_again(i, j):
                sp.wait_ge(stored[j % 2], i * 4 * 16 + 16 * (j // 2))
                sp.dma_start(again[:, j % 2, :, :], residual[i, :, :, 512 * j:512 * j + 512]).then_inc(again_in[j % 2], 16)

            def final_traffic(i):
                load_again(i, 0)
                load_again(i, 1)
                for j in range(8):
                    sp.wait_ge(back_vec_read, back_vec.after(i, "final", 3 * (j + 1)))
                    sp.dma_start(dst[i, :, :, 512 * j:512 * j + 512], again[:, j % 2, :, :]).then_inc(stored[j % 2], 16)
                    if j + 2 < 8:
                        load_again(i, j + 2)

            load_x(0)
            if batch_norm:
                bases(0)
            if pairs > 1:
                with sp.Fori(0, pairs - 1) as i:
                    sp.wait_ge(front_act_made, front_act.end(i, "conv1"))
                    load_x(i + 1)
                    if batch_norm:
                        bases(i + 1)
                    final_traffic(i)
            final_traffic(pairs - 1)
            for s in stored:
                sp.wait_ge(s, pairs * 4 * 16)

        @block.gpsimd
        def _(pool):
            def front(i):
                gn.power(pool, i)

            def keep_first(i):
                pool.wait_ge(front_act_read, front_act.end(i, "conv1"))
                pool.wait_ge(back_act_made, back_act.after(i, "turned"))
                pool.tensor_tensor(cat[:, 0:G, :], first[:, 0:G, :], zero[:, :].unsqueeze(2).to_broadcast([P, G, SIDE]), ALU.add).then_inc(first_kept, 1)

            pool.wait_ge(prepared, 3)
            front(0)
            keep_first(0)
            if pairs > 1:
                with pool.Fori(0, pairs - 1) as i:
                    front(i + 1)
                    keep_first(i + 1)

        @block.scalar
        def _(act):
            def read(ring, i, name, j, out, view=lambda b: b, **kw):
                act.activation(out, view(ring.to_read(act, i, name, j)), ACT.Copy, **kw).then_inc(ring.read, 1)

            def step(*args, **kw):
                act.activation(*args, **kw).then_inc(lut, 1)

            def conv1_read(i, j):
                if j == 0:
                    act.wait_ge(front_act_made, front_act.after(i, "conv1"))
                    act.wait_ge(first_kept, i)
                read(front_act, i, "conv1", j, first[:, :, 8 * j:8 * j + 8].rearrange("p c h -> p h c"),
                     view=lambda b: b.rearrange("p (h c) -> p h c", c=64)[:, :, 0:C1])

            def to_half_way(ring, i, name, j):
                read(ring, i, name, j, half_way[:, 2 * j:2 * j + 2, :].rearrange("p a n -> p (a n)"))

            def forward_reads(i):
                for j in range(8):
                    to_half_way(front_act, i, "forward", j)

            def polar(i, between):
                act.wait_ge(front_vec_read, front_vec.end(i, "forward"))
                step(w0, field[:, 0], ACT.Square)
                step(w1, field[:, 1], ACT.Square)
                between(0)
                act.wait_ge(calc, i * CALCS + 1)
                step(w1, w0, ACT.Sqrt)
                between(1)
                act.wait_ge(calc, i * CALCS + 5)
                step(w2, w0, ACT.Arctan)
                between(2)
                act.wait_ge(calc, i * CALCS + 10)
                step(blocked(w2[:, 0:G]), by_block(w1[:, G:MIX]), ACT.Copy)

            def back(i, last):
                for plane in range(5):
                    for half in range(2):
                        if plane == 0:
                            read(back_act, i, "turned", half, spatial_in[:, 4 * half:4 * half + 4, 1:P + 1],
                                 view=lambda b: b.rearrange("p (b w) -> p b w", b=4))
                        else:
                            if plane == 1 and half == 0:
                                act.wait_ge(back_vec_made, back_vec.after(i, "spatial"))
                            read(back_act, i, "turned", 2 * plane + half, mixed_in[:, plane - 1, 4 * half:4 * half + 4, :]
                                 .rearrange("p b n -> p (b n)"))
                act.wait_ge(back_vec_read, back_vec.end(i, "fourier"))
                for half in range(2):
                    read(back_act, i, "turned_s", half, mixed_in[:, 0, 4 * half:4 * half + 4, :].rearrange("p b n -> p (b n)"))
                for j in range(4):
                    g, half = divmod(j, 2)
                    read(back_act, i, "phase", j, w3[:, G * g:G * g + G, 32 * half:32 * half + 32],
                         view=lambda b: b.rearrange("p (o h) -> p o h", h=32), scale=1.0 / math.pi)
                if not last:
                    conv1_read(i + 1, 0)
                    conv1_read(i + 1, 1)
                act.wait_ge(calc, i * CALCS + 16)
                step(w0, w3, ACT.Abs)
                step(w2, w3, ACT.Sin, scale=TWO_PI)
                act.wait_ge(lut, i * LUTS + 6)
                step(w0, w0, ACT.Sin, scale=-TWO_PI, bias=quarter[:, 0:1])
                if not last:
                    for j in range(2, 8):
                        conv1_read(i + 1, j)
                for j in range(8):
                    to_half_way(back_act, i, "inverse", j)
                act.wait_ge(back_vec_read, back_vec.after(i, "inverse", 4))
                step(w0[:, 0:G], field[:, 0, 0:G], ACT.Square)
                step(w1[:, 0:G], field[:, 1, 0:G], ACT.Square)
                act.wait_ge(calc, i * CALCS + 19)
                step(cat[:, G:2 * G, :], w0[:, 0:G], ACT.Sqrt)

                def final_reads(js):
                    for j in js:
                        read(back_act, i, "final", j, cat_t[:, 512 * j:512 * j + 512])

                if last:
                    final_reads(range(8))
                    return
                act.wait_ge(back_vec_made, back_vec.end(i, "inverse"))
                forward_reads(i + 1)
                polar(i + 1, lambda n: final_reads(((0, 1), (2, 3), (4, 5, 6, 7))[n]))

            act.wait_ge(prepared, 2)
            for j in range(8):
                conv1_read(0, j)
            forward_reads(0)
            polar(0, lambda n: None)
            if pairs > 1:
                with act.Fori(0, pairs - 1) as i:
                    back(i, False)
            back(pairs - 1, True)

        @block.tensor
        def _(pe):
            pe.wait_ge(par_in, 16 * N_LOADS)
            pe.matmul(back_vec_ps[:, 0, 0:2 * CH], conv0[:, :], conv2_0[:, :], start=True, stop=True)
            for t in range(TILES):
                ins = pe.matmul(back_vec_ps[:, 1, t:t + 1], conv2_0[:, t * P:t * P + P], bias0[:, :], start=True, stop=True)
            ins.then_inc(prepared, 1)
            pe.wait_ge(prepared, 3)

            def statistics(i):
                pe.wait_ge(front_vec_read, front_vec.after(i, "forward"))
                gn.mix_stats(pe, i, front_vec_ps[:, 0, 0:2 * TILES])

            def conv1_products(i):
                pe.wait_ge(normed, (i + 1) * TILES)
                for j in range(8):
                    bank = front_act.to_write(i, "conv1", j)
                    for r in range(8):
                        at = slice((8 * j + r) * SIDE, (8 * j + r + 1) * SIDE)
                        out = bank[:, 64 * r:64 * r + C1]
                        pe.matmul(out[0:64], x[:, 0, at], conv1[:, 0, :], start=True, stop=False)
                        pe.matmul(out[0:64], x[0:64, 1, at], conv1[0:64, 1, :], start=False, stop=True)
                        pe.matmul(out[64:128], x[:, 2, at], conv1[:, 2, :], start=True, stop=False)
                        ins = pe.matmul(out[64:128], x[64:128, 1, at], conv1[64:128, 1, :], start=False, stop=True)
                    ins.then_inc(front_act_made, 1)

            def forward(i):
                pe.wait_ge(front_act_read, front_act.end(i, "conv1"))
                for j in range(8):
                    bank = front_act.to_write(i, "forward", j)
                    for a in range(2):
                        c = G + 4 * j + 2 * a
                        ins = pe.matmul(bank[:, 256 * a:256 * a + 256], first[:, c:c + 2, :],
                                        trans[:, FRFT if j < 4 else FFT, 0, :], start=True, stop=True)
                    ins.then_inc(front_act_made, 1)
                for j in range(8):
                    pe.wait_ge(front_act_read, front_act.after(i, "forward", j + 1))
                    bank = front_vec.to_write(i, "forward", j)
                    for a in range(2):
                        for r in range(2):
                            ins = pe.matmul(bank[:, 256 * a:256 * a + 256], half_way[:, 2 * j + a, P * r:P * r + P],
                                            trans[:, FRFT if j < 4 else FFT, r, :], start=(r == 0), stop=(r == 1))
                    ins.then_inc(front_vec_made, 1)

            def turn(i, name, j, plane, half):
                bank = back_act.to_write(i, name, j)
                for b in range(4):
                    ins = pe.matmul(bank[:, P * b:P * b + P], block_of(plane, 4 * half + b), ident[:, :], start=True, stop=True)
                ins.then_inc(back_act_made, 1)

            def mix(bank, source, w, half, made):
                bank = bank.rearrange("p (o h) -> p o h", h=32)
                for b in range(4):
                    ins = pe.matmul(bank[:, :, HB * b:HB * b + HB], mixed_in[:, source, 4 * half + b, :], mixers[:, w, :],
                                    start=True, stop=True)
                ins.then_inc(made, 1)

            def mixing(i, last):
                pe.wait_ge(calc, i * CALCS + 12)
                pe.wait_ge(lut, i * LUTS + 5)
                for n, plane in enumerate((w0[:, 0:G], w0[:, G:MIX], w3[:, 0:G], w2[:, 0:G], w3[:, G:MIX])):
                    for half in range(2):
                        turn(i, "turned", 2 * n + half, plane, half)
                pe.wait_ge(back_act_read, back_act.after(i, "turned", 4))
                for half in range(2):
                    bank = back_vec.to_write(i, "spatial", half).rearrange("p (o h) -> p o h", h=32)
                    for b in range(4):
                        q = 4 * half + b
                        terms = [(dw, n, q + n - 1) for dw in range(3) for n in range(3) if 0 <= q + n - 1 < NB]
                        for dw, n, from_q in terms:
                            ins = pe.matmul(bank[:, :, HB * b:HB * b + HB], spatial_in[:, from_q, dw:dw + P],
                                            spatial[:, 3 * dw + n, :], start=((dw, n, from_q) == terms[0]),
                                            stop=((dw, n, from_q) == terms[-1]))
                    ins.then_inc(back_vec_made, 1)
                for half in range(2):
                    mix(back_vec.to_write(i, "fourier", half), 0, MAG_F, half, back_vec_made)
                if not last:
                    statistics(i + 1)
                pe.wait_ge(calc, i * CALCS + 13)
                for half in range(2):
                    turn(i, "turned_s", half, w2[:, G:MIX], half)
                for j in range(4):
                    mix(back_act.to_write(i, "phase", j), (1, 3)[j // 2], (PHA, CONV_1)[j // 2], j % 2, back_act_made)
                pe.wait_ge(back_act_read, back_act.end(i, "turned_s"))
                for j in range(4):
                    mix(back_vec.to_write(i, "magnitude", j), (0, 2)[j // 2], (MAG, CONV_1)[j // 2], j % 2, back_vec_made)

            def inverse(i):
                pe.wait_ge(calc, i * CALCS + 18)
                for j in range(8):
                    bank = back_act.to_write(i, "inverse", j)
                    for a in range(2):
                        c = 4 * j + 2 * a
                        for r in range(2):
                            ins = pe.matmul(bank[:, 256 * a:256 * a + 256], field[:, r, c:c + 2, :],
                                            trans[:, IFRFT if j < 4 else IFFT_W, r, :], start=(r == 0), stop=(r == 1))
                    ins.then_inc(back_act_made, 1)
                for j in range(6):
                    n = 2 * (j + 1) if j < 4 else 8 + 4 * (j - 3)
                    pe.wait_ge(back_act_read, back_act.after(i, "inverse", n // 2))
                    bank = back_vec.to_write(i, "inverse", j)
                    per = 2 if j < 4 else 4
                    width = 512 // per
                    for a in range(per):
                        for r in range(2):
                            ins = pe.matmul(bank[:, width * a:width * a + width], half_way[:, n - per + a, P * r:P * r + P],
                                            trans[:, IFRFT if j < 4 else IFFT_H, r, 0:width], start=(r == 0), stop=(r == 1))
                    ins.then_inc(back_vec_made, 1)

            def final(i):
                pe.wait_ge(lut, i * LUTS + 11)
                pe.wait_ge(first_kept, i + 1)
                pe.wait_ge(back_vec_read, back_vec.end(i, "inverse"))
                for j in range(9):
                    if j < 8:
                        bank = back_act.to_write(i, "final", j)
                        for r in range(8):
                            for im in (slice(0, 64), slice(64, 128)):
                                ins = pe.matmul(bank[im, 64 * r:64 * r + 64], cat[:, :, 8 * j + r], ident[:, im],
                                                start=True, stop=True)
                        ins.then_inc(back_act_made, 1)
                    if j:
                        pe.wait_ge(back_act_read, back_act.after(i, "final", j))
                        for t in range(TILES):
                            pe.matmul(back_vec.to_write(i, "final", 3 * (j - 1) + t), conv2[:, t * P:t * P + P],
                                      cat_t[:, 512 * (j - 1):512 * j], start=True, stop=True).then_inc(back_vec_made, 1)

            statistics(0)
            conv1_products(0)
            forward(0)
            if pairs > 1:
                with pe.Fori(0, pairs - 1) as i:
                    mixing(i, False)
                    conv1_products(i + 1)
                    inverse(i)
                    forward(i + 1)
                    final(i)
            mixing(pairs - 1, True)
            inverse(pairs - 1)
            final(pairs - 1)

        @block.vector
        def _(dve):
            dve.memset(gn.half[:, :], -0.5)
            dve.memset(zero[:, :], 0.0)
            dve.memset(quarter[:, :], math.pi / 2)
            dve.memset(spatial_in[:, :, :], 0.0)
            dve.memset(cat[:, :, :], 0.0)
            dve.wait_ge(par_in, 16 * N_LOADS)
            by_channel = lambda r: rows_in[:, r, :].unsqueeze(2).to_broadcast([P, G, SIDE])
            by_row = mask[:, :].unsqueeze(1).to_broadcast([P, G, SIDE])
            dve.tensor_scalar(turn_bias[:, :], rows_in[:, PHA_B:PHA_B + 2, :].rearrange("p a c -> p (a c)"),
                              1.0 / (2 * math.pi), None, ALU.mult)
            dve.tensor_tensor(bias_map[:, :, :], by_channel(MAG_S_B), by_row, ALU.mult).then_inc(bias_steps, 1)
            dve.tensor_tensor(w2[:, 0:G], by_channel(MAG_F_B), by_row, ALU.mult).then_inc(bias_steps, 1)
            dve.wait_ge(bias_steps, 2)
            dve.tensor_tensor(w2[:, 0:G], by_channel(MAG_F_B), w2[:, 0:G], ALU.subtract).then_inc(bias_steps, 1)
            dve.wait_ge(bias_steps, 3)
            dve.tensor_tensor(bias_map[:, :, :], bias_map[:, :, :], w2[:, 0:G], ALU.add).then_inc(bias_steps, 1)
            dve.wait_ge(prepared, 1)
            if batch_norm:
                dve.tensor_tensor(out_bias[:, :], back_vec_ps[:, 1, 0:TILES], bn_cols[:, 1, :], ALU.add).then_inc(prepared, 1)
            else:
                dve.tensor_copy(out_bias[:, :], back_vec_ps[:, 1, 0:TILES]).then_inc(prepared, 1)
            dve.wait_ge(bias_steps, 4)
            dve.tensor_tensor(conv2[:, :], back_vec_ps[:, 0, 0:2 * CH], conv2[:, :], ALU.add).then_inc(prepared, 1)
            dve.wait_ge(prepared, 3)
            re, im = field[:, 0], field[:, 1]

            def statistics(i):
                def base(t):
                    dve.wait_ge(x_in_s[t], (i + 1) * 16)
                    if batch_norm:
                        dve.wait_ge(z_in, (i * TILES + t + 1) * 16)
                        dve.scalar_tensor_tensor(out=x[:, t, :], in0=z[:, :], scalar=bn_cols[:, 0, t:t + 1],
                                                 in1=x[:, t, :], op0=ALU.mult, op1=ALU.add).then_inc(based, 1)
                        dve.wait_ge(based, i * TILES + t + 1)

                gn.statistics(dve, i, x, base, bn_cols[:, 1, :] if batch_norm else None)

            def normalise(i):
                gn.scales(dve, i, front_vec_ps[:, 0, 0:2 * TILES], bn_cols[:, 1, :] if batch_norm else None)
                for t in range(TILES):
                    if batch_norm:
                        dve.wait_ge(base_stored[t], (i + 1) * 16)
                    dve.tensor_scalar(x[:, t, :], x[:, t, :], gn.rstd[:, t:t + 1], gn.shift[:, t:t + 1],
                                      ALU.mult, ALU.add).then_inc(normed, 1)

            def planes_of(bank):
                return bank.rearrange("p (a r n) -> p r a n", a=2, r=2)

            def field_of(j):
                return field[:, :, 4 * j:4 * j + 4, :].rearrange("p r (a c) h -> p r a (c h)", a=2)

            def polar(i, between):
                def after(n):
                    dve.wait_ge(calc, i * CALCS + n)

                for j in range(8):
                    dve.tensor_copy(field_of(j), planes_of(front_vec.to_read(dve, i, "forward", j))).then_inc(front_vec_read, 1)
                between(0)
                dve.wait_ge(lut, i * LUTS + 2)
                dve.tensor_tensor(w0, w0, w1, ALU.add).then_inc(calc, 1)
                between(1)
                dve.wait_ge(lut, i * LUTS + 3)
                dve.scalar_tensor_tensor(out=w0, in0=re, scalar=-1.0, in1=re, op0=ALU.mult, op1=ALU.max).then_inc(calc, 1)
                after(2)
                dve.scalar_tensor_tensor(out=w0, in0=w0, scalar=1e-30, in1=w1, op0=ALU.max, op1=ALU.add).then_inc(calc, 1)
                between(2)
                for half in range(2):
                    after(3)
                    c = slice(G * half, G * half + G)
                    ins = dve.reciprocal(w0[:, c], w0[:, c])
                    between(3 + half)
                ins.then_inc(calc, 1)
                after(4)
                dve.tensor_tensor(w0, w0, im, ALU.mult).then_inc(calc, 1)
                between(5)
                dve.wait_ge(lut, i * LUTS + 4)
                dve.tensor_scalar(w0, im, 0.0, math.pi, ALU.is_ge, ALU.mult).then_inc(calc, 1)
                after(6)
                dve.scalar_tensor_tensor(out=w0, in0=w2, scalar=-2.0, in1=w0, op0=ALU.mult, op1=ALU.add).then_inc(calc, 1)
                dve.tensor_scalar(w3, re, 0.0, None, ALU.is_lt).then_inc(calc, 1)
                after(8)
                between(6)
                dve.scalar_tensor_tensor(out=w0, in0=w0, scalar=-math.pi / 2, in1=w3, op0=ALU.add, op1=ALU.mult).then_inc(calc, 1)
                after(9)
                for g in (0, G):
                    ins = dve.tensor_tensor(blocked(w3[:, g:g + G]), by_block(w2[:, g:g + G]), by_block(w0[:, g:g + G]), ALU.add)
                ins.then_inc(calc, 1)
                between(7)
                after(10)
                dve.tensor_tensor(blocked(w0[:, 0:G]), by_block(w1[:, 0:G]), by_block(by_row), ALU.mult).then_inc(calc, 1)
                after(11)
                dve.tensor_tensor(blocked(w0[:, G:MIX]), by_block(w1[:, 0:G]), blocked(w0[:, 0:G]), ALU.subtract).then_inc(calc, 1)
                between(8)

            def back(i, last):
                def after(n):
                    dve.wait_ge(calc, i * CALCS + n)

                if not last:
                    statistics(i + 1)
                dve.wait_ge(back_act_read, back_act.after(i, "turned", 4))
                for half in range(2):
                    rows = slice(32 * half, 32 * half + 32)
                    dve.tensor_tensor(w0[:, 0:G, rows], back_vec.to_read(dve, i, "spatial", half).rearrange("p (o h) -> p o h", h=32),
                                      by_row[:, :, rows], ALU.mult).then_inc(back_vec_read, 1)
                for half in range(2):
                    rows = slice(32 * half, 32 * half + 32)
                    dve.wait_ge(back_vec_read, back_vec.after(i, "spatial", half + 1))
                    dve.tensor_tensor(w0[:, 0:G, rows], back_vec.to_read(dve, i, "fourier", half).rearrange("p (o h) -> p o h", h=32),
                                      w0[:, 0:G, rows], ALU.add).then_inc(back_vec_read, 1)
                dve.wait_ge(back_vec_read, back_vec.end(i, "fourier"))
                dve.wait_ge(back_act_read, back_act.end(i, "turned"))
                dve.tensor_tensor(blocked(w2[:, G:MIX]), by_block(w0[:, 0:G]), by_block(bias_map[:, :, :]), ALU.add).then_inc(calc, 1)
                if not last:
                    normalise(i + 1)
                for j in range(4):
                    g, half = divmod(j, 2)
                    bias = rows_in[:, MAG_B + g, :].unsqueeze(2).to_broadcast([P, G, 32])
                    dve.tensor_tensor(w1[:, G * g:G * g + G, 32 * half:32 * half + 32],
                                      back_vec.to_read(dve, i, "magnitude", j).rearrange("p (o h) -> p o h", h=32), bias, ALU.add)\
                        .then_inc(back_vec_read, 1)
                dve.wait_ge(back_act_read, back_act.end(i, "phase"))
                dve.tensor_tensor(w3, w3, turn_bias[:, :].unsqueeze(2).to_broadcast([P, MIX, SIDE]), ALU.add).then_inc(calc, 1)
                after(14)
                dve.tensor_scalar(w0, w3, ROUND, -ROUND, ALU.add, ALU.add).then_inc(calc, 1)
                after(15)
                dve.tensor_tensor(w3, w3, w0, ALU.subtract).then_inc(calc, 1)
                dve.wait_ge(back_vec_read, back_vec.end(i, "magnitude"))
                dve.wait_ge(lut, i * LUTS + 8)
                dve.tensor_tensor(re, w1, w0, ALU.mult).then_inc(calc, 1)
                dve.tensor_tensor(im, w1, w2, ALU.mult).then_inc(calc, 1)
                for j in range(4):
                    dve.tensor_copy(field_of(j), planes_of(back_vec.to_read(dve, i, "inverse", j))).then_inc(back_vec_read, 1)
                for j in range(4, 6):
                    c = 2 * G + 8 * (j - 4)
                    dve.tensor_copy(cat[:, c:c + 8, :].rearrange("p c h -> p (c h)"), back_vec.to_read(dve, i, "inverse", j))\
                        .then_inc(back_vec_read, 1)
                dve.wait_ge(lut, i * LUTS + 10)
                dve.tensor_tensor(w0[:, 0:G], w0[:, 0:G], w1[:, 0:G], ALU.add).then_inc(calc, 1)

                def results(ms):
                    for m in ms:
                        j, t = divmod(m, TILES)
                        if t == 0:
                            dve.wait_ge(again_in[j % 2], i * 4 * 16 + 16 * (j // 2 + 1))
                        dve.scalar_tensor_tensor(out=again[:, j % 2, t, :], in0=back_vec.to_read(dve, i, "final", m),
                                                 scalar=out_bias[:, t:t + 1], in1=again[:, j % 2, t, :],
                                                 op0=ALU.add, op1=ALU.add).then_inc(back_vec_read, 1)

                if last:
                    results(range(24))
                else:
                    steps = RESULT_STEPS
                    polar(i + 1, lambda n: results(range(steps[n], steps[n + 1])))

            RESULT_STEPS = (0, 0, 3, 6, 9, 12, 15, 18, 21, 24)
            statistics(0)
            normalise(0)
            polar(0, lambda n: None)
            if pairs > 1:
                with dve.Fori(0, pairs - 1) as i:
                    back(i, False)
            back(pairs - 1, True)


def wkv_layer(nc, x_in, x_out, par, pairs=PAIRS):
    T = 512
    STEPS = TOKENS // T
    UNITS = TILES * STEPS * 2
    ORDER = [b for s in range(STEPS // 2) for b in (s, STEPS - 1 - s)]
    BLOCKS = TILES * STEPS

    def unit(u):
        t, s, d = u // (2 * STEPS), u // 2 % STEPS, u % 2
        return t, s, d, (s if d == 0 else STEPS - 1 - s), u % 3

    def folds(u):
        t, r = divmod(u, 2 * STEPS)
        return t * 4 * STEPS + min(r, STEPS) + 3 * max(r - STEPS, 0)

    def copies_before(t, b, which):
        return (t * STEPS + ORDER.index(b)) * 2 + which

    def last_visit(t, b):
        s, d = (b, 0) if b >= STEPS // 2 else (STEPS - 1 - b, 1)
        return (t * STEPS + s) * 2 + d

    with ExitStack() as ctx:
        sb, ps, sem = makers(nc, ctx, "wkv_")
        xn = sb("xn", [P, TILES, TOKENS])
        h = sb("h", [P, TILES, TOKENS])
        k = sb("k", [P, TOKENS])
        v = sb("v", [P, TOKENS])
        gate = sb("gate", [P, TOKENS])
        top = sb("top", [P, 3, T + 2])
        rise = sb("rise", [P, 3, T])
        decay = sb("decay", [P, 3, T])
        own = sb("own", [P, 3, T])
        own_v = sb("own_v", [P, 3, T])
        qp = sb("qp", [P, 3, 2, T + 2])
        wk, wv, wr, wo = (sb(n, [P, 7, P]) for n in ("wk", "wv", "wr", "wo"))
        centre = h[:, 0, 0:7 * P].rearrange("p (b n) -> p b n", b=7)
        wo_raw = h[:, 1, 0:7 * P].rearrange("p (b n) -> p b n", b=7)
        col = sb("col", [P, 8, TILES])
        LNG, LNB, WD, U, OB = range(5)
        gn = GroupNorm(nc, sb, sem, P)
        ones = sb("ones", [P, 3, P])
        half_log = sb("half_log", [P, 1])
        squares = gate[:, 0:6 * T].rearrange("p (r t n) -> p r t n", r=2, t=TILES)
        spread = gate[:, 6 * T:8 * T].rearrange("p (r n) -> p r n", r=2)
        x_again = k[:, 0:6 * T].rearrange("p (r t n) -> p r t n", r=2, t=TILES)
        result = v[:, 0:6 * T].rearrange("p (r t n) -> p r t n", r=2, t=TILES)
        mean_sq = k[:, 6 * T:8 * T].rearrange("p (r n) -> p r n", r=2)

        kv_ps = ps("kv_ps", [P, 4, 512])
        gate_ps = ps("gate_ps", [P, 2, 512])
        stat_ps = ps("stat_ps", [P, 2, 512])

        par_in, prepared = sem("par_in"), sem("prepared")
        x_in_s = [sem(f"x_in{t}") for t in range(TILES)]
        normed = sem("normed")
        kv_made, kv_copied = sem("kv_made"), sem("kv_copied")
        gate_made, gate_ready = sem("gate_made"), sem("gate_ready")
        trend, weighted, sums, fraction, inverse, folded = (
            sem(n) for n in ("trend", "weighted", "sums", "fraction", "inverse", "folded"))
        squared, stats_made, var_ready, rs_ready, out_made, scaled, out_ready = (
            sem(n) for n in ("squared", "stats_made", "var_ready", "rs_ready", "out_made", "scaled", "out_ready"))
        again_in = [sem("again_in0"), sem("again_in1")]
        stored = [sem("stored0"), sem("stored1")]

        rows = x_in.rearrange("(q t p) n -> q p t n", p=P, t=TILES)
        out_rows = x_out.rearrange("(q t p) n -> q p t n", p=P, t=TILES)
        block = ctx.enter_context(nc.Block())
        LOADS = 10

        @block.sync
        def _(sp):
            for dst, name in ((wk, "wk"), (wv, "wv"), (wr, "wr")):
                sp.dma_start(dst[:, :, :], par[name].rearrange("b p n -> p b n")).then_inc(par_in, 16)
            sp.dma_start(wo_raw, par["wo"].rearrange("b p n -> p b n")).then_inc(par_in, 16)
            sp.dma_start(centre, par["centre"].rearrange("b p n -> p b n")).then_inc(par_in, 16)
            sp.dma_start(gn.mix[:, :, :], par["gn_mix"].rearrange("b p n -> p b n")).then_inc(par_in, 16)
            sp.dma_start(ones[:, :, :], par["image_mean"].rearrange("t p n -> p t n")).then_inc(par_in, 16)
            for c, name in ((LNG, "ln_g"), (LNB, "ln_b"), (WD, "w_decay")):
                sp.dma_start(col[:, c, :], par[name]).then_inc(par_in, 16)
            sp.dma_start(col[:, U, :], par["u"]).then_inc(par_in, 16)

            def load_x(i):
                for t in range(TILES):
                    sp.dma_start(xn[:, t, :], rows[i, :, t, :]).then_inc(x_in_s[t], 16)

            def final_traffic(i):
                def load(b):
                    if b < 2:
                        sp.wait_ge(folded, (i + 1) * folds(UNITS))
                    else:
                        sp.wait_ge(out_ready, i * BLOCKS + 3 * (b - 1))
                    sp.dma_start(x_again[:, b % 2, :, :], rows[i, :, :, b * T:(b + 1) * T]).then_inc(again_in[b % 2], 16)

                load(0)
                load(1)
                for b in range(STEPS):
                    sp.wait_ge(out_ready, i * BLOCKS + 3 * (b + 1))
                    sp.dma_start(out_rows[i, :, :, b * T:(b + 1) * T], result[:, b % 2, :, :]).then_inc(stored[b % 2], 16)
                    if b + 2 < STEPS:
                        load(b + 2)

            load_x(0)
            if pairs > 1:
                with sp.Fori(0, pairs - 1) as i:
                    sp.wait_ge(gate_made, i * BLOCKS + BLOCKS)
                    load_x(i + 1)
                    final_traffic(i)
            final_traffic(pairs - 1)
            for s in stored:
                sp.wait_ge(s, pairs * 16 * STEPS // 2)

        @block.gpsimd
        def _(pool):
            with pool.Fori(0, pairs) as i:
                gn.power(pool, i)
                for u in range(UNITS):
                    t, s, d, c, z = unit(u)
                    own_pos = slice(0, T) if d == 0 else slice(1, T + 1)
                    n = i * 4 * UNITS + 4 * u
                    pool.wait_ge(sums, n + 4)
                    pool.tensor_tensor(decay[:, z, :], rise[:, z, :], qp[:, z, 1, own_pos], ALU.mult).then_inc(fraction, 1)
                    pool.wait_ge(fraction, n + 1)
                    pool.tensor_tensor(decay[:, z, :], decay[:, z, :], own_v[:, z, :], ALU.add).then_inc(fraction, 1)
                    pool.tensor_tensor(rise[:, z, :], rise[:, z, :], qp[:, z, 0, own_pos], ALU.mult).then_inc(fraction, 1)
                    pool.wait_ge(fraction, n + 3)
                    pool.tensor_tensor(rise[:, z, :], rise[:, z, :], own[:, z, :], ALU.add).then_inc(fraction, 1)

        @block.scalar
        def _(act):
            act.wait_ge(par_in, 16 * (LOADS + 1))
            act.activation(col[:, 5, :], col[:, WD, :], ACT.Exp).then_inc(prepared, 1)

            act.preload_act_table_set("natural_log_exp_and_others")
            with act.Fori(0, pairs) as i:
                def copy(t, b, which):
                    m = copies_before(t, b, which)
                    act.wait_ge(kv_made, i * 2 * BLOCKS + m + 1)
                    if t:
                        u = last_visit(t - 1, b)
                        if which == 0:
                            act.wait_ge(trend, i * 4 * UNITS + 4 * u + 4)
                        else:
                            act.wait_ge(sums, i * 4 * UNITS + 4 * u + 2)
                    elif which == 0:
                        act.wait_ge(out_ready, i * BLOCKS)
                    else:
                        for q in stored:
                            act.wait_ge(q, i * 16 * STEPS // 2)
                    act.activation((k, v)[which][:, b * T:(b + 1) * T], kv_ps[:, m % 4, :], ACT.Copy).then_inc(kv_copied, 1)

                def exps(u):
                    t, s, d, c, z = unit(u)
                    act.wait_ge(trend, i * 4 * UNITS + 4 * u + 4)
                    act.activation(decay[:, z, :], rise[:, z, :], ACT.Exp, bias=col[:, 6, t:t + 1]).then_inc(weighted, 1)
                    act.wait_ge(weighted, i * 3 * UNITS + 3 * u + 1)
                    act.activation(rise[:, z, :], rise[:, z, :], ACT.Exp, bias=col[:, 7, t:t + 1]).then_inc(weighted, 1)
                    act.activation(own[:, z, :], own[:, z, :], ACT.Exp).then_inc(weighted, 1)

                def invert(u):
                    z = unit(u)[4]
                    act.wait_ge(fraction, i * 4 * UNITS + 4 * u + 4)
                    act.activation(rise[:, z, :], rise[:, z, :], ACT.Ln).then_inc(inverse, 1)
                    act.wait_ge(inverse, i * 2 * UNITS + 2 * u + 1)
                    act.activation(rise[:, z, :], rise[:, z, :], ACT.Exp, bias=half_log[:, 0:1], scale=-1.0).then_inc(inverse, 1)

                for u in range(-1, UNITS + 1):
                    if u + 1 < UNITS:
                        t, s, d, c, z = unit(u + 1)
                        if s < STEPS // 2:
                            copy(t, c, 0)
                        if u == -1:
                            act.wait_ge(prepared, 5)
                        exps(u + 1)
                    if u >= 1:
                        invert(u - 1)
                    if u + 1 < UNITS:
                        if s < STEPS // 2:
                            copy(t, c, 1)
                        if s == STEPS // 2 - 1 and d == 1:
                            for b in range(STEPS):
                                act.wait_ge(gate_made, i * BLOCKS + t * STEPS + b + 1)
                                if t and b == 0:
                                    act.wait_ge(folded, i * folds(UNITS) + folds(t * 2 * STEPS))
                                elif b == 0:
                                    act.wait_ge(out_ready, i * BLOCKS)
                                act.activation(gate[:, b * T:(b + 1) * T], gate_ps[:, b % 2, :], ACT.Sigmoid)\
                                    .then_inc(gate_ready, 1)
                            act.preload_act_table_set("natural_log_exp_and_others")
                for b in range(STEPS):
                    if b == 0:
                        act.wait_ge(folded, (i + 1) * folds(UNITS))
                    else:
                        act.wait_ge(stats_made, i * STEPS + max(b - 1, 0))
                    act.activation(squares[:, b % 2, :, :], h[:, :, b * T:(b + 1) * T], ACT.Square).then_inc(squared, 1)
                    act.wait_ge(stats_made, i * STEPS + b + 1)
                    if b >= 1:
                        act.wait_ge(var_ready, i * 2 * STEPS + 2 * b)
                    act.activation(mean_sq[:, b % 2, :], stat_ps[:, 0, :], ACT.Square).then_inc(squared, 1)
                    act.wait_ge(var_ready, i * 2 * STEPS + 2 * b + 2)
                    act.activation(spread[:, b % 2, :], spread[:, b % 2, :], ACT.Ln).then_inc(rs_ready, 1)
                    act.wait_ge(rs_ready, i * 2 * STEPS + 2 * b + 1)
                    act.activation(spread[:, b % 2, :], spread[:, b % 2, :], ACT.Exp, scale=-0.5).then_inc(rs_ready, 1)

        @block.tensor
        def _(pe):
            pe.wait_ge(par_in, 16 * (LOADS + 1))
            pe.wait_ge(prepared, 3)
            for t in range(TILES):
                for j, s in enumerate(SOURCES[t]):
                    both = [q for q in SOURCES[s] if q in SOURCES[t]]
                    for q in both:
                        pe.matmul(kv_ps[:, t, j * P:(j + 1) * P], centre[:, BLOCK[q, s], :], wo[:, BLOCK[q, t], :],
                                  start=(q == both[0]), stop=(q == both[-1]))
            for t in range(TILES):
                for n, s in enumerate(SOURCES[t]):
                    ins = pe.matmul(stat_ps[:, 0, t:t + 1], wo_raw[:, BLOCK[s, t], :], col[:, LNB, s:s + 1],
                                    start=(n == 0), stop=(n == len(SOURCES[t]) - 1))
            ins.then_inc(prepared, 1)
            pe.wait_ge(prepared, 5)

            with pe.Fori(0, pairs) as i:
                pe.wait_ge(var_ready, i * 2 * STEPS)
                gn.mix_stats(pe, i, stat_ps[:, 0, 0:2 * TILES])

                def product(w, out, t, b, sem_):
                    for n, s in enumerate(SOURCES[t]):
                        ins = pe.matmul(out, w[:, BLOCK[s, t], :], xn[:, s, b * T:(b + 1) * T],
                                        start=(n == 0), stop=(n == len(SOURCES[t]) - 1))
                    ins.then_inc(sem_, 1)

                for t in range(TILES):
                    pe.wait_ge(normed, i * TILES + (2, 3, 3)[t])
                    for j, b in enumerate(ORDER):
                        for which in range(2):
                            m = (t * STEPS + j) * 2 + which
                            pe.wait_ge(kv_copied, i * 2 * BLOCKS + max(m - 3, 0))
                            if t == 0 and j == 0:
                                pe.wait_ge(scaled, i * BLOCKS)
                            product((wk, wv)[which], kv_ps[:, m % 4, :], t, b, kv_made)
                    for b in range(STEPS):
                        pe.wait_ge(gate_ready, i * BLOCKS + max(t * STEPS + b - 1, 0))
                        product(wr, gate_ps[:, b % 2, :], t, b, gate_made)
                for b in range(STEPS):
                    chunk = slice(b * T, (b + 1) * T)
                    pe.wait_ge(squared, i * 2 * STEPS + 2 * b + 1)
                    if b:
                        pe.wait_ge(var_ready, i * 2 * STEPS + 2 * b)
                    for which in range(2):
                        for s in range(TILES):
                            ins = pe.matmul(stat_ps[:, which, :], ones[:, s, :],
                                            (h[:, s, chunk], squares[:, b % 2, s, :])[which],
                                            start=(s == 0), stop=(s == TILES - 1))
                    ins.then_inc(stats_made, 1)
                    if b == 0:
                        pe.wait_ge(kv_copied, (i + 1) * 2 * BLOCKS)
                    for t in range(TILES):
                        m = b * TILES + t
                        pe.wait_ge(scaled, i * BLOCKS + max(m - 3, 0))
                        for n, s in enumerate(SOURCES[t]):
                            ins = pe.matmul(kv_ps[:, m % 4, :], wo[:, BLOCK[s, t], :], h[:, s, chunk],
                                            start=(n == 0), stop=(n == len(SOURCES[t]) - 1))
                        ins.then_inc(out_made, 1)

        @block.vector
        def _(dve):
            dve.memset(gn.half[:, :], -0.5)
            dve.memset(half_log[:, :], -math.log(2.0)).then_inc(prepared, 1)
            dve.wait_ge(par_in, 16 * (LOADS + 1))
            for t in range(TILES):
                for s in SOURCES[t]:
                    ins = dve.tensor_scalar(wo[:, BLOCK[s, t], :], wo_raw[:, BLOCK[s, t], :], col[:, LNG, s:s + 1], None, ALU.mult)
            ins.then_inc(prepared, 1)
            dve.wait_ge(prepared, 4)
            for t in range(TILES):
                n = len(SOURCES[t])
                for j, s in enumerate(SOURCES[t]):
                    dve.tensor_copy(wo[:, BLOCK[s, t], :], kv_ps[:, t, j * P:(j + 1) * P])
            dve.tensor_copy(col[:, OB, :], stat_ps[:, 0, 0:TILES])
            dve.tensor_scalar(col[:, 6, :], col[:, 5, :], -1.0, None, ALU.mult)
            dve.tensor_scalar(col[:, 7, :], col[:, U, :], -1.0, None, ALU.mult).then_inc(prepared, 1)

            with dve.Fori(0, pairs) as i:
                gn.statistics(dve, i, xn, lambda t: dve.wait_ge(x_in_s[t], i * 16 + 16))
                gn.scales(dve, i, stat_ps[:, 0, 0:2 * TILES])
                for t in range(TILES):
                    dve.tensor_scalar(xn[:, t, :], xn[:, t, :], gn.rstd[:, t:t + 1], gn.shift[:, t:t + 1],
                                      ALU.mult, ALU.add).then_inc(normed, 1)

                def trends(u):
                    t, s, d, c, z = unit(u)
                    new, old, at = ((slice(1, T + 1), slice(0, T), 0), (slice(0, T), slice(1, T + 1), T))[d]
                    flip = (lambda a: a) if d == 0 else (lambda a: a[:, ::-1])
                    n = i * 4 * UNITS + 4 * u
                    if s == 0:
                        dve.memset(top[:, z, at:at + 1], NEG_INF).then_inc(trend, 1)
                    else:
                        y = unit(u - 2)[4]
                        dve.tensor_copy(top[:, z, at:at + 1], top[:, y, (T, 0)[d]:(T, 0)[d] + 1]).then_inc(trend, 1)
                    dve.wait_ge(trend, n + 1)
                    if s < STEPS // 2:
                        dve.wait_ge(kv_copied, i * 2 * BLOCKS + copies_before(t, c, 0) + 1)
                    chunk = k[:, c * T:(c + 1) * T]
                    dve.tensor_tensor_scan(flip(top[:, z, new]), col[:, 6, t:t + 1].to_broadcast([P, T]), flip(chunk),
                                           top[:, z, at:at + 1], ALU.add, ALU.max).then_inc(trend, 1)
                    dve.wait_ge(trend, n + 2)
                    dve.tensor_tensor(rise[:, z, :], top[:, z, old], top[:, z, new], ALU.subtract).then_inc(trend, 1)
                    dve.tensor_tensor(own[:, z, :], chunk, top[:, z, new], ALU.subtract).then_inc(trend, 1)

                def accumulate(u):
                    t, s, d, c, z = unit(u)
                    new, at = ((slice(1, T + 1), 0), (slice(0, T), T))[d]
                    flip = (lambda a: a) if d == 0 else (lambda a: a[:, ::-1])
                    n = i * 4 * UNITS + 4 * u
                    if s == 0:
                        dve.memset(qp[:, z, :, at:at + 1], 0.0).then_inc(sums, 1)
                    else:
                        y, e = unit(u - 2)[4], (T, 0)[d]
                        dve.tensor_copy(qp[:, z, :, at:at + 1], qp[:, y, :, e:e + 1]).then_inc(sums, 1)
                    dve.wait_ge(weighted, i * 3 * UNITS + 3 * u + 3)
                    if s < STEPS // 2:
                        dve.wait_ge(kv_copied, i * 2 * BLOCKS + copies_before(t, c, 1) + 1)
                    dve.tensor_tensor(own_v[:, z, :], own[:, z, :], v[:, c * T:(c + 1) * T], ALU.mult).then_inc(sums, 1)
                    dve.wait_ge(sums, n + 1)
                    dve.tensor_tensor_scan(flip(qp[:, z, 0, new]), flip(decay[:, z, :]), flip(own[:, z, :]),
                                           qp[:, z, 0, at:at + 1], ALU.mult, ALU.add).then_inc(sums, 1)
                    dve.wait_ge(sums, n + 2)
                    dve.tensor_tensor_scan(flip(qp[:, z, 1, new]), flip(decay[:, z, :]), flip(own_v[:, z, :]),
                                           qp[:, z, 1, at:at + 1], ALU.mult, ALU.add).then_inc(sums, 1)

                def fold(u):
                    t, s, d, c, z = unit(u)
                    chunk = h[:, t, c * T:(c + 1) * T]
                    n = i * folds(UNITS) + folds(u)
                    dve.wait_ge(inverse, i * 2 * UNITS + 2 * u + 2)
                    if s < STEPS // 2:
                        dve.tensor_tensor(chunk, decay[:, z, :], rise[:, z, :], ALU.mult).then_inc(folded, 1)
                        return
                    dve.tensor_tensor(decay[:, z, :], decay[:, z, :], rise[:, z, :], ALU.mult).then_inc(folded, 1)
                    dve.wait_ge(folded, n + 1)
                    dve.tensor_tensor(chunk, chunk, decay[:, z, :], ALU.add).then_inc(folded, 1)
                    dve.wait_ge(folded, n + 2)
                    dve.wait_ge(gate_ready, i * BLOCKS + t * STEPS + STEPS)
                    dve.tensor_tensor(chunk, chunk, gate[:, c * T:(c + 1) * T], ALU.mult).then_inc(folded, 1)

                for u in range(-1, UNITS + 1):
                    if u + 1 < UNITS:
                        trends(u + 1)
                    if 0 <= u < UNITS:
                        accumulate(u)
                    if u >= 1:
                        fold(u - 1)

                for b in range(STEPS):
                    chunk = slice(b * T, (b + 1) * T)
                    dve.wait_ge(squared, i * 2 * STEPS + 2 * b + 2)
                    if b >= 2:
                        dve.wait_ge(scaled, i * BLOCKS + 3 * (b - 1))
                    dve.scalar_tensor_tensor(out=spread[:, b % 2, :], in0=mean_sq[:, b % 2, :], scalar=-1.0,
                                             in1=stat_ps[:, 1, :], op0=ALU.mult, op1=ALU.add).then_inc(var_ready, 1)
                    dve.wait_ge(var_ready, i * 2 * STEPS + 2 * b + 1)
                    dve.tensor_scalar(spread[:, b % 2, :], spread[:, b % 2, :], 0.0, LN_EPS, ALU.max, ALU.add).then_inc(var_ready, 1)
                    dve.wait_ge(rs_ready, i * 2 * STEPS + 2 * b + 2)
                    if b >= 2:
                        dve.wait_ge(stored[b % 2], i * 16 * STEPS // 2 + 16 * (b // 2))
                    dve.wait_ge(again_in[b % 2], i * 16 * STEPS // 2 + 16 * (b // 2 + 1))
                    for t in range(TILES):
                        m = b * TILES + t
                        dve.wait_ge(out_made, i * BLOCKS + m + 1)
                        for half in range(2):
                            image = (0, 0, 1) [t] if half == 0 else (0, 1, 1)[t]
                            mine = slice(64 * half, 64 * half + 64)
                            ins = dve.tensor_tensor(result[mine, b % 2, t, :], kv_ps[mine, m % 4, :],
                                                    spread[64 * image:64 * image + 64, b % 2, :], ALU.mult)
                        ins.then_inc(scaled, 1)
                        dve.wait_ge(scaled, i * BLOCKS + m + 1)
                        dve.scalar_tensor_tensor(out=result[:, b % 2, t, :], in0=result[:, b % 2, t, :], scalar=col[:, OB, t:t + 1],
                                                 in1=x_again[:, b % 2, t, :], op0=ALU.add, op1=ALU.add).then_inc(out_ready, 1)



def _blocks(big):
    return np.stack([big[P * s:P * s + P, P * t:P * t + P] for (s, t) in BLOCK])


def _twice(w):
    big = np.zeros((2 * w.shape[0], 2 * w.shape[1]), np.float32)
    big[:w.shape[0], :w.shape[1]] = w
    big[w.shape[0]:, w.shape[1]:] = w
    return big


def _columns(v):
    return np.ascontiguousarray(np.concatenate([v, v]).reshape(TILES, P).T)


def wkv_params(p, inputs):
    r = np.arange(2 * CH)
    same = (r[:, None] // CH == r[None, :] // CH)
    arrays = {}
    for n, key in (("wk", "Wk"), ("wv", "Wv"), ("wr", "Wr"), ("wo", "Wo")):
        arrays[n] = _blocks(_twice(inputs[p + key].T))
    arrays["centre"] = _blocks((np.eye(2 * CH) - same / CH).astype(np.float32))
    for n, key in (("ln_g", "ln_g"), ("ln_b", "ln_b"), ("w_decay", "w_decay"), ("u", "u")):
        arrays[n] = _columns(inputs[p + key])
    return arrays


def shared_constants():
    r = np.arange(2 * CH)
    group = CH // 32
    mix = (r[:, None] // group == r[None, :] // group) / group
    image = (r.reshape(TILES, P, 1) // CH == np.arange(P)[None, None, :] // 64) / CH
    return {"gn_mix": _blocks(mix.astype(np.float32)), "image_mean": image.astype(np.float32)}


def fractional_matrix(a):
    n = SIDE
    eye = np.eye(n, dtype=np.complex128)
    if a < 0.5:
        shift = (np.arange(n) + n // 2) % n
        eye = np.fft.ifft(eye[:, shift], axis=-1) * math.sqrt(n)
        eye = eye[:, np.argsort(shift)]
        a = a + 1.0

    def full_convolution(f, kern):
        length = f.shape[-1] + kern.shape[0] - 1
        return np.fft.ifft(np.fft.fft(f, n=length, axis=-1) * np.fft.fft(kern, n=length), axis=-1)

    alpha = a * math.pi / 2
    tana2, sina = math.tan(alpha / 2), math.sin(alpha)
    y = np.zeros((n, 2 * n - 1), np.complex128)
    y[:, ::2] = eye
    fi = full_convolution(y, np.sinc(np.arange(-(2 * n - 3), 2 * n - 2) / 2.0))[:, 2 * n - 3:4 * n - 4]
    pad = np.zeros((n, n - 1))
    t = np.arange(-2 * n + 2, 2 * n - 1).astype(np.float64)
    chirp = np.exp(-1j * math.pi / n * tana2 / 4 * t ** 2)
    c = math.pi / n / sina / 4
    m = np.arange(-(4 * n - 4), 4 * n - 3).astype(np.float64)
    ret = full_convolution(chirp * np.concatenate([pad, fi, pad], axis=-1), np.exp(1j * c * m ** 2))
    ret = ret[:, 4 * n - 4:8 * n - 7] * math.sqrt(c / math.pi) * chirp
    return np.exp(-1j * (1 - a) * math.pi / 4) * ret[:, n - 1:3 * n - 2:2]


def fourier_constants():
    n = SIDE
    k = np.arange(n)
    turn = np.outer(k, k) % n
    cos, sin = np.cos(2 * math.pi * turn / n), np.sin(2 * math.pi * turn / n)
    cos[turn % 32 == 16] = 0.0
    sin[turn % 32 == 0] = 0.0
    weight = np.where((k == 0) | (k == n // 2), 1.0, np.where(k < n // 2, 2.0, 0.0)) / (n * n)
    trans = np.zeros((5, P, 2, 256), np.float32)
    for f, m in enumerate((fractional_matrix(0.5), cos - 1j * sin, fractional_matrix(-0.5),
                           (cos + 1j * sin) * weight[:, None], cos + 1j * sin)):
        for r, parts in enumerate(((m.real, m.imag), (-m.imag, m.real))):
            for c, part in enumerate(parts):
                for image in range(2):
                    q = slice(n * image, n * image + n)
                    trans[f, q, r, P * c + n * image:P * c + n * image + n] = part
    inner = int(n * math.cos(0.25 * math.pi))
    first = (n - inner) // 2
    inside = ((k >= first) & (k < first + inner)).astype(np.float32)
    mask = np.outer(np.concatenate([inside, inside]), inside)
    return {"trans": trans, "mask": mask.astype(np.float32), "ident": np.eye(P, dtype=np.float32)}


def fourier_params(p, inputs):
    g, hb = 16, 8

    def by_rows(w):
        m = np.zeros((g, hb, g, hb), np.float32)
        for r in range(hb):
            m[:, r, :, r] = w.T
        return m.reshape(P, P)

    spatial = np.zeros((3, 3, g, hb, g, hb), np.float32)
    w = inputs[p + "mag_s_w"]
    for dw in range(3):
        for dh in range(3):
            for r in range(hb):
                q, s = divmod(r + dh - 1, hb)
                spatial[dw, q + 1, :, s, :, r] = w[:, :, dh, dw].T
    conv2 = inputs[p + "conv2_w"]
    rest = np.zeros((64, CH), np.float32)
    rest[g:3 * g] = conv2[:, g:].T
    first = np.zeros((g, 64), np.float32)
    first[:, :g] = inputs[p + "conv_0_w"]
    row = lambda key: inputs[p + key]
    rows = np.stack([row("mag_s_b"), row("mag_f_b"), row("mag_b"), row("conv_1_b"), row("pha_b"), row("conv_1_b")])
    c1 = inputs[p + "conv1_w"].T
    return {
        "mixers": np.stack([by_rows(row(k)) for k in ("mag_f_w", "mag_w", "pha_w", "conv_1_w")]),
        "spatial": spatial.reshape(9, P, P),
        "conv2_rest": _twice(rest),
        "conv0": _twice(first),
        "conv2_0": _twice(conv2[:, :g].T),
        "bias0": np.concatenate([row("conv_0_b")] * 2).reshape(2 * g, 1),
        "rows": np.ascontiguousarray(np.broadcast_to(rows, (P, 6, g))),
        "conv1": np.concatenate([c1, c1]).reshape(TILES, P, 3 * g),
    }


def conv_params(p, inputs):
    dw = inputs[p + "dw_w"].reshape(CH, 9)
    return {
        "pointwise": _blocks(_twice(inputs[p + "pw_w"].T)),
        "taps": np.ascontiguousarray(np.concatenate([dw, dw]).reshape(TILES, P, 9).transpose(1, 0, 2)),
        "affine": np.stack([_columns(inputs[p + "gamma"]), _columns(inputs[p + "beta"])], axis=1),
    }


def same_channel(pairs=PAIRS):
    r = np.arange(2 * CH)
    big = ((r[:, None] % CH == r[None, :] % CH) / (2.0 * pairs)).astype(np.float32)
    return np.stack([big[P * s:P * s + P, P * t:P * t + P] for s in range(TILES) for t in range(TILES)])


def build(nc, x, out, par):
    def scratch(name, shape):
        return nc.dram_tensor(name, shape, F32, kind="Internal").ap()

    z, bn_cols = scratch("z", [ROWS, TOKENS]), scratch("bn_cols", [P, 2, TILES])
    after_1, after_2 = scratch("after_1", [ROWS, TOKENS]), scratch("after_2", [ROWS, TOKENS])
    convolution_layer(nc, x, z, bn_cols, par["L0"])
    fourier_layer(nc, x, after_1, dict(par["L1"], bn_cols=bn_cols), "f1_", (z,))
    wkv_layer(nc, after_1, after_2, par["L2"])
    fourier_layer(nc, after_2, out, par["L3"], "f3_")


def kernel(**inputs):
    import concourse.bacc as _bacc
    from concourse.bass_utils import run_bass_kernel_spmd as _run

    nc = _bacc.Bacc("TRN2", target_bir_lowering=False, num_devices=1)
    inputs = {k: np.asarray(v) for k, v in inputs.items()}
    shared, waves = shared_constants(), fourier_constants()
    layers = {
        "L0": dict(conv_params("L0_conv_", inputs), same=same_channel(), ident=waves["ident"], gn_mix=shared["gn_mix"]),
        "L1": dict(fourier_params("L1_conv_", inputs), gn_mix=shared["gn_mix"], **waves),
        "L2": dict(wkv_params("L2_conv_", inputs), **shared),
        "L3": dict(fourier_params("L3_conv_", inputs), gn_mix=shared["gn_mix"], **waves),
    }
    arrays, par = {}, {}
    for layer, named in layers.items():
        par[layer] = {}
        for name, a in named.items():
            arrays[f"{layer}_{name}"] = a = np.ascontiguousarray(a)
            par[layer][name] = nc.dram_tensor(f"{layer}_{name}", a.shape, F32, kind="ExternalInput").ap()
    arrays["x"] = np.ascontiguousarray(inputs["x"]).reshape(ROWS, TOKENS)
    x = nc.dram_tensor("x", (ROWS, TOKENS), F32, kind="ExternalInput").ap()
    out = nc.dram_tensor("out", (ROWS, TOKENS), F32, kind="ExternalOutput").ap()
    build(nc, x, out, par)
    r = _run(nc, [arrays], core_ids=[0])
    return r.results[0]["out"].reshape(BATCH, CH, SIDE, SIDE)
```

```python
import math
from contextlib import ExitStack

import numpy as np

import concourse.bass as bass
from concourse import mybir

P = 128
BATCH, CH, SIDE = 32, 192, 64
TOKENS = SIDE * SIDE
ROWS = BATCH * CH
TILES = 3
PAIRS = ROWS // (P * TILES)
SOURCES = ((0, 1), (0, 1, 2), (1, 2))
BLOCK = {(s, t): n for n, (s, t) in enumerate((s, t) for t in range(TILES) for s in SOURCES[t])}
GN_EPS, LN_EPS, BN_EPS = 1e-5, 1e-5, 1e-5
NEG_INF = -1e38

F32 = mybir.dt.float32
ALU = mybir.AluOpType
ACT = mybir.ActivationFunctionType


def makers(nc, ctx, prefix):
    return (lambda name, shape: ctx.enter_context(nc.sbuf_tensor(prefix + name, shape, F32)),
            lambda name, shape: ctx.enter_context(nc.psum_tensor(prefix + name, shape, F32)),
            lambda name: ctx.enter_context(nc.semaphore(prefix + name)))


class GroupNorm:

    DVE_STEPS = 12

    def __init__(self, nc, sb, sem, parts):
        self.mix = sb("gn_mix", [P, 7, P])
        self.raw = sb("gn_raw", [P, TILES, 8, 6])
        self.mv = sb("gn_mv", [P, TILES, 2])
        self.group = sb("gn_group", [P, TILES, 2])
        self.mean = sb("gn_mean", [P, TILES])
        self.sq = sb("gn_sq", [P, TILES])
        self.var = sb("gn_var", [P, TILES])
        self.rstd = sb("gn_rstd", [P, TILES])
        self.shift = sb("gn_shift", [P, TILES])
        self.half = sb("gn_half", [P, TILES])
        self.stat, self.mixed, self.powered = sem("gn_stat"), sem("gn_mixed"), sem("gn_powered")

    def statistics(self, dve, i, x, loaded, offset=None):
        n = i * self.DVE_STEPS
        for t in range(TILES):
            loaded(t)
            for j in range(8):
                ins = dve.bn_stats(self.raw[:, t, j, :], x[:, t, j * 512:(j + 1) * 512])
        ins.then_inc(self.stat, 1)
        dve.wait_ge(self.stat, n + 1)
        dve.memset(self.sq[:, :], 0.0)
        for t in range(TILES):
            ins = dve.bn_aggr(self.mv[:, t, :], self.raw[:, t, :, :])
        ins.then_inc(self.stat, 1)
        dve.wait_ge(self.stat, n + 2)
        if offset is None:
            dve.tensor_copy(self.mean[:, :], self.mv[:, :, 0]).then_inc(self.stat, 1)
        else:
            dve.tensor_tensor(self.mean[:, :], self.mv[:, :, 0], offset, ALU.add).then_inc(self.stat, 1)
        dve.wait_ge(self.stat, n + 3)
        dve.tensor_copy(self.mv[:, :, 0], self.mean[:, :]).then_inc(self.stat, 1)
        dve.tensor_tensor(self.sq[:, :], self.mean[:, :], self.mean[:, :], ALU.mult).then_inc(self.stat, 1)
        dve.wait_ge(self.stat, n + 5)
        dve.tensor_tensor(self.mv[:, :, 1], self.mv[:, :, 1], self.sq[:, :], ALU.add).then_inc(self.stat, 1)

    def mix_stats(self, pe, i, bank):
        pe.wait_ge(self.stat, i * self.DVE_STEPS + 6)
        for t in range(TILES):
            for n, s in enumerate(SOURCES[t]):
                ins = pe.matmul(bank[:, 2 * t:2 * t + 2], self.mix[:, BLOCK[s, t], :], self.mv[:, s, :],
                                start=(n == 0), stop=(n == len(SOURCES[t]) - 1))
        ins.then_inc(self.mixed, 1)

    def power(self, pool, i):
        pool.wait_ge(self.stat, i * self.DVE_STEPS + 10)
        pool.tensor_tensor(self.rstd[:, :], self.var[:, :], self.half[:, :], ALU.pow).then_inc(self.powered, 1)

    def scales(self, dve, i, bank, offset=None):
        n = i * self.DVE_STEPS
        dve.wait_ge(self.mixed, i + 1)
        dve.tensor_copy(self.group[:, :, :], bank.rearrange("p (t c) -> p t c", c=2)).then_inc(self.stat, 1)
        dve.wait_ge(self.stat, n + 7)
        dve.tensor_tensor(self.sq[:, :], self.group[:, :, 0], self.group[:, :, 0], ALU.mult).then_inc(self.stat, 1)
        dve.wait_ge(self.stat, n + 8)
        dve.tensor_tensor(self.var[:, :], self.group[:, :, 1], self.sq[:, :], ALU.subtract).then_inc(self.stat, 1)
        dve.wait_ge(self.stat, n + 9)
        dve.tensor_scalar(self.var[:, :], self.var[:, :], 0.0, GN_EPS, ALU.max, ALU.add).then_inc(self.stat, 1)
        if offset is None:
            dve.tensor_scalar(self.sq[:, :], self.group[:, :, 0], -1.0, None, ALU.mult).then_inc(self.stat, 1)
        else:
            dve.tensor_tensor(self.sq[:, :], offset, self.group[:, :, 0], ALU.subtract).then_inc(self.stat, 1)
        dve.wait_ge(self.stat, n + 11)
        dve.wait_ge(self.powered, i + 1)
        dve.tensor_tensor(self.shift[:, :], self.sq[:, :], self.rstd[:, :], ALU.mult).then_inc(self.stat, 1)
        dve.wait_ge(self.stat, n + 12)

    def ready(self, eng, i):
        eng.wait_ge(self.stat, (i + 1) * self.DVE_STEPS)


def convolution_layer(nc, x_in, z_out, bn_out, par, pairs=PAIRS):
    PAD = 2
    SPAN = SIDE + 2 * PAD
    PE_TAPS = 3
    VEC_TAPS = 9 - PE_TAPS
    ROWS_A_JOB = 16
    JOBS = TILES * SIDE // ROWS_A_JOB
    WIDE = ROWS_A_JOB * SIDE
    Z_JOBS = 2 * JOBS
    STATS = 5

    with ExitStack() as ctx:
        sb, ps, sem = makers(nc, ctx, "conv_")
        x = sb("x", [P, TILES, TOKENS])
        padded = sb("padded", [P, TILES, SPAN, SPAN])
        y = sb("y", [P, TILES, TOKENS])
        z = sb("z", [P, 2, TILES, 512])
        gn = GroupNorm(nc, sb, sem, P)
        pointwise = sb("pointwise", [P, 7, P])
        taps = sb("taps", [P, TILES, 9])
        ident = sb("ident", [P, P])
        diagonal = sb("diagonal", [P, TILES, PE_TAPS, P])
        same = sb("same", [P, 9, P])
        affine = sb("affine", [P, 2, TILES])
        raw = sb("raw", [P, TILES, 8, 6])
        mv = sb("mv", [P, TILES, 2])
        total = sb("total", [P, TILES, 2])
        sq = sb("sq", [P, TILES])
        cols = sb("cols", [P, 2, TILES])

        tap_ps = ps("tap_ps", [P, 2, WIDE])
        z_ps = ps("z_ps", [P, 4, 512])

        par_in, prepared, last = sem("par_in"), sem("prepared"), sem("last")
        x_in_s = [sem(f"x_in{t}") for t in range(TILES)]
        relued, taps_made, tapped = sem("relued"), sem("taps_made"), sem("tapped")
        z_made, z_seen, z_copied, z_stat = sem("z_made"), sem("z_seen"), sem("z_copied"), sem("z_stat")
        stored = [sem("stored0"), sem("stored1")]
        bn_stored = sem("bn_stored")

        rows = x_in.rearrange("(q t p) n -> q p t n", p=P, t=TILES)
        z_rows = z_out.rearrange("(q t p) n -> q p t n", p=P, t=TILES)
        loads = [(pointwise, "pointwise", "b p n -> p b n"), (taps, "taps", None), (ident, "ident", None),
                 (same, "same", "b p n -> p b n"), (affine, "affine", None), (gn.mix, "gn_mix", "b p n -> p b n")]
        block = ctx.enter_context(nc.Block())

        def job(j):
            return divmod(j, TILES)

        def shifted(t, first, count, tap):
            dh, dw = divmod(tap, 3)
            return padded[:, t, first + 2 * dh:first + 2 * dh + count, 2 * dw:2 * dw + SIDE]

        @block.sync
        def _(sp):
            for to, name, view in loads:
                sp.dma_start(to.ap(), par[name] if view is None else par[name].rearrange(view)).then_inc(par_in, 16)

            def load_x(i):
                for t in range(TILES):
                    sp.dma_start(x[:, t, :], rows[i, :, t, :]).then_inc(x_in_s[t], 16)

            def store_z(i):
                for n in range(8):
                    sp.wait_ge(z_copied, i * Z_JOBS + 3 * (n + 1))
                    sp.dma_start(z_rows[i, :, :, 512 * n:512 * n + 512], z[:, n % 2, :, :]).then_inc(stored[n % 2], 16)

            load_x(0)
            if pairs > 1:
                with sp.Fori(0, pairs - 1) as i:
                    sp.wait_ge(relued, (i + 1) * 2 * TILES)
                    load_x(i + 1)
                    store_z(i)
            store_z(pairs - 1)
            for s in stored:
                sp.wait_ge(s, pairs * 4 * 16)
            sp.wait_ge(last, 8)
            sp.dma_start(bn_out, cols[:, :, :]).then_inc(bn_stored, 16)
            sp.wait_ge(bn_stored, 16)

        @block.gpsimd
        def _(pool):
            with pool.Fori(0, pairs) as i:
                gn.power(pool, i)
            pool.wait_ge(last, 4)
            pool.tensor_tensor(mv[:, :, 1], mv[:, :, 1], gn.half[:, :], ALU.pow).then_inc(last, 1)

        @block.scalar
        def _(act):
            with act.Fori(0, pairs) as i:
                gn.ready(act, i)
                act.wait_ge(tapped, i * JOBS * VEC_TAPS)
                act.wait_ge(prepared, 1)
                for part in (slice(0, ROWS_A_JOB + PAD), slice(ROWS_A_JOB + PAD, SIDE)):
                    for t in range(TILES):
                        act.activation(padded[:, t, PAD + part.start:PAD + part.stop, PAD:PAD + SIDE],
                                       x[:, t, :].rearrange("p (h w) -> p h w", w=SIDE)[:, part, :],
                                       ACT.Relu, bias=gn.shift[:, t:t + 1], scale=gn.rstd[:, t:t + 1]).then_inc(relued, 1)
                for m in range(Z_JOBS):
                    n, t = divmod(m, TILES)
                    act.wait_ge(z_made, i * Z_JOBS + m + 1)
                    act.wait_ge(z_seen, i * Z_JOBS + max(m - 5, 0))
                    if t == 0:
                        act.wait_ge(stored[n % 2], i * 4 * 16 + 16 * (n // 2))
                    act.activation(z[:, n % 2, t, :], z_ps[:, m % 4, :], ACT.Copy).then_inc(z_copied, 1)

        @block.tensor
        def _(pe):
            pe.wait_ge(par_in, 16 * len(loads))
            pe.wait_ge(prepared, 2)
            def products(i):
                def tap_job(j):
                    b, t = job(j)
                    if b <= 1:
                        pe.wait_ge(relued, (2 * i + b) * TILES + t + 1)
                    pe.wait_ge(tapped, i * JOBS * VEC_TAPS + max(j - 1, 0) * VEC_TAPS)
                    for half in range(2):
                        for tap in range(PE_TAPS):
                            ins = pe.matmul(tap_ps[:, j % 2, 512 * half:512 * half + 512], diagonal[:, t, tap, :],
                                            shifted(t, ROWS_A_JOB * b + 8 * half, 8, tap), start=(tap == 0), stop=(tap == PE_TAPS - 1))
                    ins.then_inc(taps_made, 1)

                def z_job(m):
                    n, t = divmod(m, TILES)
                    pe.wait_ge(tapped, i * JOBS * VEC_TAPS + (n // 2 + 1) * TILES * VEC_TAPS)
                    pe.wait_ge(z_copied, i * Z_JOBS + max(m - 3, 0))
                    for q, s in enumerate(SOURCES[t]):
                        ins = pe.matmul(z_ps[:, m % 4, :], pointwise[:, BLOCK[s, t], :], y[:, s, 512 * n:512 * n + 512],
                                        start=(q == 0), stop=(q == len(SOURCES[t]) - 1))
                    ins.then_inc(z_made, 1)

                tap_job(0)
                for j in range(JOBS + TILES):
                    if j + 1 < JOBS:
                        tap_job(j + 1)
                    if j >= TILES:
                        z_job(2 * (j - TILES))
                        z_job(2 * (j - TILES) + 1)

            mixed_stats = tap_ps[:, 0, 0:2 * TILES]
            gn.mix_stats(pe, 0, mixed_stats)
            if pairs > 1:
                with pe.Fori(0, pairs - 1) as i:
                    products(i)
                    gn.mix_stats(pe, i + 1, mixed_stats)
            products(pairs - 1)
            pe.wait_ge(last, 1)
            for t in range(TILES):
                for s in range(TILES):
                    ins = pe.matmul(z_ps[:, 0, 2 * t:2 * t + 2], same[:, 3 * s + t, :], total[:, s, :],
                                    start=(s == 0), stop=(s == TILES - 1))
            ins.then_inc(last, 1)

        @block.vector
        def _(dve):
            dve.memset(gn.half[:, :], -0.5)
            dve.memset(total[:, :, :], 0.0)
            dve.memset(padded[:, :, :, :], 0.0).then_inc(prepared, 1)
            dve.wait_ge(par_in, 16 * len(loads))
            for t in range(TILES):
                for tap in range(PE_TAPS):
                    ins = dve.tensor_scalar(diagonal[:, t, tap, :], ident[:, :], taps[:, t, tap:tap + 1], None, ALU.mult)
            ins.then_inc(prepared, 1)

            def normalisation(i):
                gn.statistics(dve, i, x, lambda t: dve.wait_ge(x_in_s[t], (i + 1) * 16))
                gn.scales(dve, i, tap_ps[:, 0, 0:2 * TILES])

            def pair(i, following):
                def see(m):
                    n, t = divmod(m, TILES)
                    dve.wait_ge(z_copied, i * Z_JOBS + m + 1)
                    dve.bn_stats(raw[:, t, n, :], z[:, n % 2, t, :]).then_inc(z_seen, 1)

                for j in range(JOBS + TILES):
                    if j < JOBS:
                        b, t = job(j)
                        first = ROWS_A_JOB * b
                        at = y[:, t, first * SIDE:(first + ROWS_A_JOB) * SIDE].rearrange("p (h w) -> p h w", w=SIDE)
                        dve.wait_ge(taps_made, i * JOBS + j + 1)
                        dve.wait_ge(z_made, i * Z_JOBS)
                        for n, tap in enumerate(range(PE_TAPS, 9)):
                            if n:
                                dve.wait_ge(tapped, (i * JOBS + j) * VEC_TAPS + n)
                            so_far = at if n else tap_ps[:, j % 2, :].rearrange("p (h w) -> p h w", w=SIDE)
                            dve.scalar_tensor_tensor(out=at, in0=shifted(t, first, ROWS_A_JOB, tap), scalar=taps[:, t, tap:tap + 1],
                                                     in1=so_far, op0=ALU.mult, op1=ALU.add).then_inc(tapped, 1)
                    if j == JOBS and following is not None:
                        normalisation(following)
                    if j >= TILES:
                        see(2 * (j - TILES))
                        see(2 * (j - TILES) + 1)
                dve.wait_ge(z_seen, (i + 1) * Z_JOBS)
                dve.memset(sq[:, :], 0.0)
                for t in range(TILES):
                    ins = dve.bn_aggr(mv[:, t, :], raw[:, t, :, :])
                ins.then_inc(z_stat, 1)
                dve.wait_ge(z_stat, i * STATS + 1)
                dve.tensor_tensor(sq[:, :], mv[:, :, 0], mv[:, :, 0], ALU.mult).then_inc(z_stat, 1)
                dve.wait_ge(z_stat, i * STATS + 2)
                dve.tensor_tensor(mv[:, :, 1], mv[:, :, 1], sq[:, :], ALU.add).then_inc(z_stat, 1)
                dve.wait_ge(z_stat, i * STATS + 3)
                dve.tensor_tensor(total[:, :, :], total[:, :, :], mv[:, :, :], ALU.add).then_inc(z_stat, 1)
                dve.wait_ge(z_stat, i * STATS + 4)
                dve.tensor_copy(sq[:, :], mv[:, :, 0]).then_inc(z_stat, 1)
            normalisation(0)
            if pairs > 1:
                with dve.Fori(0, pairs - 1) as i:
                    pair(i, i + 1)
            pair(pairs - 1, None)
            dve.wait_ge(z_stat, pairs * STATS)
            dve.tensor_copy(total[:, :, :], total[:, :, :]).then_inc(last, 1)
            dve.wait_ge(last, 2)
            dve.tensor_copy(mv[:, :, :], z_ps[:, 0, 0:2 * TILES].rearrange("p (t c) -> p t c", c=2)).then_inc(z_stat, 1)
            dve.wait_ge(z_stat, pairs * STATS + 1)
            dve.tensor_tensor(sq[:, :], mv[:, :, 0], mv[:, :, 0], ALU.mult).then_inc(last, 1)
            dve.wait_ge(last, 3)
            dve.tensor_tensor(mv[:, :, 1], mv[:, :, 1], sq[:, :], ALU.subtract).then_inc(z_stat, 1)
            dve.wait_ge(z_stat, pairs * STATS + 2)
            dve.tensor_scalar(mv[:, :, 1], mv[:, :, 1], 0.0, BN_EPS, ALU.max, ALU.add).then_inc(last, 1)
            dve.wait_ge(last, 5)
            dve.tensor_tensor(cols[:, 0, :], mv[:, :, 1], affine[:, 0, :], ALU.mult).then_inc(last, 1)
            dve.wait_ge(last, 6)
            dve.tensor_tensor(sq[:, :], mv[:, :, 0], cols[:, 0, :], ALU.mult).then_inc(last, 1)
            dve.wait_ge(last, 7)
            dve.tensor_tensor(cols[:, 1, :], affine[:, 1, :], sq[:, :], ALU.subtract).then_inc(last, 1)


def fourier_layer(nc, x_in, x_out, par, tag, batch_norm=None, pairs=PAIRS):
    G = 16
    C1 = 3 * G
    MIX = 2 * G
    HB = 8
    NB = SIDE // HB
    ROUND = 12582912.0
    TWO_PI = 6.2831850
    FRONT_ACT = dict(conv1=8, forward=8)
    FRONT_VEC = dict(forward=8)
    BACK_ACT = dict(turned=10, phase=4, turned_s=2, inverse=8, final=8)
    BACK_VEC = dict(spatial=2, fourier=2, magnitude=4, inverse=6, final=24)

    def place(jobs, name):
        return sum(list(jobs.values())[:list(jobs).index(name)])

    LUTS, CALCS = 14, 19

    def blocked(plane):
        return plane.rearrange("p c h -> p (c h)").rearrange("p (b c r) -> p c b r", b=NB, c=G)

    def by_block(plane):
        return plane.rearrange("p c (b r) -> p c b r", b=NB)

    def block_of(plane, b):
        return plane.rearrange("p c h -> p (c h)")[:, b * P:(b + 1) * P]

    with ExitStack() as ctx:
        sb, ps, sem = makers(nc, ctx, tag)
        x = sb("x", [P, TILES, TOKENS])
        z = sb("z", [P, TOKENS]) if batch_norm else None
        planes = sb("planes", [P, 3 * 4096])
        flat = planes[:, :]
        field = flat[:, 0:4096].rearrange("p (r c h) -> p r c h", r=2, c=MIX)
        w0, w1 = (flat[:, 4096 + 2048 * j:6144 + 2048 * j].rearrange("p (c h) -> p c h", c=MIX) for j in range(2))
        cat_t = flat[:, 8192:12288]
        mixed_in = cat_t.rearrange("p (z b n) -> p z b n", z=4, b=NB)
        first = sb("first", [P, C1, SIDE])
        saved = sb("saved", [P, G, SIDE])
        cat = sb("cat", [P, 64, SIDE])
        again = sb("again", [P, 2, TILES, 512])
        half_way = sb("half_way", [P, MIX // 2, 256])
        halves = half_way[:, :, :].rearrange("p a n -> p (a n)")
        w2, w3 = (halves[:, 2048 * j:2048 * j + 2048].rearrange("p (c h) -> p c h", c=MIX) for j in range(2))
        spatial_in = sb("spatial_in", [P, NB, P + 2])

        gn = GroupNorm(nc, sb, sem, P)
        trans = sb("trans", [P, 5, 2, 256])
        FRFT, FFT, IFRFT, IFFT_W, IFFT_H = range(5)
        conv1 = sb("conv1", [P, TILES, C1])
        mixers = sb("mixers", [P, 4, P])
        MAG_F, MAG, PHA, CONV_1 = range(4)
        spatial = sb("spatial", [P, 9, P])
        ident = sb("ident", [P, P])
        conv2 = sb("conv2", [P, 2 * CH])
        conv0 = sb("conv0", [2 * G, P])
        conv2_0 = sb("conv2_0", [2 * G, 2 * CH])
        bias0 = sb("bias0", [2 * G, 1])
        rows_in = sb("rows_in", [P, 6, G])
        mask = sb("mask", [P, SIDE])
        bias_map = sb("bias_map", [P, G, SIDE])
        turn_bias = sb("turn_bias", [P, MIX])
        out_bias = sb("out_bias", [P, TILES])
        quarter = sb("quarter", [P, 1])
        zero = sb("zero", [P, 1])
        bn_cols = sb("bn_cols", [P, 2, TILES])

        front_act_ps = ps("front_act_ps", [P, 2, 512])
        front_vec_ps = ps("front_vec_ps", [P, 2, 512])
        back_act_ps = ps("back_act_ps", [P, 2, 512])
        back_vec_ps = ps("back_vec_ps", [P, 2, 512])

        par_in, prepared, bias_steps = sem("par_in"), sem("prepared"), sem("bias_steps")
        x_in_s = [sem(f"x_in{t}") for t in range(TILES)]
        z_in, based, normed, first_kept = sem("z_in"), sem("based"), sem("normed"), sem("first_kept")
        first_saved, rest_normed = sem("first_saved"), sem("rest_normed")
        base_stored = [sem(f"base_stored{t}") for t in range(TILES)]
        front_act_made, front_act_read = sem("front_act_made"), sem("front_act_read")
        front_vec_made, front_vec_read = sem("front_vec_made"), sem("front_vec_read")
        back_act_made, back_act_read = sem("back_act_made"), sem("back_act_read")
        back_vec_made, back_vec_read = sem("back_vec_made"), sem("back_vec_read")
        lut, calc = sem("lut"), sem("calc")
        again_in = [sem("again_in0"), sem("again_in1")]
        stored = [sem("stored0"), sem("stored1")]

        src = x_in.rearrange("(q t p) n -> q p t n", p=P, t=TILES)
        dst = x_out.rearrange("(q t p) n -> q p t n", p=P, t=TILES)
        loads = [
            (trans, "trans", "f p r n -> p f r n"), (mixers, "mixers", "b p n -> p b n"),
            (spatial, "spatial", "b p n -> p b n"), (ident, "ident", None), (conv2, "conv2_rest", None),
            (conv1, "conv1", "t p n -> p t n"), (conv0, "conv0", None), (conv2_0, "conv2_0", None),
            (bias0, "bias0", None), (rows_in, "rows", None), (mask, "mask", None), (gn.mix, "gn_mix", "b p n -> p b n")]
        if batch_norm:
            z_rows = batch_norm[0].rearrange("(q t p) n -> q p t n", p=P, t=TILES)
            loads.append((bn_cols, "bn_cols", None))
        N_LOADS = len(loads)
        residual = dst if batch_norm else src
        MAG_S_B, MAG_F_B, MAG_B, CONV_1_B, PHA_B, CONV_1_B2 = range(6)

        block = ctx.enter_context(nc.Block())

        class Ring:

            def __init__(self, banks, jobs, made, read):
                self.banks, self.jobs, self.made, self.read = banks, jobs, made, read
                self.total = sum(jobs.values())

            def after(self, i, name, j=0):
                return i * self.total + place(self.jobs, name) + j

            def end(self, i, name):
                return self.after(i, name, self.jobs[name])

            def to_write(self, i, name, j):
                m = place(self.jobs, name) + j
                nc.tensor.wait_ge(self.read, i * self.total + max(m - 1, 0))
                return self.banks[:, m % 2, :]

            def to_read(self, eng, i, name, j):
                m = place(self.jobs, name) + j
                eng.wait_ge(self.made, i * self.total + m + 1)
                return self.banks[:, m % 2, :]

        front_act = Ring(front_act_ps, FRONT_ACT, front_act_made, front_act_read)
        front_vec = Ring(front_vec_ps, FRONT_VEC, front_vec_made, front_vec_read)
        back_act = Ring(back_act_ps, BACK_ACT, back_act_made, back_act_read)
        back_vec = Ring(back_vec_ps, BACK_VEC, back_vec_made, back_vec_read)

        @block.sync
        def _(sp):
            for to, name, view in loads:
                here = par[name] if view is None else par[name].rearrange(view)
                sp.dma_start(to.ap(), here).then_inc(par_in, 16)

            def load_x(i):
                for t in range(TILES):
                    sp.dma_start(x[:, t, :], src[i, :, t, :]).then_inc(x_in_s[t], 16)
                    if t == 0 and batch_norm:
                        sp.wait_ge(based, i * TILES)
                        sp.dma_start(z[:, :], z_rows[i, :, 0, :]).then_inc(z_in, 16)

            def bases(i):
                for t in range(1, TILES):
                    sp.wait_ge(based, i * TILES + t)
                    sp.dma_start(z[:, :], z_rows[i, :, t, :]).then_inc(z_in, 16)
                    sp.dma_start(dst[i, :, t - 1, :], x[:, t - 1, :]).then_inc(base_stored[t - 1], 16)
                sp.wait_ge(based, i * TILES + TILES)
                sp.dma_start(dst[i, :, TILES - 1, :], x[:, TILES - 1, :]).then_inc(base_stored[TILES - 1], 16)
                for s in base_stored:
                    sp.wait_ge(s, (i + 1) * 16)

            def load_again(i, j):
                sp.wait_ge(stored[j % 2], i * 4 * 16 + 16 * (j // 2))
                sp.dma_start(again[:, j % 2, :, :], residual[i, :, :, 512 * j:512 * j + 512]).then_inc(again_in[j % 2], 16)

            def final_traffic(i):
                load_again(i, 0)
                load_again(i, 1)
                for j in range(8):
                    sp.wait_ge(back_vec_read, back_vec.after(i, "final", 3 * (j + 1)))
                    sp.dma_start(dst[i, :, :, 512 * j:512 * j + 512], again[:, j % 2, :, :]).then_inc(stored[j % 2], 16)
                    if j + 2 < 8:
                        load_again(i, j + 2)

            def load_next(i):
                sp.wait_ge(front_act_made, front_act.end(i - 1, "conv1"))
                load_x(i)

            load_x(0)
            if batch_norm:
                bases(0)
            if pairs > 1:
                load_next(1)
                if batch_norm:
                    bases(1)
            if pairs > 2:
                with sp.Fori(0, pairs - 2) as i:
                    load_next(i + 2)
                    if batch_norm:
                        bases(i + 2)
                    final_traffic(i)
            if pairs > 1:
                final_traffic(pairs - 2)
            final_traffic(pairs - 1)
            for s in stored:
                sp.wait_ge(s, pairs * 4 * 16)

        @block.gpsimd
        def _(pool):
            def save_first(i):
                pool.wait_ge(first_kept, i)
                pool.wait_ge(front_act_read, front_act.end(i, "conv1"))
                pool.tensor_tensor(saved[:, :, :], first[:, 0:G, :], zeros, ALU.add).then_inc(first_saved, 1)

            def keep_first(i):
                pool.wait_ge(back_act_made, back_act.after(i, "turned"))
                pool.wait_ge(first_saved, i + 1)
                pool.tensor_tensor(cat[:, 0:G, :], saved[:, :, :], zeros, ALU.add).then_inc(first_kept, 1)

            zeros = zero[:, :].unsqueeze(2).to_broadcast([P, G, SIDE])
            pool.wait_ge(prepared, 3)
            gn.power(pool, 0)
            save_first(0)
            keep_first(0)
            if pairs > 1:
                gn.power(pool, 1)
            if pairs > 2:
                with pool.Fori(0, pairs - 2) as i:
                    save_first(i + 1)
                    gn.power(pool, i + 2)
                    keep_first(i + 1)
            if pairs > 1:
                save_first(pairs - 1)
                keep_first(pairs - 1)

        @block.scalar
        def _(act):
            def read(ring, i, name, j, out, view=lambda b: b, **kw):
                act.activation(out, view(ring.to_read(act, i, name, j)), ACT.Copy, **kw).then_inc(ring.read, 1)

            def step(*args, **kw):
                act.activation(*args, **kw).then_inc(lut, 1)

            def normalise(i):
                gn.ready(act, i)
                if batch_norm:
                    act.wait_ge(base_stored[0], (i + 1) * 16)
                act.activation(x[:, 0, :], x[:, 0, :], ACT.Identity, bias=gn.shift[:, 0:1], scale=gn.rstd[:, 0:1])\
                    .then_inc(normed, 1)

            def conv1_read(i, j):
                if j == 0:
                    act.wait_ge(front_act_made, front_act.after(i, "conv1"))
                    act.wait_ge(first_saved, i)
                read(front_act, i, "conv1", j, first[:, :, 8 * j:8 * j + 8].rearrange("p c h -> p h c"),
                     view=lambda b: b.rearrange("p (h c) -> p h c", c=64)[:, :, 0:C1])

            def to_half_way(ring, i, name, j):
                read(ring, i, name, j, half_way[:, 2 * j:2 * j + 2, :].rearrange("p a n -> p (a n)"))

            def forward_reads(i):
                for j in range(8):
                    to_half_way(front_act, i, "forward", j)

            def polar(i, between):
                act.wait_ge(front_vec_read, front_vec.end(i, "forward"))
                step(w0, field[:, 0], ACT.Square)
                step(w1, field[:, 1], ACT.Square)
                between(0)
                act.wait_ge(calc, i * CALCS + 1)
                step(w1, w0, ACT.Sqrt)
                act.wait_ge(lut, i * LUTS + 3)
                step(w0, field[:, 0], ACT.Abs)
                between(1)
                act.preload_act_table_set("natural_log_exp_and_others")
                act.wait_ge(calc, i * CALCS + 2)
                step(w3, w0, ACT.Ln)
                act.wait_ge(lut, i * LUTS + 5)
                step(w3, w3, ACT.Exp, scale=-1.0)
                between(2)
                act.wait_ge(calc, i * CALCS + 5)
                step(w2, w0, ACT.Arctan)
                between(3)
                act.wait_ge(calc, i * CALCS + 10)
                step(blocked(w2[:, 0:G]), by_block(w1[:, G:MIX]), ACT.Copy)

            def back(i):
                for plane in range(5):
                    for half in range(2):
                        if plane == 0:
                            read(back_act, i, "turned", half, spatial_in[:, 4 * half:4 * half + 4, 1:P + 1],
                                 view=lambda b: b.rearrange("p (b w) -> p b w", b=4))
                        else:
                            if plane == 1 and half == 0:
                                act.wait_ge(back_vec_made, back_vec.after(i, "spatial"))
                            read(back_act, i, "turned", 2 * plane + half, mixed_in[:, plane - 1, 4 * half:4 * half + 4, :]
                                 .rearrange("p b n -> p (b n)"))
                for j in range(4):
                    g, half = divmod(j, 2)
                    read(back_act, i, "phase", j, w3[:, G * g:G * g + G, 32 * half:32 * half + 32],
                         view=lambda b: b.rearrange("p (o h) -> p o h", h=32), scale=1.0 / math.pi)
                act.wait_ge(calc, i * CALCS + 15)
                step(field[:, 0], w3, ACT.Abs)
                step(field[:, 1], w3, ACT.Sin, scale=TWO_PI)
                act.wait_ge(lut, i * LUTS + 9)
                step(field[:, 0], field[:, 0], ACT.Sin, scale=-TWO_PI, bias=quarter[:, 0:1])
                act.wait_ge(back_vec_read, back_vec.end(i, "fourier"))
                for half in range(2):
                    read(back_act, i, "turned_s", half, mixed_in[:, 0, 4 * half:4 * half + 4, :].rearrange("p b n -> p (b n)"))
                for j in range(8):
                    to_half_way(back_act, i, "inverse", j)
                act.wait_ge(back_vec_read, back_vec.after(i, "inverse", 4))
                step(w0[:, 0:G], field[:, 0, 0:G], ACT.Square)
                step(w1[:, 0:G], field[:, 1, 0:G], ACT.Square)
                act.wait_ge(calc, i * CALCS + CALCS)
                step(cat[:, G:2 * G, :], w0[:, 0:G], ACT.Sqrt)

            def final_read(i, j):
                read(back_act, i, "final", j, cat_t[:, 512 * j:512 * j + 512])

            def turn_over(i, following, ahead):
                if i is not None:
                    act.wait_ge(back_vec_made, back_vec.end(i, "inverse"))
                forward_reads(following)

                def reads(finals, conv1s):
                    for j in range(8):
                        if j in conv1s and ahead is not None:
                            conv1_read(ahead, j)
                        if j + 2 in finals and i is not None:
                            final_read(i, j + 2)

                def between(n):
                    if n == 0 and i is not None:
                        final_read(i, 0)
                        final_read(i, 1)
                    elif n == 1:
                        if ahead is not None:
                            normalise(ahead)
                    elif n == 2:
                        reads((2, 3, 4), (0, 1, 2))
                    elif n == 3:
                        reads((5, 6, 7), (3, 4, 5))

                polar(following, between)
                reads((), (6, 7))

            act.wait_ge(prepared, 2)
            normalise(0)
            for j in range(8):
                conv1_read(0, j)
            turn_over(None, 0, 1 if pairs > 1 else None)
            if pairs > 2:
                with act.Fori(0, pairs - 2) as i:
                    back(i)
                    turn_over(i, i + 1, i + 2)
            if pairs > 1:
                back(pairs - 2)
                turn_over(pairs - 2, pairs - 1, None)
            back(pairs - 1)
            for j in range(8):
                final_read(pairs - 1, j)

        @block.tensor
        def _(pe):
            pe.wait_ge(par_in, 16 * N_LOADS)
            pe.matmul(back_vec_ps[:, 0, 0:2 * CH], conv0[:, :], conv2_0[:, :], start=True, stop=True)
            for t in range(TILES):
                ins = pe.matmul(back_vec_ps[:, 1, t:t + 1], conv2_0[:, t * P:t * P + P], bias0[:, :], start=True, stop=True)
            ins.then_inc(prepared, 1)
            pe.wait_ge(prepared, 3)

            def statistics(i):
                pe.wait_ge(front_vec_read, front_vec.after(i, "forward"))
                gn.mix_stats(pe, i, front_vec_ps[:, 0, 0:2 * TILES])

            def conv1_products(i, j):
                if j == 0:
                    pe.wait_ge(normed, i + 1)
                    pe.wait_ge(rest_normed, (i + 1) * 2)
                bank = front_act.to_write(i, "conv1", j)
                for r in range(8):
                    at = slice((8 * j + r) * SIDE, (8 * j + r + 1) * SIDE)
                    out = bank[:, 64 * r:64 * r + C1]
                    pe.matmul(out[0:64], x[:, 0, at], conv1[:, 0, :], start=True, stop=False)
                    pe.matmul(out[0:64], x[0:64, 1, at], conv1[0:64, 1, :], start=False, stop=True)
                    pe.matmul(out[64:128], x[:, 2, at], conv1[:, 2, :], start=True, stop=False)
                    ins = pe.matmul(out[64:128], x[64:128, 1, at], conv1[64:128, 1, :], start=False, stop=True)
                ins.then_inc(front_act_made, 1)

            def forward(i):
                pe.wait_ge(front_act_read, front_act.end(i, "conv1"))
                for j in range(8):
                    bank = front_act.to_write(i, "forward", j)
                    for a in range(2):
                        c = G + 4 * j + 2 * a
                        ins = pe.matmul(bank[:, 256 * a:256 * a + 256], first[:, c:c + 2, :],
                                        trans[:, FRFT if j < 4 else FFT, 0, :], start=True, stop=True)
                    ins.then_inc(front_act_made, 1)
                for j in range(8):
                    pe.wait_ge(front_act_read, front_act.after(i, "forward", j + 1))
                    bank = front_vec.to_write(i, "forward", j)
                    for a in range(2):
                        for r in range(2):
                            ins = pe.matmul(bank[:, 256 * a:256 * a + 256], half_way[:, 2 * j + a, P * r:P * r + P],
                                            trans[:, FRFT if j < 4 else FFT, r, :], start=(r == 0), stop=(r == 1))
                    ins.then_inc(front_vec_made, 1)

            def turn(i, name, j, plane, half):
                bank = back_act.to_write(i, name, j)
                for b in range(4):
                    ins = pe.matmul(bank[:, P * b:P * b + P], block_of(plane, 4 * half + b), ident[:, :], start=True, stop=True)
                ins.then_inc(back_act_made, 1)

            def mix(bank, source, w, half, made):
                bank = bank.rearrange("p (o h) -> p o h", h=32)
                for b in range(4):
                    ins = pe.matmul(bank[:, :, HB * b:HB * b + HB], mixed_in[:, source, 4 * half + b, :], mixers[:, w, :],
                                    start=True, stop=True)
                ins.then_inc(made, 1)

            def mixing(i):
                pe.wait_ge(calc, i * CALCS + 12)
                pe.wait_ge(lut, i * LUTS + 8)
                for n, plane in enumerate((w0[:, 0:G], w0[:, G:MIX], w3[:, 0:G], w2[:, 0:G], w3[:, G:MIX])):
                    for half in range(2):
                        turn(i, "turned", 2 * n + half, plane, half)
                pe.wait_ge(back_act_read, back_act.after(i, "turned", 4))
                for half in range(2):
                    bank = back_vec.to_write(i, "spatial", half).rearrange("p (o h) -> p o h", h=32)
                    for b in range(4):
                        q = 4 * half + b
                        terms = [(dw, n, q + n - 1) for dw in range(3) for n in range(3) if 0 <= q + n - 1 < NB]
                        for dw, n, from_q in terms:
                            ins = pe.matmul(bank[:, :, HB * b:HB * b + HB], spatial_in[:, from_q, dw:dw + P],
                                            spatial[:, 3 * dw + n, :], start=((dw, n, from_q) == terms[0]),
                                            stop=((dw, n, from_q) == terms[-1]))
                    ins.then_inc(back_vec_made, 1)
                    if half == 0:
                        pe.wait_ge(back_act_read, back_act.end(i, "turned"))
                        for j in range(4):
                            mix(back_act.to_write(i, "phase", j), (1, 3)[j // 2], (PHA, CONV_1)[j // 2], j % 2, back_act_made)
                for half in range(2):
                    mix(back_vec.to_write(i, "fourier", half), 0, MAG_F, half, back_vec_made)
                pe.wait_ge(calc, i * CALCS + 16)
                for half in range(2):
                    turn(i, "turned_s", half, w2[:, G:MIX], half)
                pe.wait_ge(back_act_read, back_act.end(i, "turned_s"))
                for j in range(4):
                    mix(back_vec.to_write(i, "magnitude", j), (0, 2)[j // 2], (MAG, CONV_1)[j // 2], j % 2, back_vec_made)

            def inverse(i):
                for j in range(8):
                    pe.wait_ge(calc, i * CALCS + 17 + j // 4)
                    bank = back_act.to_write(i, "inverse", j)
                    for a in range(2):
                        c = 4 * j + 2 * a
                        for r in range(2):
                            ins = pe.matmul(bank[:, 256 * a:256 * a + 256], field[:, r, c:c + 2, :],
                                            trans[:, IFRFT if j < 4 else IFFT_W, r, :], start=(r == 0), stop=(r == 1))
                    ins.then_inc(back_act_made, 1)
                for j in range(6):
                    n = 2 * (j + 1) if j < 4 else 8 + 4 * (j - 3)
                    pe.wait_ge(back_act_read, back_act.after(i, "inverse", n // 2))
                    bank = back_vec.to_write(i, "inverse", j)
                    per = 2 if j < 4 else 4
                    width = 512 // per
                    for a in range(per):
                        for r in range(2):
                            ins = pe.matmul(bank[:, width * a:width * a + width], half_way[:, n - per + a, P * r:P * r + P],
                                            trans[:, IFRFT if j < 4 else IFFT_H, r, 0:width], start=(r == 0), stop=(r == 1))
                    ins.then_inc(back_vec_made, 1)

            def final(i, ahead):
                pe.wait_ge(lut, i * LUTS + LUTS)
                pe.wait_ge(first_kept, i + 1)
                pe.wait_ge(back_vec_read, back_vec.end(i, "inverse"))
                for j in range(9):
                    if j == 1 and ahead is not None:
                        statistics(ahead)
                    if j < 8:
                        bank = back_act.to_write(i, "final", j)
                        for r in range(8):
                            for im in (slice(0, 64), slice(64, 128)):
                                ins = pe.matmul(bank[im, 64 * r:64 * r + 64], cat[:, :, 8 * j + r], ident[:, im],
                                                start=True, stop=True)
                        ins.then_inc(back_act_made, 1)
                    if j:
                        pe.wait_ge(back_act_read, back_act.after(i, "final", j))
                        for t in range(TILES):
                            pe.matmul(back_vec.to_write(i, "final", 3 * (j - 1) + t), conv2[:, t * P:t * P + P],
                                      cat_t[:, 512 * (j - 1):512 * j], start=True, stop=True).then_inc(back_vec_made, 1)
                        if ahead is not None:
                            conv1_products(ahead, j - 1)

            statistics(0)
            for j in range(8):
                conv1_products(0, j)
            forward(0)
            if pairs > 1:
                statistics(1)
                for j in range(8):
                    conv1_products(1, j)
            if pairs > 2:
                with pe.Fori(0, pairs - 2) as i:
                    mixing(i)
                    inverse(i)
                    forward(i + 1)
                    final(i, i + 2)
            if pairs > 1:
                mixing(pairs - 2)
                inverse(pairs - 2)
                forward(pairs - 1)
                final(pairs - 2, None)
            mixing(pairs - 1)
            inverse(pairs - 1)
            final(pairs - 1, None)

        @block.vector
        def _(dve):
            dve.memset(gn.half[:, :], -0.5)
            dve.memset(zero[:, :], 0.0)
            dve.memset(quarter[:, :], math.pi / 2)
            dve.memset(spatial_in[:, :, :], 0.0)
            dve.memset(cat[:, :, :], 0.0)
            dve.wait_ge(par_in, 16 * N_LOADS)
            by_channel = lambda r: rows_in[:, r, :].unsqueeze(2).to_broadcast([P, G, SIDE])
            by_row = mask[:, :].unsqueeze(1).to_broadcast([P, G, SIDE])
            dve.tensor_scalar(turn_bias[:, :], rows_in[:, PHA_B:PHA_B + 2, :].rearrange("p a c -> p (a c)"),
                              1.0 / (2 * math.pi), None, ALU.mult)
            dve.tensor_tensor(bias_map[:, :, :], by_channel(MAG_S_B), by_row, ALU.mult).then_inc(bias_steps, 1)
            dve.tensor_tensor(w2[:, 0:G], by_channel(MAG_F_B), by_row, ALU.mult).then_inc(bias_steps, 1)
            dve.wait_ge(bias_steps, 2)
            dve.tensor_tensor(w2[:, 0:G], by_channel(MAG_F_B), w2[:, 0:G], ALU.subtract).then_inc(bias_steps, 1)
            dve.wait_ge(bias_steps, 3)
            dve.tensor_tensor(bias_map[:, :, :], bias_map[:, :, :], w2[:, 0:G], ALU.add).then_inc(bias_steps, 1)
            dve.wait_ge(prepared, 1)
            if batch_norm:
                dve.tensor_tensor(out_bias[:, :], back_vec_ps[:, 1, 0:TILES], bn_cols[:, 1, :], ALU.add).then_inc(prepared, 1)
            else:
                dve.tensor_copy(out_bias[:, :], back_vec_ps[:, 1, 0:TILES]).then_inc(prepared, 1)
            dve.wait_ge(bias_steps, 4)
            dve.tensor_tensor(conv2[:, :], back_vec_ps[:, 0, 0:2 * CH], conv2[:, :], ALU.add).then_inc(prepared, 1)
            dve.wait_ge(prepared, 3)
            re, im = field[:, 0], field[:, 1]

            def statistics(i, between=lambda t: None):
                def base(t):
                    between(t)
                    dve.wait_ge(x_in_s[t], (i + 1) * 16)
                    if batch_norm:
                        dve.wait_ge(z_in, (i * TILES + t + 1) * 16)
                        dve.scalar_tensor_tensor(out=x[:, t, :], in0=z[:, :], scalar=bn_cols[:, 0, t:t + 1],
                                                 in1=x[:, t, :], op0=ALU.mult, op1=ALU.add).then_inc(based, 1)
                        dve.wait_ge(based, i * TILES + t + 1)

                gn.statistics(dve, i, x, base, bn_cols[:, 1, :] if batch_norm else None)

            def normalise(i):
                gn.scales(dve, i, front_vec_ps[:, 0, 0:2 * TILES], bn_cols[:, 1, :] if batch_norm else None)
                for t in (1, 2):
                    if batch_norm:
                        dve.wait_ge(base_stored[t], (i + 1) * 16)
                    dve.tensor_scalar(x[:, t, :], x[:, t, :], gn.rstd[:, t:t + 1], gn.shift[:, t:t + 1],
                                      ALU.mult, ALU.add).then_inc(rest_normed, 1)

            def planes_of(bank):
                return bank.rearrange("p (a r n) -> p r a n", a=2, r=2)

            def field_of(j):
                return field[:, :, 4 * j:4 * j + 4, :].rearrange("p r (a c) h -> p r a (c h)", a=2)

            def forward_reads(i):
                for j in range(8):
                    dve.tensor_copy(field_of(j), planes_of(front_vec.to_read(dve, i, "forward", j))).then_inc(front_vec_read, 1)

            def polar(i, between):
                def after(n):
                    dve.wait_ge(calc, i * CALCS + n)

                between(0)
                dve.wait_ge(lut, i * LUTS + 2)
                dve.tensor_tensor(w0, w0, w1, ALU.add).then_inc(calc, 1)
                between(1)
                dve.wait_ge(lut, i * LUTS + 4)
                dve.scalar_tensor_tensor(out=w0, in0=w0, scalar=1e-30, in1=w1, op0=ALU.max, op1=ALU.add).then_inc(calc, 1)
                between(2)
                dve.wait_ge(lut, i * LUTS + 6)
                dve.tensor_tensor(w0, w0, w3, ALU.mult).then_inc(calc, 1)
                between(3)
                after(3)
                dve.scalar_tensor_tensor(out=w0, in0=w0, scalar=-2.0, in1=w3, op0=ALU.add, op1=ALU.mult).then_inc(calc, 1)
                between(4)
                after(4)
                dve.scalar_tensor_tensor(out=w0, in0=w0, scalar=-1.0, in1=im, op0=ALU.mult, op1=ALU.mult).then_inc(calc, 1)
                dve.tensor_scalar(w3, re, 0.0, None, ALU.is_lt).then_inc(calc, 1)
                between(5)
                dve.wait_ge(lut, i * LUTS + 7)
                dve.tensor_scalar(w0, im, 0.0, math.pi, ALU.is_ge, ALU.mult).then_inc(calc, 1)
                after(7)
                dve.scalar_tensor_tensor(out=w0, in0=w2, scalar=-2.0, in1=w0, op0=ALU.mult, op1=ALU.add).then_inc(calc, 1)
                between(6)
                after(8)
                dve.scalar_tensor_tensor(out=w0, in0=w0, scalar=-math.pi / 2, in1=w3, op0=ALU.add, op1=ALU.mult).then_inc(calc, 1)
                after(9)
                for g in (0, G):
                    ins = dve.tensor_tensor(blocked(w3[:, g:g + G]), by_block(w2[:, g:g + G]), by_block(w0[:, g:g + G]), ALU.add)
                ins.then_inc(calc, 1)
                between(7)
                after(10)
                dve.tensor_tensor(blocked(w0[:, 0:G]), by_block(w1[:, 0:G]), by_block(by_row), ALU.mult).then_inc(calc, 1)
                after(11)
                dve.tensor_tensor(blocked(w0[:, G:MIX]), by_block(w1[:, 0:G]), blocked(w0[:, 0:G]), ALU.subtract).then_inc(calc, 1)
                between(8)

            def back(i):
                def after(n):
                    dve.wait_ge(calc, i * CALCS + n)

                dve.wait_ge(back_act_read, back_act.end(i, "phase"))
                dve.tensor_tensor(w3, w3, turn_bias[:, :].unsqueeze(2).to_broadcast([P, MIX, SIDE]), ALU.add).then_inc(calc, 1)
                after(13)
                dve.tensor_scalar(re, w3, ROUND, -ROUND, ALU.add, ALU.add).then_inc(calc, 1)
                after(14)
                dve.tensor_tensor(w3, w3, re, ALU.subtract).then_inc(calc, 1)
                dve.wait_ge(back_act_read, back_act.after(i, "turned", 4))
                for half in range(2):
                    rows = slice(32 * half, 32 * half + 32)
                    dve.tensor_tensor(w0[:, 0:G, rows], back_vec.to_read(dve, i, "spatial", half).rearrange("p (o h) -> p o h", h=32),
                                      by_row[:, :, rows], ALU.mult).then_inc(back_vec_read, 1)
                for half in range(2):
                    rows = slice(32 * half, 32 * half + 32)
                    dve.wait_ge(back_vec_read, back_vec.after(i, "spatial", half + 1))
                    dve.tensor_tensor(w0[:, 0:G, rows], back_vec.to_read(dve, i, "fourier", half).rearrange("p (o h) -> p o h", h=32),
                                      w0[:, 0:G, rows], ALU.add).then_inc(back_vec_read, 1)
                dve.wait_ge(back_vec_read, back_vec.end(i, "fourier"))
                dve.wait_ge(back_act_read, back_act.end(i, "turned"))
                dve.tensor_tensor(blocked(w2[:, G:MIX]), by_block(w0[:, 0:G]), by_block(bias_map[:, :, :]), ALU.add).then_inc(calc, 1)
                for g in range(2):
                    group = slice(G * g, G * g + G)
                    for half in range(2):
                        bias = rows_in[:, MAG_B + g, :].unsqueeze(2).to_broadcast([P, G, 32])
                        dve.tensor_tensor(w1[:, group, 32 * half:32 * half + 32],
                                          back_vec.to_read(dve, i, "magnitude", 2 * g + half).rearrange("p (o h) -> p o h", h=32),
                                          bias, ALU.add).then_inc(back_vec_read, 1)
                    dve.wait_ge(back_vec_read, back_vec.after(i, "magnitude", 2 * g + 2))
                    dve.wait_ge(lut, i * LUTS + 11)
                    dve.tensor_tensor(re[:, group], w1[:, group], re[:, group], ALU.mult)
                    dve.tensor_tensor(im[:, group], w1[:, group], im[:, group], ALU.mult).then_inc(calc, 1)

            def inverse_reads(i):
                for j in range(4):
                    dve.tensor_copy(field_of(j), planes_of(back_vec.to_read(dve, i, "inverse", j))).then_inc(back_vec_read, 1)
                for j in range(4, 6):
                    c = 2 * G + 8 * (j - 4)
                    dve.tensor_copy(cat[:, c:c + 8, :].rearrange("p c h -> p (c h)"), back_vec.to_read(dve, i, "inverse", j))\
                        .then_inc(back_vec_read, 1)
                dve.wait_ge(lut, i * LUTS + 13)
                dve.tensor_tensor(w0[:, 0:G], w0[:, 0:G], w1[:, 0:G], ALU.add).then_inc(calc, 1)

            def results(i, ms):
                for m in ms:
                    j, t = divmod(m, TILES)
                    if t == 0:
                        dve.wait_ge(again_in[j % 2], i * 4 * 16 + 16 * (j // 2 + 1))
                    dve.scalar_tensor_tensor(out=again[:, j % 2, t, :], in0=back_vec.to_read(dve, i, "final", m),
                                             scalar=out_bias[:, t:t + 1], in1=again[:, j % 2, t, :],
                                             op0=ALU.add, op1=ALU.add).then_inc(back_vec_read, 1)

            RESULT_STEPS = (0, 0, 3, 6, 9, 12, 15, 18, 21, 24)

            def turn_over(i, following, ahead):
                inverse_at, forward_at = (1, 2) if batch_norm else (2, 3)

                def before_tile(t):
                    if t == inverse_at and i is not None:
                        inverse_reads(i)
                    if t == forward_at:
                        forward_reads(following)

                def between(n):
                    if n == 1 and ahead is not None:
                        normalise(ahead)
                    if i is not None:
                        results(i, range(RESULT_STEPS[n], RESULT_STEPS[n + 1]))

                if ahead is not None:
                    statistics(ahead, before_tile)
                    before_tile(TILES)
                else:
                    for t in range(TILES + 1):
                        before_tile(t)
                polar(following, between)

            statistics(0)
            normalise(0)
            turn_over(None, 0, 1 if pairs > 1 else None)
            if pairs > 2:
                with dve.Fori(0, pairs - 2) as i:
                    back(i)
                    turn_over(i, i + 1, i + 2)
            if pairs > 1:
                back(pairs - 2)
                turn_over(pairs - 2, pairs - 1, None)
            back(pairs - 1)
            inverse_reads(pairs - 1)
            results(pairs - 1, range(8 * TILES))

def wkv_layer(nc, x_in, x_out, par, pairs=PAIRS):
    T = 512
    STEPS = TOKENS // T
    UNITS = TILES * STEPS * 2
    BLOCKS = TILES * STEPS
    ORDER = [b for s in range(STEPS // 2) for b in (s, STEPS - 1 - s)]
    GATES = ORDER[::-1]
    JOBS = 3 * STEPS
    BANKS = 4
    SLOTS = STEPS + 2
    FRAME = 5
    FINAL_UNITS = FRAME * STEPS + 3

    def unit(u):
        t, s, d = u // (2 * STEPS), u // 2 % STEPS, u % 2
        return t, s, d, (s if d == 0 else STEPS - 1 - s)

    def second(u):
        return unit(u)[1] >= STEPS // 2

    def seconds(u):
        t, r = divmod(u, 2 * STEPS)
        return t * STEPS + max(r - STEPS, 0)

    def folds(u):
        return u + seconds(u)

    def kv_job(t, b, which):
        return t * JOBS + ORDER.index(b) * 2 + which

    def gate_job(t, n):
        return t * JOBS + 2 * STEPS + n

    def last_visit(t, b):
        s, d = (b, 0) if b >= STEPS // 2 else (STEPS - 1 - b, 1)
        return (t * STEPS + s) * 2 + d

    def slot_of(t, b):
        n = t * STEPS + ORDER.index(b)
        return n % SLOTS, n // SLOTS, len(range(n % SLOTS, BLOCKS, SLOTS))

    with ExitStack() as ctx:
        sb, ps, sem = makers(nc, ctx, "wkv_")
        xn = sb("xn", [P, TILES, TOKENS])
        k = sb("k", [P, TOKENS])
        v = sb("v", [P, TOKENS])
        gate = sb("gate", [P, TOKENS])
        h = sb("h", [P, SLOTS, T])
        top = sb("top", [P, 2, T + 2])
        qp = sb("qp", [P, 2, 2, T + 2])
        rise = sb("rise", [P, 4, T])
        decay = sb("decay", [P, 4, T])
        own = sb("own", [P, 3, T])
        own_v = sb("own_v", [P, 2, T])
        h_again = sb("h_again", [P, 2, TILES, T])
        x_again = sb("x_again", [P, TILES, T])
        squares = sb("squares", [P, TILES, T])
        spread = sb("spread", [P, TILES, T])
        MIDDLE = 1
        mean_sq = spread[:, 2, :]
        wk, wv, wr, wo = (sb(n, [P, 7, P]) for n in ("wk", "wv", "wr", "wo"))
        centre = h[:, 0:2, :].rearrange("p s n -> p (s n)")[:, 0:7 * P].rearrange("p (b n) -> p b n", b=7)
        wo_raw = h[:, 2:4, :].rearrange("p s n -> p (s n)")[:, 0:7 * P].rearrange("p (b n) -> p b n", b=7)
        col = sb("col", [P, 8, TILES])
        LNG, LNB, WD, U, OB, DECAY, MINUS_DECAY, MINUS_U = range(8)
        gn = GroupNorm(nc, sb, sem, P)
        ones = sb("ones", [P, 3, P])
        half_log = sb("half_log", [P, 1])

        job_ps = ps("job_ps", [P, BANKS, 512])
        stat_ps = ps("stat_ps", [P, 2, 512])
        out_ps = ps("out_ps", [P, 2, 512])

        par_in, prepared = sem("par_in"), sem("prepared")
        x_in_s = [sem(f"x_in{t}") for t in range(TILES)]
        normed_rest = sem("normed_rest")
        normed, job_made, job_read = sem("normed"), sem("job_made"), sem("job_read")
        trend, weighted, sums, fraction, inverse, folded, gated = (
            sem(n) for n in ("trend", "weighted", "sums", "fraction", "inverse", "folded", "gated"))
        h_stored = [sem(f"h_stored{n}") for n in range(SLOTS)]
        squared, stats_made, var_ready, rs_ready, out_made, scaled, out_ready = (
            sem(n) for n in ("squared", "stats_made", "var_ready", "rs_ready", "out_made", "scaled", "out_ready"))
        h_again_in = [sem("h_again_in0"), sem("h_again_in1")]
        x_again_in, stored = sem("x_again_in"), sem("stored")

        rows = x_in.rearrange("(q t p) n -> q p t n", p=P, t=TILES)
        out_rows = x_out.rearrange("(q t p) n -> q p t n", p=P, t=TILES)
        block = ctx.enter_context(nc.Block())
        LOADS = 11

        @block.sync
        def _(sp):
            for dst, name in ((wk, "wk"), (wv, "wv"), (wr, "wr")):
                sp.dma_start(dst[:, :, :], par[name].rearrange("b p n -> p b n")).then_inc(par_in, 16)
            sp.dma_start(wo_raw, par["wo"].rearrange("b p n -> p b n")).then_inc(par_in, 16)
            sp.dma_start(centre, par["centre"].rearrange("b p n -> p b n")).then_inc(par_in, 16)
            sp.dma_start(gn.mix[:, :, :], par["gn_mix"].rearrange("b p n -> p b n")).then_inc(par_in, 16)
            sp.dma_start(ones[:, :, :], par["image_mean"].rearrange("t p n -> p t n")).then_inc(par_in, 16)
            for c, name in ((LNG, "ln_g"), (LNB, "ln_b"), (WD, "w_decay"), (U, "u")):
                sp.dma_start(col[:, c, :], par[name]).then_inc(par_in, 16)

            def load_x(i):
                for t in range(TILES):
                    sp.dma_start(xn[:, t, :], rows[i, :, t, :]).then_inc(x_in_s[t], 16)

            def final_traffic(i):
                def load_h(b):
                    for t in range(TILES):
                        n, before, uses = slot_of(t, b)
                        sp.wait_ge(h_stored[n], (i * uses + before + 1) * 16)
                    if b >= 2:
                        sp.wait_ge(out_made, i * BLOCKS + 3 * (b - 1))
                    sp.dma_start(h_again[:, b % 2, :, :], out_rows[i, :, :, b * T:(b + 1) * T]).then_inc(h_again_in[b % 2], 16)

                def load_x_again(b):
                    sp.wait_ge(stored, (i * STEPS + b) * 16)
                    sp.dma_start(x_again[:, :, :], rows[i, :, :, b * T:(b + 1) * T]).then_inc(x_again_in, 16)

                load_h(0)
                load_h(1)
                load_x_again(0)
                for b in range(STEPS):
                    sp.wait_ge(out_ready, i * BLOCKS + 3 * (b + 1))
                    sp.dma_start(out_rows[i, :, :, b * T:(b + 1) * T], x_again[:, :, :]).then_inc(stored, 16)
                    if b + 2 < STEPS:
                        load_h(b + 2)
                    if b + 1 < STEPS:
                        load_x_again(b + 1)

            load_x(0)
            if pairs > 1:
                with sp.Fori(0, pairs - 1) as i:
                    sp.wait_ge(job_made, (i + 1) * TILES * JOBS)
                    load_x(i + 1)
                    final_traffic(i)
            final_traffic(pairs - 1)
            sp.wait_ge(stored, pairs * STEPS * 16)

        @block.gpsimd
        def _(pool):
            def fractions(i, u):
                d, z = unit(u)[2], u % 4
                own_pos = slice(0, T) if d == 0 else slice(1, T + 1)
                n = i * 4 * UNITS + 4 * u
                pool.wait_ge(sums, n + 4)
                pool.tensor_tensor(decay[:, z, :], rise[:, z, :], qp[:, d, 1, own_pos], ALU.mult).then_inc(fraction, 1)
                pool.wait_ge(fraction, n + 1)
                pool.tensor_tensor(decay[:, z, :], decay[:, z, :], own_v[:, u % 2, :], ALU.add).then_inc(fraction, 1)
                pool.tensor_tensor(rise[:, z, :], rise[:, z, :], qp[:, d, 0, own_pos], ALU.mult).then_inc(fraction, 1)
                pool.wait_ge(fraction, n + 3)
                pool.tensor_tensor(rise[:, z, :], rise[:, z, :], own[:, u % 3, :], ALU.add).then_inc(fraction, 1)

            def gating(i, u):
                t, s, d, c = unit(u)
                chunk = h[:, slot_of(t, c)[0], :]
                pool.wait_ge(folded, i * folds(UNITS) + folds(u + 1))
                pool.wait_ge(job_read, i * TILES * JOBS + gate_job(t, GATES.index(c)) + 1)
                pool.tensor_tensor(chunk, chunk, gate[:, c * T:(c + 1) * T], ALU.mult).then_inc(gated, 1)

            with pool.Fori(0, pairs) as i:
                gn.power(pool, i)
                for u in range(UNITS + 2):
                    if u < UNITS:
                        fractions(i, u)
                    if u >= 2 and second(u - 2):
                        gating(i, u - 2)

        @block.scalar
        def _(act):
            act.wait_ge(par_in, 16 * LOADS)
            act.activation(col[:, DECAY, :], col[:, WD, :], ACT.Exp).then_inc(prepared, 1)
            act.preload_act_table_set("natural_log_exp_and_others")

            def normalise(i):
                gn.ready(act, i)
                for part in (slice(0, T), slice(T, TOKENS)):
                    act.activation(xn[:, 0, part], xn[:, 0, part], ACT.Identity, bias=gn.shift[:, 0:1], scale=gn.rstd[:, 0:1])\
                        .then_inc(normed, 1)
                    if part.start == 0:
                        copy(i, 0, 0)

            def copy(i, u, which):
                t, s, d, b = unit(u)
                m = kv_job(t, b, which)
                act.wait_ge(job_made, i * TILES * JOBS + m + 1)
                e = last_visit(t - 1, b)
                if which == 0:
                    act.wait_ge(trend, i * 4 * UNITS + max(4 * e + 4, 0))
                else:
                    act.wait_ge(sums, i * 4 * UNITS + max(4 * e + 2, 0))
                act.activation((k, v)[which][:, b * T:(b + 1) * T], job_ps[:, m % BANKS, :], ACT.Copy).then_inc(job_read, 1)

            def exps(i, u):
                t, z = unit(u)[0], u % 4
                act.wait_ge(trend, i * 4 * UNITS + 4 * u + 4)
                act.activation(decay[:, z, :], rise[:, z, :], ACT.Exp, bias=col[:, MINUS_DECAY, t:t + 1]).then_inc(weighted, 1)
                act.wait_ge(weighted, i * 3 * UNITS + 3 * u + 1)
                act.activation(rise[:, z, :], rise[:, z, :], ACT.Exp, bias=col[:, MINUS_U, t:t + 1]).then_inc(weighted, 1)
                act.activation(own[:, u % 3, :], own[:, u % 3, :], ACT.Exp).then_inc(weighted, 1)

            def invert(i, u):
                z = u % 4
                act.wait_ge(fraction, i * 4 * UNITS + 4 * u + 4)
                act.activation(rise[:, z, :], rise[:, z, :], ACT.Ln).then_inc(inverse, 1)
                act.wait_ge(inverse, i * 2 * UNITS + 2 * u + 1)
                act.activation(rise[:, z, :], rise[:, z, :], ACT.Exp, bias=half_log[:, 0:1], scale=-1.0).then_inc(inverse, 1)

            def gates(i, t, ns):
                for n in ns:
                    m, b = gate_job(t, n), GATES[n]
                    act.wait_ge(job_made, i * TILES * JOBS + m + 1)
                    act.wait_ge(gated, i * BLOCKS + seconds(last_visit(t - 1, b) + 1) if t else i * BLOCKS)
                    act.activation(gate[:, b * T:(b + 1) * T], job_ps[:, m % BANKS, :], ACT.Sigmoid).then_inc(job_read, 1)
                act.preload_act_table_set("natural_log_exp_and_others")

            def store_h(i, u):
                t, s, d, c = unit(u)
                n = slot_of(t, c)[0]
                act.wait_ge(gated, i * BLOCKS + seconds(u + 1))
                act.dma_start(out_rows[i, :, t, c * T:(c + 1) * T], h[:, n, :]).then_inc(h_stored[n], 16)

            def final(i, v):
                b, f = divmod(v, FRAME)

                def deviation(b, image):
                    for half in (slice(0, 64), slice(64, 128)):
                        ins = act.activation(spread[half, 2 * image, :], spread[64 * image:64 * image + 64, MIDDLE, :],
                                             ACT.Exp, scale=-0.5)
                    ins.then_inc(rs_ready, 1)

                if f == 0 and b > 0:
                    deviation(b - 1, 1)
                    act.wait_ge(rs_ready, i * 4 * STEPS + 4 * (b - 1) + 3)
                    act.activation(spread[:, MIDDLE, :], spread[:, MIDDLE, :], ACT.Exp, scale=-0.5).then_inc(rs_ready, 1)
                elif b == STEPS:
                    return
                elif f == 1:
                    act.wait_ge(h_again_in[b % 2], (i * STEPS // 2 + b // 2 + 1) * 16)
                    act.wait_ge(stats_made, i * STEPS + b)
                    act.activation(squares[:, :, :], h_again[:, b % 2, :, :], ACT.Square).then_inc(squared, 1)
                elif f == 3:
                    act.wait_ge(stats_made, i * STEPS + b + 1)
                    act.wait_ge(scaled, i * BLOCKS + b * TILES)
                    act.activation(mean_sq, stat_ps[:, 0, :], ACT.Square).then_inc(squared, 1)
                elif f == 4:
                    act.wait_ge(var_ready, i * 2 * STEPS + 2 * b + 2)
                    act.activation(spread[:, MIDDLE, :], spread[:, MIDDLE, :], ACT.Ln).then_inc(rs_ready, 1)
                    act.wait_ge(rs_ready, i * 4 * STEPS + 4 * b + 1)
                    deviation(b, 0)

            def recurrence(i, before):
                normalise(i)
                for v in range(-1, UNITS + 2):
                    finals = before is not None and 0 <= v < FINAL_UNITS
                    if finals and v % FRAME == 3:
                        final(before, v)
                    if v + 1 < UNITS:
                        if v == -1 and before is None:
                            act.wait_ge(prepared, 5)
                        exps(i, v + 1)
                        if not second(v + 1):
                            copy(i, v + 1, 1)
                        if v + 2 < UNITS and not second(v + 2):
                            copy(i, v + 2, 0)
                        if v >= 0:
                            t, r = divmod(v, 2 * STEPS)
                            if r in (STEPS, STEPS + STEPS // 2):
                                half = STEPS // 2
                                gates(i, t, range(0, half) if r == STEPS else range(half, STEPS))
                    if 1 <= v <= UNITS:
                        invert(i, v - 1)
                    if finals and v % FRAME != 3:
                        final(before, v)
                    if v >= 3 and second(v - 3):
                        store_h(i, v - 3)
                store_h(i, UNITS - 1)

            recurrence(0, None)
            if pairs > 1:
                with act.Fori(0, pairs - 1) as i:
                    recurrence(i + 1, i)
            for step in range(FINAL_UNITS):
                final(pairs - 1, step)

        @block.tensor
        def _(pe):
            pe.wait_ge(par_in, 16 * LOADS)
            pe.wait_ge(prepared, 3)
            for t in range(TILES):
                for j, s in enumerate(SOURCES[t]):
                    both = [q for q in SOURCES[s] if q in SOURCES[t]]
                    for q in both:
                        pe.matmul(job_ps[:, t, j * P:(j + 1) * P], centre[:, BLOCK[q, s], :], wo[:, BLOCK[q, t], :],
                                  start=(q == both[0]), stop=(q == both[-1]))
            for t in range(TILES):
                for n, s in enumerate(SOURCES[t]):
                    ins = pe.matmul(stat_ps[:, 0, t:t + 1], wo_raw[:, BLOCK[s, t], :], col[:, LNB, s:s + 1],
                                    start=(n == 0), stop=(n == len(SOURCES[t]) - 1))
            ins.then_inc(prepared, 1)
            pe.wait_ge(prepared, 5)

            def product(i, m, w, t, b):
                pe.wait_ge(job_read, i * TILES * JOBS + max(m - BANKS + 1, 0))
                for n, s in enumerate(SOURCES[t]):
                    ins = pe.matmul(job_ps[:, m % BANKS, :], w[:, BLOCK[s, t], :], xn[:, s, b * T:(b + 1) * T],
                                    start=(n == 0), stop=(n == len(SOURCES[t]) - 1))
                ins.then_inc(job_made, 1)

            def keys_and_values(i, u):
                t, s, d, b = unit(u)
                if u <= 1:
                    pe.wait_ge(normed, i * 2 + u + 1)
                    pe.wait_ge(normed_rest, i * TILES + u + 1)
                elif u == 2 * STEPS:
                    pe.wait_ge(normed_rest, (i + 1) * TILES)
                product(i, kv_job(t, b, 0), wk, t, b)
                product(i, kv_job(t, b, 1), wv, t, b)

            def result(i, b, t):
                m = b * TILES + t
                pe.wait_ge(out_ready, i * BLOCKS + max(m - 1, 0))
                for n, s in enumerate(SOURCES[t]):
                    ins = pe.matmul(out_ps[:, m % 2, :], wo[:, BLOCK[s, t], :], h_again[:, b % 2, s, :],
                                    start=(n == 0), stop=(n == len(SOURCES[t]) - 1))
                ins.then_inc(out_made, 1)

            def statistic(i, b, which):
                if which == 0:
                    pe.wait_ge(h_again_in[b % 2], (i * STEPS // 2 + b // 2 + 1) * 16)
                    pe.wait_ge(var_ready, i * 2 * STEPS + 2 * b)
                else:
                    pe.wait_ge(squared, i * 2 * STEPS + 2 * b + 1)
                for s in range(TILES):
                    ins = pe.matmul(stat_ps[:, which, :], ones[:, s, :], (h_again[:, b % 2, s, :], squares[:, s, :])[which],
                                    start=(s == 0), stop=(s == TILES - 1))
                if which == 1:
                    ins.then_inc(stats_made, 1)

            def final(i, v):
                b, f = divmod(v, FRAME)
                if f == 1 and b > 0:
                    result(i, b - 1, 2)
                if b < STEPS:
                    if f in (1, 2):
                        statistic(i, b, f - 1)
                    elif f in (3, 4):
                        result(i, b, f - 3)

            def recurrence(i, before):
                if before is not None:
                    pe.wait_ge(squared, before * 2 * STEPS)
                gn.mix_stats(pe, i, stat_ps[:, 0, 0:2 * TILES])
                keys_and_values(i, 0)
                keys_and_values(i, 1)
                for v in range(UNITS):
                    if v + 2 < UNITS and not second(v + 2):
                        keys_and_values(i, v + 2)
                    t, r = divmod(v, 2 * STEPS)
                    for n in {6: (0, 1), 7: (2, 3), 9: (4, 5), 10: (6, 7)}.get(r, ()):
                        product(i, gate_job(t, n), wr, t, GATES[n])
                    if before is not None and v < FINAL_UNITS:
                        final(before, v)

            recurrence(0, None)
            if pairs > 1:
                with pe.Fori(0, pairs - 1) as i:
                    recurrence(i + 1, i)
            for step in range(FINAL_UNITS):
                final(pairs - 1, step)

        @block.vector
        def _(dve):
            dve.memset(gn.half[:, :], -0.5)
            dve.memset(half_log[:, :], -math.log(2.0)).then_inc(prepared, 1)
            dve.wait_ge(par_in, 16 * LOADS)
            for t in range(TILES):
                for s in SOURCES[t]:
                    ins = dve.tensor_scalar(wo[:, BLOCK[s, t], :], wo_raw[:, BLOCK[s, t], :], col[:, LNG, s:s + 1], None, ALU.mult)
            ins.then_inc(prepared, 1)
            dve.wait_ge(prepared, 4)
            for t in range(TILES):
                for j, s in enumerate(SOURCES[t]):
                    dve.tensor_copy(wo[:, BLOCK[s, t], :], job_ps[:, t, j * P:(j + 1) * P])
            dve.tensor_copy(col[:, OB, :], stat_ps[:, 0, 0:TILES])
            dve.tensor_scalar(col[:, MINUS_DECAY, :], col[:, DECAY, :], -1.0, None, ALU.mult)
            dve.tensor_scalar(col[:, MINUS_U, :], col[:, U, :], -1.0, None, ALU.mult).then_inc(prepared, 1)

            def trends(i, u):
                t, s, d, c = unit(u)
                new, old, at, end = ((slice(1, T + 1), slice(0, T), 0, T), (slice(0, T), slice(1, T + 1), T, 0))[d]
                flip = (lambda a: a) if d == 0 else (lambda a: a[:, ::-1])
                n = i * 4 * UNITS + 4 * u
                if s == 0:
                    dve.memset(top[:, d, at:at + 1], NEG_INF).then_inc(trend, 1)
                else:
                    dve.tensor_copy(top[:, d, at:at + 1], top[:, d, end:end + 1]).then_inc(trend, 1)
                dve.wait_ge(trend, n + 1)
                if not second(u):
                    dve.wait_ge(job_read, i * TILES * JOBS + kv_job(t, c, 0) + 1)
                chunk = k[:, c * T:(c + 1) * T]
                dve.tensor_tensor_scan(flip(top[:, d, new]), col[:, MINUS_DECAY, t:t + 1].to_broadcast([P, T]), flip(chunk),
                                       top[:, d, at:at + 1], ALU.add, ALU.max).then_inc(trend, 1)
                dve.wait_ge(fraction, i * 4 * UNITS + max(4 * (u - 2), 0))
                dve.wait_ge(trend, n + 2)
                dve.tensor_tensor(rise[:, u % 4, :], top[:, d, old], top[:, d, new], ALU.subtract).then_inc(trend, 1)
                dve.tensor_tensor(own[:, u % 3, :], chunk, top[:, d, new], ALU.subtract).then_inc(trend, 1)

            def accumulate(i, u):
                t, s, d, c = unit(u)
                new, at, end = ((slice(1, T + 1), 0, T), (slice(0, T), T, 0))[d]
                flip = (lambda a: a) if d == 0 else (lambda a: a[:, ::-1])
                n = i * 4 * UNITS + 4 * u
                dve.wait_ge(fraction, i * 4 * UNITS + max(4 * (u - 1), 0))
                if s == 0:
                    dve.memset(qp[:, d, :, at:at + 1], 0.0).then_inc(sums, 1)
                else:
                    dve.tensor_copy(qp[:, d, :, at:at + 1], qp[:, d, :, end:end + 1]).then_inc(sums, 1)
                dve.wait_ge(weighted, i * 3 * UNITS + 3 * u + 3)
                if not second(u):
                    dve.wait_ge(job_read, i * TILES * JOBS + kv_job(t, c, 1) + 1)
                dve.tensor_tensor(own_v[:, u % 2, :], own[:, u % 3, :], v[:, c * T:(c + 1) * T], ALU.mult).then_inc(sums, 1)
                dve.wait_ge(sums, n + 1)
                dve.tensor_tensor_scan(flip(qp[:, d, 0, new]), flip(decay[:, u % 4, :]), flip(own[:, u % 3, :]),
                                       qp[:, d, 0, at:at + 1], ALU.mult, ALU.add).then_inc(sums, 1)
                dve.wait_ge(sums, n + 2)
                dve.tensor_tensor_scan(flip(qp[:, d, 1, new]), flip(decay[:, u % 4, :]), flip(own_v[:, u % 2, :]),
                                       qp[:, d, 1, at:at + 1], ALU.mult, ALU.add).then_inc(sums, 1)

            def fold(i, u):
                t, s, d, c = unit(u)
                z = u % 4
                slot, used, uses = slot_of(t, c)
                chunk = h[:, slot, :]
                n = i * folds(UNITS) + folds(u)
                dve.wait_ge(inverse, i * 2 * UNITS + 2 * u + 2)
                if not second(u):
                    dve.wait_ge(h_stored[slot], (i * uses + used) * 16)
                    dve.tensor_tensor(chunk, decay[:, z, :], rise[:, z, :], ALU.mult).then_inc(folded, 1)
                    return
                dve.tensor_tensor(decay[:, z, :], decay[:, z, :], rise[:, z, :], ALU.mult).then_inc(folded, 1)
                dve.wait_ge(folded, n + 1)
                dve.tensor_tensor(chunk, chunk, decay[:, z, :], ALU.add).then_inc(folded, 1)

            def final_result(i, b, t):
                m = b * TILES + t
                dve.wait_ge(rs_ready, i * 4 * STEPS + 4 * b + (2, 4, 3)[t])
                if t == 0:
                    dve.wait_ge(x_again_in, (i * STEPS + b + 1) * 16)
                dve.wait_ge(out_made, i * BLOCKS + m + 1)
                dve.tensor_tensor(out_ps[:, m % 2, :], out_ps[:, m % 2, :], spread[:, t, :], ALU.mult).then_inc(scaled, 1)
                dve.wait_ge(scaled, i * BLOCKS + m + 1)
                dve.scalar_tensor_tensor(out=x_again[:, t, :], in0=out_ps[:, m % 2, :], scalar=col[:, OB, t:t + 1],
                                         in1=x_again[:, t, :], op0=ALU.add, op1=ALU.add).then_inc(out_ready, 1)

            def final(i, v):
                b, f = divmod(v, FRAME)
                if f < TILES and b > 0:
                    final_result(i, b - 1, f)
                elif f == 3 and b < STEPS:
                    dve.wait_ge(squared, i * 2 * STEPS + 2 * b + 2)
                    var = spread[:, MIDDLE, :]
                    dve.scalar_tensor_tensor(out=var, in0=mean_sq, scalar=-1.0, in1=stat_ps[:, 1, :],
                                             op0=ALU.mult, op1=ALU.add).then_inc(var_ready, 1)
                    dve.wait_ge(var_ready, i * 2 * STEPS + 2 * b + 1)
                    dve.tensor_scalar(var, var, 0.0, LN_EPS, ALU.max, ALU.add).then_inc(var_ready, 1)

            def recurrence(i, before):
                gn.statistics(dve, i, xn, lambda t: dve.wait_ge(x_in_s[t], (i + 1) * 16))
                if before is not None:
                    fold(before, UNITS - 2)
                    fold(before, UNITS - 1)
                gn.scales(dve, i, stat_ps[:, 0, 0:2 * TILES])
                def normalise(t, part):
                    dve.tensor_scalar(xn[:, t, part], xn[:, t, part], gn.rstd[:, t:t + 1], gn.shift[:, t:t + 1], ALU.mult, ALU.add)\
                        .then_inc(normed_rest, 1)

                normalise(1, slice(0, T))
                normalise(1, slice(T, TOKENS))
                trends(i, 0)
                normalise(2, slice(0, TOKENS))
                for u in range(UNITS):
                    if u + 1 < UNITS:
                        trends(i, u + 1)
                    accumulate(i, u)
                    if u >= 2:
                        fold(i, u - 2)
                    if before is not None and u < FINAL_UNITS:
                        final(before, u)

            recurrence(0, None)
            if pairs > 1:
                with dve.Fori(0, pairs - 1) as i:
                    recurrence(i + 1, i)
            fold(pairs - 1, UNITS - 2)
            fold(pairs - 1, UNITS - 1)
            for step in range(FINAL_UNITS):
                final(pairs - 1, step)



def _blocks(big):
    return np.stack([big[P * s:P * s + P, P * t:P * t + P] for (s, t) in BLOCK])


def _twice(w):
    big = np.zeros((2 * w.shape[0], 2 * w.shape[1]), np.float32)
    big[:w.shape[0], :w.shape[1]] = w
    big[w.shape[0]:, w.shape[1]:] = w
    return big


def _columns(v):
    return np.ascontiguousarray(np.concatenate([v, v]).reshape(TILES, P).T)


def wkv_params(p, inputs):
    r = np.arange(2 * CH)
    same = (r[:, None] // CH == r[None, :] // CH)
    arrays = {}
    for n, key in (("wk", "Wk"), ("wv", "Wv"), ("wr", "Wr"), ("wo", "Wo")):
        arrays[n] = _blocks(_twice(inputs[p + key].T))
    arrays["centre"] = _blocks((np.eye(2 * CH) - same / CH).astype(np.float32))
    for n, key in (("ln_g", "ln_g"), ("ln_b", "ln_b"), ("w_decay", "w_decay"), ("u", "u")):
        arrays[n] = _columns(inputs[p + key])
    return arrays


def shared_constants():
    r = np.arange(2 * CH)
    group = CH // 32
    mix = (r[:, None] // group == r[None, :] // group) / group
    image = (r.reshape(TILES, P, 1) // CH == np.arange(P)[None, None, :] // 64) / CH
    return {"gn_mix": _blocks(mix.astype(np.float32)), "image_mean": image.astype(np.float32)}


def fractional_matrix(a):
    n = SIDE
    eye = np.eye(n, dtype=np.complex128)
    if a < 0.5:
        shift = (np.arange(n) + n // 2) % n
        eye = np.fft.ifft(eye[:, shift], axis=-1) * math.sqrt(n)
        eye = eye[:, np.argsort(shift)]
        a = a + 1.0

    def full_convolution(f, kern):
        length = f.shape[-1] + kern.shape[0] - 1
        return np.fft.ifft(np.fft.fft(f, n=length, axis=-1) * np.fft.fft(kern, n=length), axis=-1)

    alpha = a * math.pi / 2
    tana2, sina = math.tan(alpha / 2), math.sin(alpha)
    y = np.zeros((n, 2 * n - 1), np.complex128)
    y[:, ::2] = eye
    fi = full_convolution(y, np.sinc(np.arange(-(2 * n - 3), 2 * n - 2) / 2.0))[:, 2 * n - 3:4 * n - 4]
    pad = np.zeros((n, n - 1))
    t = np.arange(-2 * n + 2, 2 * n - 1).astype(np.float64)
    chirp = np.exp(-1j * math.pi / n * tana2 / 4 * t ** 2)
    c = math.pi / n / sina / 4
    m = np.arange(-(4 * n - 4), 4 * n - 3).astype(np.float64)
    ret = full_convolution(chirp * np.concatenate([pad, fi, pad], axis=-1), np.exp(1j * c * m ** 2))
    ret = ret[:, 4 * n - 4:8 * n - 7] * math.sqrt(c / math.pi) * chirp
    return np.exp(-1j * (1 - a) * math.pi / 4) * ret[:, n - 1:3 * n - 2:2]


def fourier_constants():
    n = SIDE
    k = np.arange(n)
    turn = np.outer(k, k) % n
    cos, sin = np.cos(2 * math.pi * turn / n), np.sin(2 * math.pi * turn / n)
    cos[turn % 32 == 16] = 0.0
    sin[turn % 32 == 0] = 0.0
    weight = np.where((k == 0) | (k == n // 2), 1.0, np.where(k < n // 2, 2.0, 0.0)) / (n * n)
    trans = np.zeros((5, P, 2, 256), np.float32)
    for f, m in enumerate((fractional_matrix(0.5), cos - 1j * sin, fractional_matrix(-0.5),
                           (cos + 1j * sin) * weight[:, None], cos + 1j * sin)):
        for r, parts in enumerate(((m.real, m.imag), (-m.imag, m.real))):
            for c, part in enumerate(parts):
                for image in range(2):
                    q = slice(n * image, n * image + n)
                    trans[f, q, r, P * c + n * image:P * c + n * image + n] = part
    inner = int(n * math.cos(0.25 * math.pi))
    first = (n - inner) // 2
    inside = ((k >= first) & (k < first + inner)).astype(np.float32)
    mask = np.outer(np.concatenate([inside, inside]), inside)
    return {"trans": trans, "mask": mask.astype(np.float32), "ident": np.eye(P, dtype=np.float32)}


def fourier_params(p, inputs):
    g, hb = 16, 8

    def by_rows(w):
        m = np.zeros((g, hb, g, hb), np.float32)
        for r in range(hb):
            m[:, r, :, r] = w.T
        return m.reshape(P, P)

    spatial = np.zeros((3, 3, g, hb, g, hb), np.float32)
    w = inputs[p + "mag_s_w"]
    for dw in range(3):
        for dh in range(3):
            for r in range(hb):
                q, s = divmod(r + dh - 1, hb)
                spatial[dw, q + 1, :, s, :, r] = w[:, :, dh, dw].T
    conv2 = inputs[p + "conv2_w"]
    rest = np.zeros((64, CH), np.float32)
    rest[g:3 * g] = conv2[:, g:].T
    first = np.zeros((g, 64), np.float32)
    first[:, :g] = inputs[p + "conv_0_w"]
    row = lambda key: inputs[p + key]
    rows = np.stack([row("mag_s_b"), row("mag_f_b"), row("mag_b"), row("conv_1_b"), row("pha_b"), row("conv_1_b")])
    c1 = inputs[p + "conv1_w"].T
    return {
        "mixers": np.stack([by_rows(row(k)) for k in ("mag_f_w", "mag_w", "pha_w", "conv_1_w")]),
        "spatial": spatial.reshape(9, P, P),
        "conv2_rest": _twice(rest),
        "conv0": _twice(first),
        "conv2_0": _twice(conv2[:, :g].T),
        "bias0": np.concatenate([row("conv_0_b")] * 2).reshape(2 * g, 1),
        "rows": np.ascontiguousarray(np.broadcast_to(rows, (P, 6, g))),
        "conv1": np.concatenate([c1, c1]).reshape(TILES, P, 3 * g),
    }


def conv_params(p, inputs):
    dw = inputs[p + "dw_w"].reshape(CH, 9)
    return {
        "pointwise": _blocks(_twice(inputs[p + "pw_w"].T)),
        "taps": np.ascontiguousarray(np.concatenate([dw, dw]).reshape(TILES, P, 9).transpose(1, 0, 2)),
        "affine": np.stack([_columns(inputs[p + "gamma"]), _columns(inputs[p + "beta"])], axis=1),
    }


def same_channel(pairs=PAIRS):
    r = np.arange(2 * CH)
    big = ((r[:, None] % CH == r[None, :] % CH) / (2.0 * pairs)).astype(np.float32)
    return np.stack([big[P * s:P * s + P, P * t:P * t + P] for s in range(TILES) for t in range(TILES)])


def build(nc, x, out, par):
    def scratch(name, shape):
        return nc.dram_tensor(name, shape, F32, kind="Internal").ap()

    z, bn_cols = scratch("z", [ROWS, TOKENS]), scratch("bn_cols", [P, 2, TILES])
    after_1, after_2 = scratch("after_1", [ROWS, TOKENS]), scratch("after_2", [ROWS, TOKENS])
    convolution_layer(nc, x, z, bn_cols, par["L0"])
    fourier_layer(nc, x, after_1, dict(par["L1"], bn_cols=bn_cols), "f1_", (z,))
    wkv_layer(nc, after_1, after_2, par["L2"])
    fourier_layer(nc, after_2, out, par["L3"], "f3_")


def kernel(**inputs):
    import concourse.bacc as _bacc
    from concourse.bass_utils import run_bass_kernel_spmd as _run

    nc = _bacc.Bacc("TRN2", target_bir_lowering=False, num_devices=1)
    inputs = {k: np.asarray(v) for k, v in inputs.items()}
    shared, waves = shared_constants(), fourier_constants()
    layers = {
        "L0": dict(conv_params("L0_conv_", inputs), same=same_channel(), ident=waves["ident"], gn_mix=shared["gn_mix"]),
        "L1": dict(fourier_params("L1_conv_", inputs), gn_mix=shared["gn_mix"], **waves),
        "L2": dict(wkv_params("L2_conv_", inputs), **shared),
        "L3": dict(fourier_params("L3_conv_", inputs), gn_mix=shared["gn_mix"], **waves),
    }
    arrays, par = {}, {}
    for layer, named in layers.items():
        par[layer] = {}
        for name, a in named.items():
            arrays[f"{layer}_{name}"] = a = np.ascontiguousarray(a)
            par[layer][name] = nc.dram_tensor(f"{layer}_{name}", a.shape, F32, kind="ExternalInput").ap()
    arrays["x"] = np.ascontiguousarray(inputs["x"]).reshape(ROWS, TOKENS)
    x = nc.dram_tensor("x", (ROWS, TOKENS), F32, kind="ExternalInput").ap()
    out = nc.dram_tensor("out", (ROWS, TOKENS), F32, kind="ExternalOutput").ap()
    build(nc, x, out, par)
    r = _run(nc, [arrays], core_ids=[0])
    return r.results[0]["out"].reshape(BATCH, CH, SIDE, SIDE)
```
